# Optimizing a Trainium2 kernel written in Bass

```python
import numpy as np
import jax
import jax.numpy as jnp

def _softmax(x, axis=-1):
    return jax.nn.softmax(x, axis=axis)

def _gelu(x):
    return jax.nn.gelu(x, approximate=True)

def _silu(x):
    return jax.nn.silu(x)

def _sigmoid(x):
    return jax.nn.sigmoid(x)

def _layernorm(x, axis=-1, eps=1e-05):
    m = jnp.mean(x, axis=axis, keepdims=True)
    v = jnp.var(x, axis=axis, keepdims=True)
    return (x - m) / jnp.sqrt(v + eps)

def _scatter_add(tgt, idx, src, axis=0):
    return tgt.at[idx].add(src)

def _segment_sum(src, seg, n):
    return jax.ops.segment_sum(src, seg, n)
kernel_name = 'mk_vit_tower_d4_tok_img768_r4_6240df'

def setup_inputs(seed: int=0):
    np.random.seed(seed)
    _w = jnp.asarray

    def _rec_inputs():
        import jax
        import jax.numpy as jnp
        _rk = jax.random.key(seed)
        x = -0.00016672 + 0.999947 * jax.random.normal(jax.random.fold_in(_rk, 1), (16, 96, 96, 3), jnp.float32)
        return x
    x = _rec_inputs()

    def _L0_tok_setup():
        import jax, jax.numpy as jnp
        import numpy as np
        P = 16
        D = 192

        def _patchify(x):
            B, H, W_, C = x.shape
            gh, gw = (H // P, W_ // P)
            x = x.reshape(B, gh, P, gw, P, C)
            x = x.transpose(0, 1, 3, 2, 4, 5)
            return x.reshape(B, gh * gw, P * P * C)
        key = jax.random.key(seed)
        k1, k2, k3 = jax.random.split(key, 3)
        B, H, W_, C = (64, 96, 96, 3)
        x = jax.random.normal(k1, (B, H, W_, C), dtype=jnp.float32)
        Wk = jax.random.normal(k2, (P * P * C, D), dtype=jnp.float32) * 0.02
        class_emb = jnp.zeros((1, 1, D), dtype=jnp.float32)
        N = H // P * (W_ // P)
        pos_emb = jax.random.normal(k3, (1, N + 1, D), dtype=jnp.float32) * 0.02
        return {'x': x, 'W': Wk, 'class_emb': class_emb, 'pos_emb': pos_emb}
    _L0_tok_all = _L0_tok_setup()
    _L0_tok_in = {k: v for k, v in _L0_tok_all.items() if k in ('W', 'class_emb', 'pos_emb')}
    del _L0_tok_all

    def _L0_attn_setup():
        import jax, jax.numpy as jnp
        import numpy as np
        NUM_HEADS = 12

        def _reference_tuple_inner(x, w_qkv, w_proj, b_proj):
            b, n, c = x.shape
            h = NUM_HEADS
            d = c // h
            qkv = (x @ w_qkv.T).reshape(b, n, 3, h, d).transpose(2, 0, 3, 1, 4)
            q, k, v = (qkv[0], qkv[1], qkv[2])
            q = jax.nn.elu(q) + 1.0
            k = jax.nn.elu(k) + 1.0
            kv = jnp.einsum('bhsd,bhse->bhde', k, v)
            z = 1.0 / jnp.einsum('bhsd,bhd->bhs', q, k.sum(axis=-2))
            out = jnp.einsum('bhde,bhsd,bhs->bhse', kv, q, z)
            out = out.transpose(0, 2, 1, 3).reshape(b, n, c)
            out = out @ w_proj.T + b_proj
            return (out, kv)
        key = jax.random.key(seed)
        k0, k1, k2 = jax.random.split(key, 3)
        b, n, c = (4, 1024, 192)
        x = jax.random.normal(k0, (b, n, c), dtype=jnp.float32)
        w_qkv = jax.random.normal(k1, (3 * c, c), dtype=jnp.float32) * 0.02
        w_proj = jax.random.normal(k2, (c, c), dtype=jnp.float32) * 0.02
        b_proj = jnp.zeros((c,), dtype=jnp.float32)
        return {'x': x, 'w_qkv': w_qkv, 'w_proj': w_proj, 'b_proj': b_proj}
    _L0_attn_all = _L0_attn_setup()
    _L0_attn_in = {k: v for k, v in _L0_attn_all.items() if k in ('w_qkv', 'w_proj', 'b_proj')}
    del _L0_attn_all

    def _L0_ffn_setup():
        import jax, jax.numpy as jnp
        import numpy as np
        B_SZ, S, D = (8, 128, 192)
        H = 12
        N_EXP = 8
        RANK = 16
        ALPHA = 32
        TOP_K = 2
        key = jax.random.key(seed)
        ks = jax.random.split(key, 9)
        x = jax.random.normal(ks[0], (B_SZ, S, D), jnp.float32)
        W_qkv = jax.random.normal(ks[1], (3 * D, D), jnp.float32) * 0.02
        b_qkv = jnp.zeros((3 * D,), jnp.float32)
        W_gate = jax.random.normal(ks[2], (N_EXP, D), jnp.float32) * 0.02
        b_gate = jnp.zeros((N_EXP,), jnp.float32)
        A = jax.random.normal(ks[3], (N_EXP, RANK, D), jnp.float32) * 0.02
        B_lora = jax.random.normal(ks[4], (N_EXP, 3 * D, RANK), jnp.float32) * 0.02
        W_proj = jax.random.normal(ks[5], (D, D), jnp.float32) * 0.02
        b_proj = jnp.zeros((D,), jnp.float32)
        return {'x': x, 'W_qkv': W_qkv, 'b_qkv': b_qkv, 'W_gate': W_gate, 'b_gate': b_gate, 'A': A, 'B_lora': B_lora, 'W_proj': W_proj, 'b_proj': b_proj}
    _L0_ffn_all = _L0_ffn_setup()
    _L0_ffn_in = {k: v for k, v in _L0_ffn_all.items() if k in ('W_qkv', 'b_qkv', 'W_gate', 'b_gate', 'A', 'B_lora', 'W_proj', 'b_proj')}
    del _L0_ffn_all

    def _L1_attn_setup():
        import jax, jax.numpy as jnp
        import numpy as np
        NHEAD = 12
        EPS = 1e-05

        def layernorm_nobias(x, gamma):
            mu = jnp.mean(x, axis=-1, keepdims=True)
            var = jnp.var(x, axis=-1, keepdims=True)
            return (x - mu) * jax.lax.rsqrt(var + EPS) * gamma
        key = jax.random.key(seed)
        ks = jax.random.split(key, 10)
        b, l, d = (4, 512, 192)
        s = d ** (-0.5)
        return {'x': jax.random.normal(ks[0], (b, l, d), jnp.float32), 'Wq': jax.random.normal(ks[1], (d, d), jnp.float32) * s, 'Wk': jax.random.normal(ks[2], (d, d), jnp.float32) * s, 'bk': jax.random.normal(ks[3], (d,), jnp.float32) * 0.02, 'Wv': jax.random.normal(ks[4], (d, d), jnp.float32) * s, 'bv': jax.random.normal(ks[5], (d,), jnp.float32) * 0.02, 'gq': jnp.ones((d,), jnp.float32), 'gk': jnp.ones((d,), jnp.float32), 'Wo': jax.random.normal(ks[6], (d, d), jnp.float32) * s, 'bo': jnp.zeros((d,), jnp.float32)}
    _L1_attn_all = _L1_attn_setup()
    _L1_attn_in = {k: v for k, v in _L1_attn_all.items() if k in ('Wq', 'Wk', 'bk', 'Wv', 'bv', 'gq', 'gk', 'Wo', 'bo')}
    del _L1_attn_all

    def _L1_ffn_setup():
        import jax, jax.numpy as jnp
        import numpy as np
        H = 12
        ALPHA = (1, 2, 3)
        DEPTH = 5
        BLOCK_DEPTH = 3
        TOTAL_DEPTH_M1 = 14 - 1
        SMALL_ACTIVE = BLOCK_DEPTH <= DEPTH <= TOTAL_DEPTH_M1 - BLOCK_DEPTH

        def _ln(x, g, b, eps=1e-05):
            m = jnp.mean(x, axis=-1, keepdims=True)
            v = jnp.mean((x - m) ** 2, axis=-1, keepdims=True)
            return (x - m) * jax.lax.rsqrt(v + eps) * g + b

        def _attn_branch(xp, w_qkv, w_proj, b_proj, keep_heads, keep_ch):
            B2, N, C = xp.shape
            hd = C // H
            scale = hd ** (-0.5)
            qkv = (xp @ w_qkv).reshape(B2, N, 3, H, hd).transpose(2, 0, 3, 1, 4)
            hmask = (jnp.arange(H) < keep_heads).astype(xp.dtype)[None, :, None, None]
            q, k, v = (qkv[0] * hmask, qkv[1] * hmask, qkv[2] * hmask)
            a = jax.nn.softmax(jnp.einsum('bhnd,bhmd->bhnm', q, k) * scale, axis=-1)
            o = jnp.einsum('bhnm,bhmd->bhnd', a, v).transpose(0, 2, 1, 3).reshape(B2, N, C)
            o = o @ w_proj + b_proj
            cmask = (jnp.arange(C) < keep_ch).astype(xp.dtype)
            return o * cmask

        def _mlp_branch(xp, w1, b1, w2, b2, keep_ch):
            C = xp.shape[-1]
            cmask = (jnp.arange(C) < keep_ch).astype(xp.dtype)
            h = jax.nn.gelu(xp * cmask @ w1 + b1, approximate=False)
            return (h @ w2 + b2) * cmask
        key = jax.random.key(seed)
        ks = jax.random.split(key, 8)
        B, N, C = (64, 257, 192)
        HID = 4 * C

        def w(k, shape):
            return jax.random.normal(k, shape, jnp.float32) * 0.02
        return {'x': jax.random.normal(ks[0], (B, N, C), jnp.float32), 'gumbel_weights': jax.random.uniform(ks[1], (3,), jnp.float32), 'n1l_g': jnp.ones((C,), jnp.float32), 'n1l_b': jnp.zeros((C,), jnp.float32), 'n1s_g': jnp.ones((C,), jnp.float32), 'n1s_b': jnp.zeros((C,), jnp.float32), 'w_qkv': w(ks[2], (C, 3 * C)), 'w_proj': w(ks[3], (C, C)), 'b_proj': jnp.zeros((C,), jnp.float32), 'n2l_g': jnp.ones((C,), jnp.float32), 'n2l_b': jnp.zeros((C,), jnp.float32), 'n2s_g': jnp.ones((C,), jnp.float32), 'n2s_b': jnp.zeros((C,), jnp.float32), 'w_fc1': w(ks[4], (C, HID)), 'b_fc1': jnp.zeros((HID,), jnp.float32), 'w_fc2': w(ks[5], (HID, C)), 'b_fc2': jnp.zeros((C,), jnp.float32)}
    _L1_ffn_all = _L1_ffn_setup()
    _L1_ffn_in = {k: v for k, v in _L1_ffn_all.items() if k in ('gumbel_weights', 'n1l_g', 'n1l_b', 'n1s_g', 'n1s_b', 'w_qkv', 'w_proj', 'b_proj', 'n2l_g', 'n2l_b', 'n2s_g', 'n2s_b', 'w_fc1', 'b_fc1', 'w_fc2', 'b_fc2')}
    del _L1_ffn_all

    def _L2_attn_setup():
        import jax, jax.numpy as jnp
        import numpy as np
        import math
        DIM = 192
        NUM_HEADS = 12
        HEAD_DIM = DIM // NUM_HEADS
        ORDER = 2
        SCALE = HEAD_DIM ** (-0.5)
        key = jax.random.key(seed)
        ks = jax.random.split(key, 5)
        B, N, C = (8, 256, DIM)
        x = jax.random.normal(ks[0], (B, N, C), dtype=jnp.float32)
        w_qkv = jax.random.normal(ks[1], (C, 3 * C), dtype=jnp.float32) * C ** (-0.5)
        w_proj = jax.random.normal(ks[2], (C, C), dtype=jnp.float32) * C ** (-0.5)
        b_proj = jax.random.normal(ks[3], (C,), dtype=jnp.float32) * 0.02
        return {'x': x, 'w_qkv': w_qkv, 'w_proj': w_proj, 'b_proj': b_proj}
    _L2_attn_all = _L2_attn_setup()
    _L2_attn_in = {k: v for k, v in _L2_attn_all.items() if k in ('w_qkv', 'w_proj', 'b_proj')}
    del _L2_attn_all

    def _L2_ffn_setup():
        import jax, jax.numpy as jnp
        import numpy as np
        ACT_SCALE = 0.02
        W_SCALE = 0.01
        EFF_SCALE = ACT_SCALE * W_SCALE
        B, S, D, M = (8, 1024, 192, 192)
        key = jax.random.key(seed)
        kx, kw, kb = jax.random.split(key, 3)
        x = jax.random.normal(kx, (B, S, D), dtype=jnp.float32)
        weight_t = jax.random.randint(kw, (D, M), -128, 128, dtype=jnp.int32).astype(jnp.int8)
        bias = jax.random.normal(kb, (M,), dtype=jnp.float32)
        return {'x': x, 'weight_t': weight_t, 'bias': bias}
    _L2_ffn_all = _L2_ffn_setup()
    _L2_ffn_in = {k: v for k, v in _L2_ffn_all.items() if k in ('weight_t', 'bias')}
    del _L2_ffn_all

    def _L3_attn_setup():
        import jax, jax.numpy as jnp
        import numpy as np
        NUM_HEADS = 12
        LN_EPS = 1e-05
        key = jax.random.key(seed)
        k1, k2, k3 = jax.random.split(key, 3)
        B, S, E = (8, 256, 192)
        x = jax.random.normal(k1, (B, S, E), dtype=jnp.float32)
        w_qkv = jax.random.normal(k2, (E, 3 * E), dtype=jnp.float32) * (1.0 / np.sqrt(E))
        b_qkv = jax.random.normal(k3, (3 * E,), dtype=jnp.float32) * 0.02
        ln_gamma = jnp.ones((E,), dtype=jnp.float32)
        ln_beta = jnp.zeros((E,), dtype=jnp.float32)
        return {'x': x, 'w_qkv': w_qkv, 'b_qkv': b_qkv, 'ln_gamma': ln_gamma, 'ln_beta': ln_beta}
    _L3_attn_all = _L3_attn_setup()
    _L3_attn_in = {k: v for k, v in _L3_attn_all.items() if k in ('w_qkv', 'b_qkv', 'ln_gamma', 'ln_beta')}
    del _L3_attn_all

    def _L3_ffn_setup():
        import jax, jax.numpy as jnp
        import numpy as np
        E = 8
        K = 2
        D = 192
        I = 768
        B, S = (2, 512)
        key = jax.random.key(seed)
        ks = jax.random.split(key, 8)
        x = jax.random.normal(ks[0], (B, S, D), dtype=jnp.float32)
        W1 = jax.random.normal(ks[1], (E, D, I), dtype=jnp.float32) * 0.02
        b1 = jnp.zeros((E, I), dtype=jnp.float32)
        W2 = jax.random.normal(ks[2], (E, I, D), dtype=jnp.float32) * 0.02
        b2 = jnp.zeros((E, D), dtype=jnp.float32)
        Wr = jax.random.normal(ks[3], (D, E), dtype=jnp.float32) * 0.02
        br = jnp.zeros((E,), dtype=jnp.float32)
        return {'x': x, 'W1': W1, 'b1': b1, 'W2': W2, 'b2': b2, 'Wr': Wr, 'br': br}
    _L3_ffn_all = _L3_ffn_setup()
    _L3_ffn_in = {k: v for k, v in _L3_ffn_all.items() if k in ('W1', 'b1', 'W2', 'b2', 'Wr', 'br')}
    del _L3_ffn_all
    return {'x': x, 'L0_tok_W': _L0_tok_in['W'], 'L0_tok_class_emb': _L0_tok_in['class_emb'], 'L0_tok_pos_emb': _L0_tok_in['pos_emb'], 'L0_attn_w_qkv': _L0_attn_in['w_qkv'], 'L0_attn_w_proj': _L0_attn_in['w_proj'], 'L0_attn_b_proj': _L0_attn_in['b_proj'], 'L0_ffn_W_qkv': _L0_ffn_in['W_qkv'], 'L0_ffn_b_qkv': _L0_ffn_in['b_qkv'], 'L0_ffn_W_gate': _L0_ffn_in['W_gate'], 'L0_ffn_b_gate': _L0_ffn_in['b_gate'], 'L0_ffn_A': _L0_ffn_in['A'], 'L0_ffn_B_lora': _L0_ffn_in['B_lora'], 'L0_ffn_W_proj': _L0_ffn_in['W_proj'], 'L0_ffn_b_proj': _L0_ffn_in['b_proj'], 'L1_attn_Wq': _L1_attn_in['Wq'], 'L1_attn_Wk': _L1_attn_in['Wk'], 'L1_attn_bk': _L1_attn_in['bk'], 'L1_attn_Wv': _L1_attn_in['Wv'], 'L1_attn_bv': _L1_attn_in['bv'], 'L1_attn_gq': _L1_attn_in['gq'], 'L1_attn_gk': _L1_attn_in['gk'], 'L1_attn_Wo': _L1_attn_in['Wo'], 'L1_attn_bo': _L1_attn_in['bo'], 'L1_ffn_gumbel_weights': _L1_ffn_in['gumbel_weights'], 'L1_ffn_n1l_g': _L1_ffn_in['n1l_g'], 'L1_ffn_n1l_b': _L1_ffn_in['n1l_b'], 'L1_ffn_n1s_g': _L1_ffn_in['n1s_g'], 'L1_ffn_n1s_b': _L1_ffn_in['n1s_b'], 'L1_ffn_w_qkv': _L1_ffn_in['w_qkv'], 'L1_ffn_w_proj': _L1_ffn_in['w_proj'], 'L1_ffn_b_proj': _L1_ffn_in['b_proj'], 'L1_ffn_n2l_g': _L1_ffn_in['n2l_g'], 'L1_ffn_n2l_b': _L1_ffn_in['n2l_b'], 'L1_ffn_n2s_g': _L1_ffn_in['n2s_g'], 'L1_ffn_n2s_b': _L1_ffn_in['n2s_b'], 'L1_ffn_w_fc1': _L1_ffn_in['w_fc1'], 'L1_ffn_b_fc1': _L1_ffn_in['b_fc1'], 'L1_ffn_w_fc2': _L1_ffn_in['w_fc2'], 'L1_ffn_b_fc2': _L1_ffn_in['b_fc2'], 'L2_attn_w_qkv': _L2_attn_in['w_qkv'], 'L2_attn_w_proj': _L2_attn_in['w_proj'], 'L2_attn_b_proj': _L2_attn_in['b_proj'], 'L2_ffn_weight_t': _L2_ffn_in['weight_t'], 'L2_ffn_bias': _L2_ffn_in['bias'], 'L3_attn_w_qkv': _L3_attn_in['w_qkv'], 'L3_attn_b_qkv': _L3_attn_in['b_qkv'], 'L3_attn_ln_gamma': _L3_attn_in['ln_gamma'], 'L3_attn_ln_beta': _L3_attn_in['ln_beta'], 'L3_ffn_W1': _L3_ffn_in['W1'], 'L3_ffn_b1': _L3_ffn_in['b1'], 'L3_ffn_W2': _L3_ffn_in['W2'], 'L3_ffn_b2': _L3_ffn_in['b2'], 'L3_ffn_Wr': _L3_ffn_in['Wr'], 'L3_ffn_br': _L3_ffn_in['br']}

def reference(x, L0_tok_W, L0_tok_class_emb, L0_tok_pos_emb, L0_attn_w_qkv, L0_attn_w_proj, L0_attn_b_proj, L0_ffn_W_qkv, L0_ffn_b_qkv, L0_ffn_W_gate, L0_ffn_b_gate, L0_ffn_A, L0_ffn_B_lora, L0_ffn_W_proj, L0_ffn_b_proj, L1_attn_Wq, L1_attn_Wk, L1_attn_bk, L1_attn_Wv, L1_attn_bv, L1_attn_gq, L1_attn_gk, L1_attn_Wo, L1_attn_bo, L1_ffn_gumbel_weights, L1_ffn_n1l_g, L1_ffn_n1l_b, L1_ffn_n1s_g, L1_ffn_n1s_b, L1_ffn_w_qkv, L1_ffn_w_proj, L1_ffn_b_proj, L1_ffn_n2l_g, L1_ffn_n2l_b, L1_ffn_n2s_g, L1_ffn_n2s_b, L1_ffn_w_fc1, L1_ffn_b_fc1, L1_ffn_w_fc2, L1_ffn_b_fc2, L2_attn_w_qkv, L2_attn_w_proj, L2_attn_b_proj, L2_ffn_weight_t, L2_ffn_bias, L3_attn_w_qkv, L3_attn_b_qkv, L3_attn_ln_gamma, L3_attn_ln_beta, L3_ffn_W1, L3_ffn_b1, L3_ffn_W2, L3_ffn_b2, L3_ffn_Wr, L3_ffn_br):
    import jax
    import jax.numpy as jnp

    def _L0_tok_ref(x, W, class_emb, pos_emb):
        import jax, jax.numpy as jnp
        import numpy as np
        P = 16
        D = 192

        def _patchify(x):
            B, H, W_, C = x.shape
            gh, gw = (H // P, W_ // P)
            x = x.reshape(B, gh, P, gw, P, C)
            x = x.transpose(0, 1, 3, 2, 4, 5)
            return x.reshape(B, gh * gw, P * P * C)
        B = x.shape[0]
        patches = _patchify(x)
        proj = jnp.einsum('bnk,kd->bnd', patches, W)
        cls = jnp.broadcast_to(class_emb, (B, 1, D))
        tokens = jnp.concatenate((cls, proj), axis=1)
        return tokens + pos_emb

    def _L0_attn_ref(x, w_qkv, w_proj, b_proj):
        import jax, jax.numpy as jnp
        import numpy as np
        NUM_HEADS = 12

        def _reference_tuple_inner(x, w_qkv, w_proj, b_proj):
            b, n, c = x.shape
            h = NUM_HEADS
            d = c // h
            qkv = (x @ w_qkv.T).reshape(b, n, 3, h, d).transpose(2, 0, 3, 1, 4)
            q, k, v = (qkv[0], qkv[1], qkv[2])
            q = jax.nn.elu(q) + 1.0
            k = jax.nn.elu(k) + 1.0
            kv = jnp.einsum('bhsd,bhse->bhde', k, v)
            z = 1.0 / jnp.einsum('bhsd,bhd->bhs', q, k.sum(axis=-2))
            out = jnp.einsum('bhde,bhsd,bhs->bhse', kv, q, z)
            out = out.transpose(0, 2, 1, 3).reshape(b, n, c)
            out = out @ w_proj.T + b_proj
            return (out, kv)
        return _reference_tuple_inner(x, w_qkv, w_proj, b_proj)[0]

    def _L0_ffn_ref(x, W_qkv, b_qkv, W_gate, b_gate, A, B_lora, W_proj, b_proj):
        import jax, jax.numpy as jnp
        import numpy as np
        B_SZ, S, D = (8, 128, 192)
        H = 12
        N_EXP = 8
        RANK = 16
        ALPHA = 32
        TOP_K = 2
        b, s, d = x.shape
        n_exp, rank = (A.shape[0], A.shape[1])
        scaling = ALPHA / rank
        head_dim = d // H
        scale = head_dim ** (-0.5)
        t = b * s
        x_flat = x.reshape(t, d)
        qkv_base = x @ W_qkv.T + b_qkv
        logits = x_flat @ W_gate.T + b_gate
        router_probs = jax.nn.softmax(logits, axis=-1)
        top_k_weights, top_k_indices = jax.lax.top_k(router_probs, TOP_K)
        a_down = jnp.einsum('td,nrd->tnr', x_flat, A)
        expert_out = jnp.einsum('tnr,nor->tno', a_down, B_lora) * scaling
        dispatch = jnp.zeros((t, n_exp), x.dtype).at[jnp.arange(t)[:, None], top_k_indices].add(top_k_weights)
        sparse_out = jnp.einsum('tno,tn->to', expert_out, dispatch)
        qkv = qkv_base + sparse_out.reshape(b, s, 3 * d)
        qkv = qkv.reshape(b, s, 3, H, head_dim).transpose(2, 0, 3, 1, 4)
        q, k, v = (qkv[0], qkv[1], qkv[2])
        attn = jax.nn.softmax(jnp.einsum('bhqd,bhkd->bhqk', q, k) * scale, axis=-1)
        out = jnp.einsum('bhqk,bhkd->bhqd', attn, v)
        out = out.transpose(0, 2, 1, 3).reshape(b, s, d)
        return out @ W_proj.T + b_proj

    def _L1_attn_ref(x, Wq, Wk, bk, Wv, bv, gq, gk, Wo, bo):
        import jax, jax.numpy as jnp
        import numpy as np
        NHEAD = 12
        EPS = 1e-05

        def layernorm_nobias(x, gamma):
            mu = jnp.mean(x, axis=-1, keepdims=True)
            var = jnp.var(x, axis=-1, keepdims=True)
            return (x - mu) * jax.lax.rsqrt(var + EPS) * gamma
        b, l, d = x.shape
        n = NHEAD
        hd = d // n
        scale = hd ** (-0.5)
        q = layernorm_nobias(x @ Wq.T, gq)
        k = layernorm_nobias(x @ Wk.T + bk, gk)
        v = x @ Wv.T + bv
        q = q.reshape(b, l, n, hd).transpose(0, 2, 1, 3)
        k = k.reshape(b, l, n, hd).transpose(0, 2, 1, 3)
        v = v.reshape(b, l, n, hd).transpose(0, 2, 1, 3)
        scores = jnp.einsum('bnqd,bnkd->bnqk', q, k) * scale
        attn = jax.nn.softmax(scores, axis=-2)
        o = jnp.einsum('bnqk,bnkd->bnqd', attn, v)
        o = o.transpose(0, 2, 1, 3).reshape(b, l, d)
        return o @ Wo.T + bo + x

    def _L1_ffn_ref(x, gumbel_weights, n1l_g, n1l_b, n1s_g, n1s_b, w_qkv, w_proj, b_proj, n2l_g, n2l_b, n2s_g, n2s_b, w_fc1, b_fc1, w_fc2, b_fc2):
        import jax, jax.numpy as jnp
        import numpy as np
        H = 12
        ALPHA = (1, 2, 3)
        DEPTH = 5
        BLOCK_DEPTH = 3
        TOTAL_DEPTH_M1 = 14 - 1
        SMALL_ACTIVE = BLOCK_DEPTH <= DEPTH <= TOTAL_DEPTH_M1 - BLOCK_DEPTH

        def _ln(x, g, b, eps=1e-05):
            m = jnp.mean(x, axis=-1, keepdims=True)
            v = jnp.mean((x - m) ** 2, axis=-1, keepdims=True)
            return (x - m) * jax.lax.rsqrt(v + eps) * g + b

        def _attn_branch(xp, w_qkv, w_proj, b_proj, keep_heads, keep_ch):
            B2, N, C = xp.shape
            hd = C // H
            scale = hd ** (-0.5)
            qkv = (xp @ w_qkv).reshape(B2, N, 3, H, hd).transpose(2, 0, 3, 1, 4)
            hmask = (jnp.arange(H) < keep_heads).astype(xp.dtype)[None, :, None, None]
            q, k, v = (qkv[0] * hmask, qkv[1] * hmask, qkv[2] * hmask)
            a = jax.nn.softmax(jnp.einsum('bhnd,bhmd->bhnm', q, k) * scale, axis=-1)
            o = jnp.einsum('bhnm,bhmd->bhnd', a, v).transpose(0, 2, 1, 3).reshape(B2, N, C)
            o = o @ w_proj + b_proj
            cmask = (jnp.arange(C) < keep_ch).astype(xp.dtype)
            return o * cmask

        def _mlp_branch(xp, w1, b1, w2, b2, keep_ch):
            C = xp.shape[-1]
            cmask = (jnp.arange(C) < keep_ch).astype(xp.dtype)
            h = jax.nn.gelu(xp * cmask @ w1 + b1, approximate=False)
            return (h @ w2 + b2) * cmask
        B, N, C = x.shape
        B2 = B // 2
        nl = _ln(x[:B2], n1l_g, n1l_b)
        ns = _ln(x[B2:], n1s_g, n1s_b)
        a_large = _attn_branch(nl, w_qkv, w_proj, b_proj, H, C)
        if SMALL_ACTIVE:
            a_small = sum((gumbel_weights[i] * _attn_branch(ns, w_qkv, w_proj, b_proj, H // ALPHA[i], C // ALPHA[i]) for i in range(3)))
            attn_out = jnp.concatenate([a_large, a_small], axis=0)
        else:
            attn_out = jnp.concatenate([a_large, a_large], axis=0)
        x = x + attn_out
        nl2 = _ln(x[:B2], n2l_g, n2l_b)
        ns2 = _ln(x[B2:], n2s_g, n2s_b)
        m_large = _mlp_branch(nl2, w_fc1, b_fc1, w_fc2, b_fc2, C)
        if SMALL_ACTIVE:
            m_small = sum((gumbel_weights[i] * _mlp_branch(ns2, w_fc1, b_fc1, w_fc2, b_fc2, C // ALPHA[i]) for i in range(3)))
            mlp_out = jnp.concatenate([m_large, m_small], axis=0)
        else:
            mlp_out = jnp.concatenate([m_large, m_large], axis=0)
        return x + mlp_out

    def _L2_attn_ref(x, w_qkv, w_proj, b_proj):
        import jax, jax.numpy as jnp
        import numpy as np
        import math
        DIM = 192
        NUM_HEADS = 12
        HEAD_DIM = DIM // NUM_HEADS
        ORDER = 2
        SCALE = HEAD_DIM ** (-0.5)
        B, N, C = x.shape
        H, Dh = (NUM_HEADS, HEAD_DIM)
        qkv = (x @ w_qkv).reshape(B, N, 3, H, Dh)
        qkv = jnp.transpose(qkv, (2, 0, 3, 1, 4))
        q, k, v = (qkv[0], qkv[1], qkv[2])
        q = q * SCALE
        qk = jnp.einsum('bhnd,bhmd->bhnm', q, k)
        attn = jnp.ones_like(qk)
        x_power = qk
        for i in range(1, ORDER + 1):
            attn = attn + x_power / math.factorial(i)
            if i < ORDER:
                x_power = x_power * qk
        attn = jax.nn.relu(attn)
        attn = attn / jnp.sum(attn, axis=-1, keepdims=True)
        out = jnp.einsum('bhnm,bhmd->bhnd', attn, v)
        out = jnp.transpose(out, (0, 2, 1, 3)).reshape(B, N, C)
        return out @ w_proj + b_proj

    def _L2_ffn_ref(x, weight_t, bias):
        import jax, jax.numpy as jnp
        import numpy as np
        ACT_SCALE = 0.02
        W_SCALE = 0.01
        EFF_SCALE = ACT_SCALE * W_SCALE
        B, S, D, M = (8, 1024, 192, 192)
        orig_shape = x.shape
        x_flat = x.reshape(-1, orig_shape[-1])
        x_int8 = jnp.clip(jnp.round(x_flat / ACT_SCALE), -128, 127).astype(jnp.int8)
        acc_i32 = jnp.matmul(x_int8, weight_t, preferred_element_type=jnp.int32)
        out = acc_i32.astype(jnp.float32) * jnp.float32(EFF_SCALE) + bias
        return out.reshape(orig_shape[:-1] + (M,))

    def _L3_attn_ref(x, w_qkv, b_qkv, ln_gamma, ln_beta):
        import jax, jax.numpy as jnp
        import numpy as np
        NUM_HEADS = 12
        LN_EPS = 1e-05
        B, S, E = x.shape
        H = NUM_HEADS
        D = E // H
        qkv = x @ w_qkv + b_qkv
        qkv = qkv.reshape(B, S, 3, H, D)
        q, k, v = (qkv[:, :, 0], qkv[:, :, 1], qkv[:, :, 2])
        scores = jnp.einsum('bshd,bthd->bhst', q, k) / jnp.sqrt(jnp.float32(D))
        attn = jax.nn.softmax(scores, axis=-1)
        out = jnp.einsum('bhst,bthd->bshd', attn, v)
        out = out.reshape(B, S, E)
        y = x + out
        mean = jnp.mean(y, axis=-1, keepdims=True)
        var = jnp.var(y, axis=-1, keepdims=True)
        y = (y - mean) * jax.lax.rsqrt(var + LN_EPS)
        return y * ln_gamma + ln_beta

    def _L3_ffn_ref(x, W1, b1, W2, b2, Wr, br):
        import jax, jax.numpy as jnp
        import numpy as np
        E = 8
        K = 2
        D = 192
        I = 768
        B, S = (2, 512)
        Bv, Sv, Dv = x.shape
        xf = x.reshape(-1, Dv)
        logits = xf @ Wr + br
        gates = jax.nn.softmax(logits, axis=-1)
        top_g, top_i = jax.lax.top_k(gates, K)
        out = jnp.zeros_like(xf)
        for e in range(E):
            w_e = jnp.sum(top_g * (top_i == e), axis=-1)
            h = jax.nn.gelu(xf @ W1[e] + b1[e], approximate=False)
            y = h @ W2[e] + b2[e]
            out = out + w_e[:, None] * y
        return out.reshape(Bv, Sv, Dv)
    h = _L0_tok_ref(x, L0_tok_W, L0_tok_class_emb, L0_tok_pos_emb)
    h = h + _L0_attn_ref(_layernorm(h, axis=-1), L0_attn_w_qkv, L0_attn_w_proj, L0_attn_b_proj)
    h = h + _L0_ffn_ref(_layernorm(h, axis=-1), L0_ffn_W_qkv, L0_ffn_b_qkv, L0_ffn_W_gate, L0_ffn_b_gate, L0_ffn_A, L0_ffn_B_lora, L0_ffn_W_proj, L0_ffn_b_proj)
    h = h + _L1_attn_ref(_layernorm(h, axis=-1), L1_attn_Wq, L1_attn_Wk, L1_attn_bk, L1_attn_Wv, L1_attn_bv, L1_attn_gq, L1_attn_gk, L1_attn_Wo, L1_attn_bo)
    h = h + _L1_ffn_ref(_layernorm(h, axis=-1), L1_ffn_gumbel_weights, L1_ffn_n1l_g, L1_ffn_n1l_b, L1_ffn_n1s_g, L1_ffn_n1s_b, L1_ffn_w_qkv, L1_ffn_w_proj, L1_ffn_b_proj, L1_ffn_n2l_g, L1_ffn_n2l_b, L1_ffn_n2s_g, L1_ffn_n2s_b, L1_ffn_w_fc1, L1_ffn_b_fc1, L1_ffn_w_fc2, L1_ffn_b_fc2)
    h = h + _L2_attn_ref(_layernorm(h, axis=-1), L2_attn_w_qkv, L2_attn_w_proj, L2_attn_b_proj)
    h = h + _L2_ffn_ref(_layernorm(h, axis=-1), L2_ffn_weight_t, L2_ffn_bias)
    h = h + _L3_attn_ref(_layernorm(h, axis=-1), L3_attn_w_qkv, L3_attn_b_qkv, L3_attn_ln_gamma, L3_attn_ln_beta)
    h = h + _L3_ffn_ref(_layernorm(h, axis=-1), L3_ffn_W1, L3_ffn_b1, L3_ffn_W2, L3_ffn_b2, L3_ffn_Wr, L3_ffn_br)
    return h

_drawn_inputs = setup_inputs


def setup_inputs(seed=0):
    import zlib

    import numpy as np

    out = dict(_drawn_inputs(seed))
    spreads = {'L0_tok_class_emb': (0.0, 0.1),
     'L0_attn_b_proj': (0.0, 0.1),
     'L0_ffn_b_qkv': (0.0, 0.1),
     'L0_ffn_b_gate': (0.0, 0.8),
     'L0_ffn_b_proj': (0.0, 0.1),
     'L1_attn_gq': (1.0, 0.2),
     'L1_attn_gk': (1.0, 0.2),
     'L1_attn_bo': (0.0, 0.1),
     'L1_ffn_n1l_g': (1.0, 0.6),
     'L1_ffn_n1l_b': (0.0, 0.8),
     'L1_ffn_n1s_g': (1.0, 0.6),
     'L1_ffn_n1s_b': (0.0, 0.8),
     'L1_ffn_b_proj': (0.0, 0.1),
     'L1_ffn_n2l_g': (1.0, 0.6),
     'L1_ffn_n2l_b': (0.0, 2.0),
     'L1_ffn_n2s_g': (1.0, 0.6),
     'L1_ffn_n2s_b': (0.0, 2.0),
     'L1_ffn_b_fc1': (0.0, 0.699),
     'L1_ffn_b_fc2': (0.0, 0.1),
     'L3_attn_ln_gamma': (1.0, 0.6),
     'L3_attn_ln_beta': (0.0, 0.8),
     'L3_ffn_b1': (0.0, 0.8),
     'L3_ffn_b2': (0.0, 0.8),
     'L3_ffn_br': (0.0, 0.8)}
    factors = {'L0_ffn_W_gate': 8.0,
     'L0_ffn_A': 8.0,
     'L0_ffn_B_lora': 8.0,
     'L1_attn_bk': 8.0,
     'L1_attn_bv': 3.148,
     'L1_ffn_gumbel_weights': 6.625,
     'L1_ffn_w_qkv': 6.297,
     'L1_ffn_w_proj': 6.185,
     'L2_attn_b_proj': 6.011,
     'L3_attn_b_qkv': 24.853,
     'L3_ffn_W1': 8.0,
     'L3_ffn_W2': 8.0,
     'L3_ffn_Wr': 8.0}
    for name, (base, spread) in spreads.items():
        noise = np.random.default_rng([zlib.crc32(name.encode()), seed]).standard_normal(out[name].shape)
        drawn = base * np.exp(spread * noise) if base else spread * noise
        out[name] = jnp.asarray(drawn.astype(out[name].dtype))
    for name, factor in factors.items():
        out[name] = (out[name] * factor).astype(out[name].dtype)
    return out
```

```python
import concourse.bass as bass
from concourse import mybir
from contextlib import ExitStack

B, TOK, D, H = 16, 37, 192, 12
HD = D // H
PAIRS = B // 2
GAP = 64
ROWS = GAP + TOK
T = B * TOK
HALF = D // 2
HH = H // 2
NG, HG = 4, 3
GR = HG * TOK
Q8 = 8
QT = Q8 * TOK
PATCH_K = 6
HID, MT = 768, 6
NE, RANK, TOPK = 8, 16, 2
CT = 5
TPAD = CT * 128
EPS = 1e-5
LORA_SCALE = 2.0
ACT_SCALE, EFF_SCALE = 0.02, 0.02 * 0.01
ROUND = 1.5 * 2.0 ** 23
SCALE = HD ** -0.5

SEGS = [("A_qkv", 3 * D), ("A_proj", D), ("B_qkv", 3 * D), ("B_gate", NE), ("B_down", 128), ("B_proj", D),
        ("C_qkv", 3 * D), ("C_proj", D), ("D_qkv", 3 * D), ("D_proj", D), ("D_fc1", HID),
        ("E_qkv", 3 * D), ("E_proj", D), ("G_qkv", 3 * D), ("H_gate", NE)]
SEG_DRAM, WCOLS = {}, 0
for _n, _w in SEGS:
    SEG_DRAM[_n] = WCOLS
    WCOLS += 2 * _w
LATE = SEG_DRAM["E_qkv"]
SEG_AT = {_n: (SEG_DRAM[_n] % LATE, _w) for _n, _w in SEGS}
W1_AT = WCOLS - LATE
W2_AT = W1_AT + 2 * 2 * HID
WT_COLS = W2_AT + 2 * MT * D
LOADS = [("A_qkv", "A_proj"), ("B_qkv", "B_proj"), ("C_qkv", "C_proj"), ("D_qkv", "D_fc1"), ("E_qkv", "H_gate")]

CONSTS = [("ident", 128), ("mask_k", HH), ("ones_g", 2 * HALF), ("mask_v", D), ("mask_kv", HH * (HD + 1)),
          ("tri", NE * NE), ("expand", 128), ("m96", 2 * D), ("m64", 2 * D), ("c96", 2), ("c64", 2)]
CONST_AT, CCOLS = {}, 0
for _n, _w in CONSTS:
    CONST_AT[_n] = (CCOLS, _w)
    CCOLS += _w

PARAMS = [("n1l_g", 2), ("n1l_b", 2), ("n1s_g", 2), ("n1s_b", 2), ("n2l_g", 2), ("n2l_b", 2), ("n2s_g", 2),
          ("n2s_b", 2), ("gq", 2), ("gk", 2), ("b_fc1", MT), ("b_fc2", 2), ("b1", NE * MT), ("gumbel", 3),
          ("bias_q", D), ("gamma", D), ("beta", D), ("pos", D), ("cls", D)]
PARAM_AT, PCOLS = {}, 0
for _n, _w in PARAMS:
    PARAM_AT[_n] = (PCOLS, _w)
    PCOLS += _w

LINEAR, SOFTMAX, COLUMN, POLY = "linear", "softmax", "column", "poly"
ATT = [("A", LINEAR), ("B", SOFTMAX), ("C", COLUMN), ("D", SOFTMAX), ("E", POLY), ("G", SOFTMAX)]
KIND = dict(ATT)
HAS_PROJ = "ABCDE"
ET_JOBS = [(i, min(3, B - i)) for i in range(0, B, 3)]


def nt_jobs(n):
    return [("nT", n, q, s) for q in range(2) for s in range(2)]


def job_order():
    jobs = [("tok", p) for p in range(PAIRS // 2)]
    for n, kind in ATT:
        jobs += nt_jobs(n)
        if n == "B":
            jobs += [("gate", "B")] + [("dT", q) for q in range(2)]
            jobs += [(k, q) for q in range(2) for k in ("dx", "a")]
        if kind == COLUMN:
            jobs += [("qk", p) for p in range(PAIRS)]
            jobs += [(k, n, q, s) for q in range(2) for s in range(2) for k in ("q", "k")]
        elif kind == LINEAR:
            jobs += [("q", n, q, s) for q in range(2) for s in range(2)]
            jobs += [("kv", p) for p in range(PAIRS)]
            jobs += [("kvm", c, par) for c in range(PAIRS // 2) for par in range(2)]
            jobs += [("lo", c) for c in range(PAIRS // 2)]
            jobs += [("oT", n, q, s) for q in range(2) for s in range(2)]
        else:
            jobs += [(k, n, q, s) for q in range(2) for s in range(2) for k in ("q", "k")]
        if kind == SOFTMAX:
            jobs += [("s", n, p) for p in range(4)]
            jobs += [("v", n, p) for p in range(4)]
            for q in range(2):
                jobs += [("t", n, 4 * q + p) for p in range(4)]
                if q == 0:
                    jobs += [("s", n, 4 + p) for p in range(4)]
                    jobs += [("v", n, 4 + p) for p in range(4)]
                jobs += [(k, n, q, s) for s in range(2) for k in ("d", "o")]
        if kind in (COLUMN, POLY):
            jobs += [("e", n, j) for j in range(3)]
            jobs += [("v", n, p) for p in range(4)]
            jobs += [("e", n, j) for j in range(3, 6)]
            jobs += [("v", n, p) for p in range(4, 8)]
            for q in range(2):
                jobs += [(k, n, q, s) for s in range(2) for k in (("d", "o") if kind == POLY else ("o",))]
        if n in HAS_PROJ:
            jobs += [("p", n, c) for c in range(PAIRS // 2)]
        else:
            jobs += [("back", n, c) for c in range(PAIRS // 2)]
        if n == "D":
            jobs += nt_jobs("D2")
            jobs += [("f1", q, br, m) for q, br in MLP for m in range(MT)][:MT]
            jobs += [("f1", 1, 0, m) for m in range(MT)]
            jobs += [("f2", 0, s) for s in range(2)]
            jobs += [("f1", 1, br, m) for br in (1, 2) for m in range(MT)]
            jobs += [("f2", 1, s) for s in range(2)]
            jobs += [("back", "M", c) for c in range(PAIRS // 2)]
        if n == "E":
            jobs += nt_jobs("F") + [("int", c) for c in range(PAIRS // 2)]
    jobs += nt_jobs("H") + [("gate", "H"), ("eT", 0), ("eT", 1)] + [("eb", c) for c in range(3)]
    return jobs


UPD = ("tok", "Dy", "F", "G", "D", "Gy")
MLP = [(0, 0), (1, 0), (1, 1), (1, 2)]
KEEP = [D, D // 2, D // 3]


class Signal:

    def __init__(self, sem, events):
        self.sem, self.index, self.seen = sem, {e: i for i, e in enumerate(events)}, 0

    def inc(self, event):
        assert self.index[event] == self.seen, (event, self.seen)
        self.seen += 1
        return self.sem, 1

    def at(self, event):
        return self.sem, self.index[event] + 1


def build_tower(nc, patches, wpack, c128, consts, params, w8, b2e, w1, w2, out):
    F, FB = mybir.dt.float32, mybir.dt.bfloat16
    ALU, ACT, AX = mybir.AluOpType, mybir.ActivationFunctionType, mybir.AxisListType
    ctx = ExitStack()
    with ctx:
        def sb(name, shape, dt=F):
            return ctx.enter_context(nc.sbuf_tensor(name, shape, dt))

        def sem(name):
            return ctx.enter_context(nc.semaphore(name))

        wt = sb("weights", [128, WT_COLS])
        cst = sb("constants", [128, CCOLS])
        par = sb("parameters", [128, PCOLS])
        tokw = sb("tok_w", [128, PATCH_K, D])
        bup = sb("lora_up", [128, 3 * D])
        fc2w = sb("fc2_w", [128, MT, D])
        h = sb("h", [128, PAIRS, D])
        xn = sb("xn", [128, PAIRS, D])
        xy = sb("x2_y", [128, 2, PAIRS, D])
        x2 = xy[:, 0]
        yt = xy[:, 1]
        adrep = xy[:].rearrange("p a c d -> p (a c d)")[:, 0:B * GR].rearrange("p (i c) -> p i c", c=GR)
        nT = [sb(f"nT{s}", [97, B, GAP]) for s in range(2)]
        oT = [sb(f"oT{s}", [97, B, GAP]) for s in range(2)]
        qT = [sb(f"qT{s}", [96, T]) for s in range(2)]
        rep_raw = sb("rep", [128, 2 * B * GR])
        nrep = [rep_raw[0:97, s * B * GR:(s + 1) * B * GR].rearrange("p (i c) -> p i c", c=GR) for s in range(2)]
        big = sb("arena_k", [128, 2 * HH * T])
        kblk = [big[0:96, s * HH * T:(s + 1) * HH * T].rearrange("p (i h k) -> p i h k", h=HH, k=TOK) for s in range(2)]
        patch = big[:, 0:PAIRS * PATCH_K * ROWS].rearrange("p (c k t) -> p c k t", k=PATCH_K, t=ROWS)
        hid = big[:, 0:4 * MT * QT].rearrange("p (b m t) -> p b m t", b=4, t=QT)
        hbuf = [big[:, b * MT * 592:(b + 1) * MT * 592].rearrange("p (m t) -> p m t", t=592) for b in range(2)]
        vblk = sb("vblk", [GR, B, NG, HALF])
        ar = sb("arena_e", [128, 4, H * TOK])
        arf = ar[:].rearrange("p c k -> p (c k)")
        et_raw = sb("et", [128, NG * T])
        et = et_raw[0:GR].rearrange("p (g t) -> p g t", t=T)
        ad, dX, dispT = et_raw[:, 0:T], et_raw[:, T:2 * T], et_raw[0:NE, 2 * T:3 * T]
        disp = sb("disp", [128, PAIRS, NE])
        gts = sb("gating", [128, 2, PAIRS * NE * NE])
        gsm = sb("gates", [128, 4, PAIRS * NE])
        rd = sb("rden", [96, 2, QT])
        stats = sb("stats", [128, 2 * PAIRS, 6])
        mv = sb("mean_var", [128, 2 * PAIRS, 2])
        rstd = sb("rstd", [128, 2 * PAIRS])
        rtmp = sb("rstd_tmp", [128, 2, 2 * PAIRS])
        mhalf = sb("minus_half", [128, 2 * PAIRS])
        mx = sb("score_max", [128, 8, H])
        rs = sb("row_recip", [128, 8, 2 * H])
        maskg = sb("mask_k_gain", [96, 2, HH])
        wps = sb("proj_small", [97, 2, D])
        b2s = sb("b_fc2_small", [96, 2])
        gcol = sb("gumbel_cols", [96, 2, 2])
        fc2s = [tokw[:]] + [sb(f"fc2_small{i}", [128, MT, KEEP[i]])[:] for i in (1, 2)]
        w8i = sb("w8_int", [96, 2 * D // 4], mybir.dt.int32)
        w8b = sb("w8_bf16", [96, 2, D], FB)
        nq = sb("n_quant", [96, 2, B, GAP], FB)
        b2t = sb("expert_b2", [NE, D])
        b1cur = sb("expert_b1", [128, 2, MT])

        PS = [ctx.enter_context(nc.psum_tensor(f"bank{b}", [128, 512], F)) for b in range(8)]

        def w(name, k, a=0, n=None):
            at, width = SEG_AT[name]
            n = width if n is None else n
            return wt[0:96 + k, at + k * width + a:at + k * width + a + n]

        def con(name, rows=128):
            at, width = CONST_AT[name]
            return cst[0:rows, at:at + width]

        def prm(name, rows=128):
            at, width = PARAM_AT[name]
            return par[0:rows, at:at + width]

        ident = con("ident")

        order = job_order()
        where = {j: (i % 8, i // 8) for i, j in enumerate(order)}
        bank_filled = [sem(f"bank{b}_filled") for b in range(8)]
        bank_read = [sem(f"bank{b}_read") for b in range(8)]
        filled_seen, read_seen = [0] * 8, [0] * 8

        def bank(j):
            return PS[where[j][0]]

        def filled(j):
            b, k = where[j]
            return bank_filled[b], k + 1

        def evacuated(j):
            b, k = where[j]
            return bank_read[b], k + 1

        def updated(name, c):
            return {"tok": evacuated(("tok", c)), "Dy": evacuated(("p", "D", c)), "F": evacuated(("int", c)), "D": evacuated(("back", "M", c)),
                    "Gy": evacuated(("back", "G", c)), "G": g_done.at(c)}[name] if name in UPD else evacuated(("p", name, c))

        def freed(j):
            return bank_read[where[j][0]], 1

        loaded = {n: sem(f"loaded_{n}") for n in ["consts", "params", "tokw", "bup", "fc2w", "w8", "b2e"]
                  + [f"patch{c}" for c in range(2)] + [a for a, _ in LOADS]}
        lns = ["A", "B", "C", "D", "D2", "E", "F", "G", "G2", "H"]
        lnq = [(n, q) for n in lns for q in range(2)]
        g_done = Signal(sem("g_done"), range(4))
        var_ready = Signal(sem("var_ready"), lnq[:6] + [("Cqk", p) for p in range(8)] + lnq[6:])
        rstd_ready = Signal(sem("rstd_ready"), lnq[:6] + [("Cqk", p) for p in range(8)] + lnq[6:])
        xn_ready = Signal(sem("xn_ready"), lnq)
        rep_ready = Signal(sem("rep_ready"), [(n, q) for n in "BCDEG" for q in range(2)])
        adrep_ready = sem("adrep_ready")
        h_plus = Signal(sem("h_plus"), [(n, q) for n in ["C", "D", "F"] for q in range(2)])
        exp_ready = Signal(sem("exp_ready"), [(n, p) for n in "BDG" for p in range(8)])
        eexp = Signal(sem("eexp"), [(n, j) for n in "CE" for j in range(6)])
        et_ready = Signal(sem("et_ready"), [(n, j) for n in "CE" for j in range(6)])
        elu_exp = Signal(sem("elu_exp"), [("q", q, s) for q in range(2) for s in range(2)]
                         + [("k", p) for p in range(8)])
        zeroed = sem("zeroed")
        mixed = sem("mixed")
        gate_exp = Signal(sem("gate_exp"), ["B", "H"])
        disp_ready = Signal(sem("disp_ready"), ["B", "H"])
        wconv = sem("w8_converted")
        nq_ready = Signal(sem("nq_ready"), [(q, s) for q in range(2) for s in range(2)])
        dve_chain = sem("dve_chain")
        pool_chain = sem("pool_chain")
        b1_ready = sem("b1_ready")
        fc1_done, gelu_done = sem("fc1_done"), sem("gelu_done")
        fc2_done, acc_done = sem("fc2_done"), sem("acc_done")
        w1_loaded = [sem(f"w1_loaded{b}") for b in range(2)]
        w2_loaded = [sem(f"w2_loaded{b}") for b in range(2)]
        h_stored, h_back, stored = sem("h_stored"), sem("h_back"), sem("stored")

        w1b = wt[0:96, W1_AT:W2_AT].rearrange("p (b k n) -> p b k n", b=2, k=2)
        w2b = wt[:, W2_AT:WT_COLS].rearrange("p (b m d) -> p b m d", b=2, m=MT)
        xc = rep_raw[0:97, 0:2 * TPAD].rearrange("p (s t) -> p s t", s=2)
        hc = rep_raw[:, 2 * TPAD:2 * TPAD + CT * D].rearrange("p (c d) -> p c d", d=D)
        acc = rep_raw[:, 2 * TPAD + CT * D:2 * TPAD + 2 * CT * D].rearrange("p (c d) -> p c d", d=D)
        scratch = nc.dram_tensor("h_compact", (T, D), F).ap()
        crow = [min(128, T - 128 * c) for c in range(CT)]

        block = ctx.enter_context(nc.Block())

        @block.sync
        def _(sp):
            sp.dma_start(tokw[:], c128[:, 0:PATCH_K * D].rearrange("p (k d) -> p k d", d=D)).then_inc(loaded["tokw"], 16)
            for c in range(2):
                sp.dma_start(patch[:, 4 * c:4 * c + 4], patches[:, 4 * c:4 * c + 4]).then_inc(loaded[f"patch{c}"], 16)
            sp.dma_start(par[:], params).then_inc(loaded["params"], 16)
            sp.dma_start(w8i[:], w8).then_inc(loaded["w8"], 16)
            sp.dma_start(b2t[:], b2e).then_inc(loaded["b2e"], 16)
            for first, last in LOADS:
                a, z = SEG_AT[first][0], SEG_AT[last][0] + 2 * SEG_AT[last][1]
                late = first == "E_qkv"
                if late:
                    sp.wait_ge(*updated("B", 3))
                d = SEG_DRAM[first]
                sp.dma_start(wt[0:97, a:z], wpack[:, d:d + z - a]).then_inc(loaded[first], 16)
                if first == "A_qkv":
                    sp.dma_start(bup[:], c128[:, PATCH_K * D:PATCH_K * D + 3 * D]).then_inc(loaded["bup"], 16)
                if first == "C_qkv":
                    sp.dma_start(fc2w[:], c128[:, PATCH_K * D + 3 * D:].rearrange("p (m d) -> p m d", d=D)).then_inc(loaded["fc2w"], 16)
            sp.wait_ge(*updated("D", 3))
            for b in range(2):
                sp.dma_start(w1b[:, b], w1[b]).then_inc(w1_loaded[b], 16)
                sp.dma_start(w2b[:, b], w2[b]).then_inc(w2_loaded[b], 16)
            sp.wait_ge(*updated("G", 3))
            hd = scratch.rearrange("(p i k) d -> i k p d", i=2, k=TOK)
            for i in range(2):
                sp.dma_start(hd[i], h[GAP * i:GAP * i + TOK]).then_inc(h_stored, 16)
            sp.wait_ge(h_stored, 32)
            sp.dma_start(hc[:, 0:CT - 1], scratch[0:128 * (CT - 1)].rearrange("(c p) d -> p c d", p=128)).then_inc(h_back, 16)
            sp.dma_start(hc[0:crow[-1], CT - 1], scratch[128 * (CT - 1):T]).then_inc(h_back, 16)
            with sp.Fori(0, NE // 2 - 1) as i:
                for b in range(2):
                    sp.wait_ge(fc1_done, i * 24 + 12 * (b + 1))
                    sp.dma_start(w1b[:, b], w1[i * 2 + (2 + b)]).then_inc(w1_loaded[b], 16)
                    sp.wait_ge(fc2_done, i * 6 + 3 * (b + 1))
                    sp.dma_start(w2b[:, b], w2[i * 2 + (2 + b)]).then_inc(w2_loaded[b], 16)
            sp.wait_ge(acc_done, 3 * NE)
            sp.dma_start(out[0:128 * (CT - 1)].rearrange("(c p) d -> p c d", p=128), acc[:, 0:CT - 1]).then_inc(stored, 16)
            sp.dma_start(out[128 * (CT - 1):T], acc[0:crow[-1], CT - 1]).then_inc(stored, 16)
            sp.wait_ge(stored, 32)

        @block.gpsimd
        def _(pool):
            g = nc.gpsimd
            links = [0]

            def link(ins):
                links[0] += 1
                ins.then_inc(pool_chain, 1)
                pool.wait_ge(pool_chain, links[0])

            link(g.memset(mhalf[:], -0.5))
            link(g.memset(vblk[:], 0.0))
            link(g.memset(nq[:], 0.0))

            def root(ln, q=None, p=None):
                key = (ln, q if p is None else p)
                a = slice(4 * q, 4 * q + 4) if p is None else slice(2 * p, 2 * p + 2)
                pool.wait_ge(*var_ready.at(key))
                link(g.tensor_scalar(rtmp[0:ROWS, 0, a], mv[0:ROWS, a, 1], EPS, None, ALU.add))
                if ln == "D":
                    link(g.tensor_tensor(rstd[0:ROWS, a], rtmp[0:ROWS, 0, a], mhalf[0:ROWS, a], ALU.pow))
                    link(g.tensor_tensor(rtmp[0:ROWS, 0, a], mv[0:ROWS, a, 1], rstd[0:ROWS, a], ALU.mult))
                    link(g.tensor_tensor(rtmp[0:ROWS, 0, a], rtmp[0:ROWS, 0, a], rstd[0:ROWS, a], ALU.mult))
                    link(g.tensor_scalar(rtmp[0:ROWS, 0, a], rtmp[0:ROWS, 0, a], EPS, None, ALU.add))
                    g.tensor_tensor(rtmp[0:ROWS, 1, a], rtmp[0:ROWS, 0, a], mhalf[0:ROWS, a], ALU.pow).then_inc(*rstd_ready.inc(key))
                    pool.wait_ge(*rstd_ready.at(key))
                else:
                    g.tensor_tensor(rstd[0:ROWS, a], rtmp[0:ROWS, 0, a], mhalf[0:ROWS, a], ALU.pow).then_inc(*rstd_ready.inc(key))
                    pool.wait_ge(*rstd_ready.at(key))

            def replicate(n, q):
                for s in range(2):
                    pool.wait_ge(*evacuated(("nT", n, q, s)))
                    ins = g.tensor_copy(
                        nrep[s][0:96, Q8 * q:Q8 * q + Q8].rearrange("p i (r k) -> p i r k", k=TOK),
                        nT[s][0:96, Q8 * q:Q8 * q + Q8, 0:TOK].unsqueeze(2).broadcast_to([96, Q8, HG, TOK]))
                    if s == 1:
                        ins.then_inc(*rep_ready.inc((n, q)))
                        pool.wait_ge(*rep_ready.at((n, q)))
                    else:
                        link(ins)

            def add_to_h(n, src, q, wait):
                pool.wait_ge(*wait)
                g.tensor_tensor(h[0:ROWS, 4 * q:4 * q + 4], h[0:ROWS, 4 * q:4 * q + 4], src, ALU.add).then_inc(*h_plus.inc((n, q)))
                pool.wait_ge(*h_plus.at((n, q)))

            for q in range(2):
                root("A", q)
            pool.wait_ge(loaded["params"], 16)
            pool.wait_ge(loaded["consts"], 16)
            pool.wait_ge(loaded["D_qkv"], 16)
            pool.wait_ge(loaded["fc2w"], 16)
            gw = prm("gumbel")
            m96, m64 = con("m96", 97), con("m64", 97)
            gm = m96.rearrange("p (k d) -> p k d", k=2)
            link(g.tensor_scalar(m96, m96, gw[0:97, 1:2], gw[0:97, 0:1], ALU.mult, ALU.add))
            link(g.tensor_scalar(m64, m64, gw[0:97, 2:3], None, ALU.mult))
            link(g.tensor_tensor(m96, m96, m64, ALU.add))
            for k in range(2):
                link(g.tensor_tensor(wps[0:96 + k, k], w("D_proj", k), gm[0:96 + k, k], ALU.mult))
            link(g.tensor_scalar(gcol[:, 0], con("c96", 96), gw[0:96, 1:2], gw[0:96, 0:1], ALU.mult, ALU.add))
            link(g.tensor_scalar(gcol[:, 1], con("c64", 96), gw[0:96, 2:3], None, ALU.mult))
            link(g.tensor_tensor(gcol[:, 0], gcol[:, 0], gcol[:, 1], ALU.add))
            link(g.tensor_tensor(b2s[:], prm("b_fc2", 96), gcol[:, 0], ALU.mult))
            pool.wait_ge(*filled(("tok", 3)))
            for i in range(3):
                g.tensor_scalar(fc2s[i], fc2w[:, :, 0:KEEP[i]], gw[:, i:i + 1], None, ALU.mult).then_inc(mixed, 1)
                pool.wait_ge(mixed, i + 1)
            pool.wait_ge(loaded["w8"], 16)
            g.tensor_copy(w8b[:].rearrange("p k d -> p (k d)"), w8i[:].bitcast(mybir.dt.int8)).then_inc(wconv, 1)
            pool.wait_ge(wconv, 1)

            for q in range(2):
                root("B", q)
            for q in range(2):
                replicate("B", q)
            for q in range(2):
                pool.wait_ge(*evacuated(("a", q)))
                g.tensor_copy(adrep[:, Q8 * q:Q8 * q + Q8].rearrange("p i (r k) -> p i r k", k=TOK),
                              ad[:, QT * q:QT * q + QT].rearrange("p (i k) -> p i k", k=TOK).unsqueeze(2)
                              .broadcast_to([128, Q8, HG, TOK])).then_inc(adrep_ready, 1)
                pool.wait_ge(adrep_ready, q + 1)
            for q in range(2):
                root("C", q)
            for q in range(2):
                add_to_h("C", xn[0:ROWS, 4 * q:4 * q + 4], q, xn_ready.at(("C", q)))
            for q in range(2):
                replicate("C", q)
            for p in range(PAIRS):
                root("Cqk", p=p)
            for q in range(2):
                root("D", q)
            for q in range(2):
                replicate("D", q)
            for q in range(2):
                add_to_h("D", yt[0:ROWS, 4 * q:4 * q + 4], q, updated("Dy", 2 * q + 1))
            for q in range(2):
                root("D2", q)
            for q in range(2):
                root("E", q)
            for q in range(2):
                replicate("E", q)
            for q in range(2):
                root("F", q)
            for q in range(2):
                add_to_h("F", prm("bias_q", ROWS).unsqueeze(1).broadcast_to([ROWS, 4, D]), q, xn_ready.at(("F", q)))
            for q in range(2):
                root("G", q)
            for q in range(2):
                replicate("G", q)
            for n in ("G2", "H"):
                for q in range(2):
                    root(n, q)

        @block.scalar
        def _(act):
            sc = nc.scalar
            act.dma_start(cst[:], consts).then_inc(loaded["consts"], 16)

            def nt_copy(n, q, s):
                j = ("nT", n, q, s)
                act.wait_ge(*filled(j))
                src = bank(j)[0:96, :].rearrange("p (i k) -> p i k", k=GAP)[:, :, 0:TOK]
                act_out = nT[s][0:96, Q8 * q:Q8 * q + Q8, 0:TOK]
                if n in ("D", "D2"):
                    pre = ("n1" if n == "D" else "n2") + ("l" if q == 0 else "s")
                    sc.activation(act_out, src, ACT.Identity, bias=prm(pre + "_b", 96)[:, s:s + 1],
                                  scale=prm(pre + "_g", 96)[:, s:s + 1]).then_inc(*freed(j))
                elif n == "H":
                    sc.activation(xc[0:96, s, QT * q:QT * q + QT].rearrange("p (i k) -> p i k", k=TOK), src,
                                  ACT.Copy).then_inc(*freed(j))
                else:
                    sc.activation(act_out, src, ACT.Copy).then_inc(*freed(j))

            act.wait_ge(zeroed, 9)
            act.wait_ge(loaded["params"], 16)
            for n, kind in ATT:
                for q in range(2):
                    nt_copy(n, q, 0)
                if n == "B":
                    act.wait_ge(*evacuated(("gate", "B")))
                    sc.activation(gsm[0:ROWS, 1], gsm[0:ROWS, 0], ACT.Exp).then_inc(*gate_exp.inc("B"))
                    for q in range(2):
                        j = ("dx", q)
                        act.wait_ge(*filled(j))
                        sc.activation(dX[:, QT * q:QT * q + QT], bank(j)[:, 0:QT], ACT.Copy).then_inc(*freed(j))
                if kind in (SOFTMAX, POLY):
                    for q in range(2):
                        for s in range(2):
                            j = ("q", n, q, s)
                            act.wait_ge(*filled(j))
                            sc.activation(qT[s][:, QT * q:QT * q + QT], bank(j)[0:96, 0:QT], ACT.Copy, scale=SCALE).then_inc(*freed(j))
                if kind == LINEAR:
                    for q in range(2):
                        for s in range(2):
                            act.wait_ge(*filled(("q", n, q, s)))
                            sc.activation(qT[s][:, QT * q:QT * q + QT], bank(("q", n, q, s))[0:96, 0:QT], ACT.Exp).then_inc(*elu_exp.inc(("q", q, s)))
                    for p in range(PAIRS):
                        act.wait_ge(*filled(("kv", p)))
                        sc.activation(x2[0:ROWS, p], bank(("kv", p))[0:ROWS, 0:D], ACT.Exp).then_inc(*elu_exp.inc(("k", p)))
                    for q in range(2):
                        j = ("oT", n, q, 0)
                        act.wait_ge(*filled(j))
                        sc.activation(oT[0][0:96, Q8 * q:Q8 * q + Q8, 0:TOK],
                                      bank(j)[0:96, :].rearrange("p (i k) -> p i k", k=GAP)[:, :, 0:TOK], ACT.Copy).then_inc(*freed(j))
                if kind == SOFTMAX:
                    def exp_pair(p):
                        act.wait_ge(*evacuated(("s", n, p)))
                        a = ar[0:ROWS, p % 4]
                        sc.activation(a, a, ACT.Exp).then_inc(*exp_ready.inc((n, p)))

                    def et_copy(p):
                        if n == "B" and p == 0:
                            act.wait_ge(adrep_ready, 2)
                        j = ("t", n, p)
                        act.wait_ge(*filled(j))
                        sc.activation(et[:, :, 2 * TOK * p:2 * TOK * p + 2 * TOK].rearrange("p g (i k) -> p g i k", k=TOK),
                                      bank(j)[0:GR, :].rearrange("p (g i k) -> p g i k", g=NG, k=GAP)[:, :, :, 0:TOK],
                                      ACT.Copy).then_inc(*freed(j))
                    for p in range(4):
                        exp_pair(p)
                    for p in range(4):
                        et_copy(p)
                    for p in range(4, 8):
                        exp_pair(p)
                    for p in range(4, 8):
                        et_copy(p)
                if kind == COLUMN:
                    for j in range(6):
                        m = ET_JOBS[j][1] * NG * TOK
                        act.wait_ge(*evacuated(("e", n, j)))
                        a = ar[0:GR, j % 4, 0:m]
                        sc.activation(a, a, ACT.Exp).then_inc(*eexp.inc((n, j)))
                if kind == POLY:
                    for j in range(6):
                        m = ET_JOBS[j][1] * NG * TOK
                        act.wait_ge(*filled(("e", n, j)))
                        if j >= 4:
                            act.wait_ge(*et_ready.at((n, j - 4)))
                        sc.activation(ar[0:GR, j % 4, 0:m], bank(("e", n, j))[0:GR, 0:m], ACT.Square, bias=1.0).then_inc(*freed(("e", n, j)))
                if n == "D":
                    for q in range(2):
                        nt_copy("D2", q, 0)
                    for qb, br, m in [(q, br, m) for q, br in MLP for m in range(MT)]:
                        j = ("f1", qb, br, m)
                        act.wait_ge(*filled(j))
                        sc.activation(hid[:, qb + br, m], bank(j)[:, 0:QT], ACT.Gelu, bias=prm("b_fc1")[:, m:m + 1]).then_inc(*freed(j))
            for q in range(2):
                nt_copy("H", q, 0)
            act.wait_ge(*evacuated(("gate", "H")))
            sc.activation(gsm[:, 1, 0:CT * NE], gsm[:, 0, 0:CT * NE], ACT.Exp).then_inc(*gate_exp.inc("H"))

            def gelus(e, i, b):
                at = PARAM_AT["b1"][0]
                src = par[:, bass.ds(at + (i * 2 + b) * MT, MT)] if e is None else par[:, at + e * MT:at + e * MT + MT]
                sc.activation(b1cur[:, b], src, ACT.Copy).then_inc(b1_ready, 1)
                act.wait_ge(b1_ready, i * 2 + (b + 1))
                if e is None:
                    act.wait_ge(fc2_done, i * 6 + (3 * (b + 1) - 6))
                for m in range(MT):
                    for c in range(2):
                        act.wait_ge(fc1_done, i * 24 + (12 * b + 2 * m + c + 1))
                        sc.activation(hbuf[b][:, m, QT * c:QT * c + QT], PS[(2 * m + c) % 4][:, 0:QT], ACT.Gelu,
                                      bias=b1cur[:, b, m:m + 1]).then_inc(gelu_done, 1)
            gelus(0, 0, 0)
            gelus(1, 0, 1)
            with act.Fori(1, NE // 2) as i:
                for b in range(2):
                    gelus(None, i, b)

        @block.vector
        def _(dve):
            v = nc.vector
            links = [0]

            def mark(ins):
                links[0] += 1
                ins.then_inc(dve_chain, 1)

            def settle():
                dve.wait_ge(dve_chain, links[0])

            def link(ins):
                mark(ins)
                settle()

            def moments(key, src, q):
                for p in range(4 * q, 4 * q + 4):
                    mark(v.bn_stats(stats[0:ROWS, p], src[0:ROWS, p]))
                settle()
                for p in range(4 * q, 4 * q + 4):
                    ins = v.bn_aggr(mv[0:ROWS, p], stats[0:ROWS, p])
                    if p < 4 * q + 3:
                        mark(ins)
                ins.then_inc(*var_ready.inc(key))

            def normalise(key, src, dst, q):
                dve.wait_ge(*rstd_ready.at(key))
                for p in range(4 * q, 4 * q + 4):
                    ins = v.tensor_scalar(dst[0:ROWS, p], src[0:ROWS, p], mv[0:ROWS, p, 0:1], rstd[0:ROWS, p:p + 1],
                                          ALU.subtract, ALU.mult)
                    if p == 4 * q + 3 and key[0] != "D":
                        ins.then_inc(*xn_ready.inc(key))
                    else:
                        mark(ins)
                if key[0] == "D":
                    settle()
                    for p in range(4 * q, 4 * q + 4):
                        ins = v.tensor_scalar(x2[0:ROWS, p], dst[0:ROWS, p], rtmp[0:ROWS, 1, p:p + 1], None, ALU.mult)
                        if p == 4 * q + 3:
                            ins.then_inc(*xn_ready.inc(key))
                        else:
                            mark(ins)

            def layernorm(n, src, dst, upd):
                for q in range(2):
                    dve.wait_ge(*updated(upd, 2 * q + 1))
                    moments((n, q), src, q)
                for q in range(2):
                    normalise((n, q), src, dst, q)

            def nt_copy(n, q):
                j = ("nT", n, q, 1)
                dve.wait_ge(*filled(j))
                src = bank(j)[0:96, :].rearrange("p (i k) -> p i k", k=GAP)[:, :, 0:TOK]
                dst = nT[1][0:96, Q8 * q:Q8 * q + Q8, 0:TOK]
                if n in ("D", "D2"):
                    pre = ("n1" if n == "D" else "n2") + ("l" if q == 0 else "s")
                    v.tensor_scalar(dst, src, prm(pre + "_g", 96)[:, 1:2], prm(pre + "_b", 96)[:, 1:2],
                                    ALU.mult, ALU.add).then_inc(*freed(j))
                elif n == "H":
                    v.tensor_copy(xc[0:96, 1, QT * q:QT * q + QT].rearrange("p (i k) -> p i k", k=TOK), src).then_inc(*freed(j))
                else:
                    v.tensor_copy(dst, src).then_inc(*freed(j))

            def key_blocks(n, q, s):
                j = ("k", n, q, s)
                dve.wait_ge(*filled(j))
                mask = maskg[:, s] if n == "C" else con("mask_k", 96)
                src = bank(j)[0:96, :].rearrange("p (i k) -> p i k", k=GAP)[:, :, 0:TOK] if n == "C" \
                    else bank(j)[0:96, 0:QT].rearrange("p (i k) -> p i k", k=TOK)
                v.tensor_tensor(kblk[s][:, Q8 * q:Q8 * q + Q8], src.unsqueeze(2).broadcast_to([96, Q8, HH, TOK]),
                                mask.unsqueeze(1).unsqueeze(3).broadcast_to([96, Q8, HH, TOK]), ALU.mult).then_inc(*freed(j))

            def value_blocks(n, p):
                j = ("v", n, p)
                dve.wait_ge(*filled(j))
                vi = vblk[:, 2 * p:2 * p + 2].rearrange("p i g c -> p (i g c)")
                dst = vi.rearrange("p (a c) -> p a c", c=2 * HALF)
                m = con("mask_v", GR).rearrange("p (a c) -> p a c", a=2)
                for gg in range(2):
                    src = bank(j)[0:GR, 0:2 * D].rearrange("p (a c) -> p a c", c=HALF)[:, :, 48 * gg:48 * gg + 48]
                    ins = v.tensor_tensor(dst[:, :, 144 * gg:144 * gg + 48], src,
                                          m[:, 0:1, 48 * gg:48 * gg + 48].broadcast_to([GR, 4, 48]), ALU.mult)
                    if gg == 0:
                        mark(ins)
                ins.then_inc(*freed(j))

            def score_pair(n, p):
                j = ("s", n, p)
                dve.wait_ge(*filled(j))
                sc = bank(j)[0:ROWS, 0:H * TOK].rearrange("p (h k) -> p h k", k=TOK)
                link(v.tensor_reduce(mx[0:ROWS, p], sc, AX.X, ALU.max))
                if p >= 4:
                    dve.wait_ge(*filled(("t", n, p - 4)))
                v.tensor_tensor(ar[0:ROWS, p % 4].rearrange("p (h k) -> p h k", k=TOK), sc,
                                mx[0:ROWS, p].unsqueeze(2).broadcast_to([ROWS, H, TOK]), ALU.subtract).then_inc(*freed(j))

            def attend_out(n, q, s, den):
                o = bank(("o", n, q, s))[0:96, 0:QT].rearrange("p (i k) -> p i k", k=TOK)
                dst = oT[s][0:96, Q8 * q:Q8 * q + Q8, 0:TOK]
                if den:
                    j = ("d", n, q, s)
                    dve.wait_ge(*filled(j))
                    v.reciprocal(rd[:, s], bank(j)[0:96, 0:QT]).then_inc(*freed(j))
                    dve.wait_ge(*evacuated(j))
                    dve.wait_ge(*filled(("o", n, q, s)))
                    v.tensor_tensor(dst, o, rd[:, s].rearrange("p (i k) -> p i k", k=TOK), ALU.mult).then_inc(*freed(("o", n, q, s)))
                else:
                    dve.wait_ge(*filled(("o", n, q, s)))
                    v.tensor_copy(dst, o).then_inc(*freed(("o", n, q, s)))

            def add_bank(j, dst, other, event, plus=None):
                dve.wait_ge(*filled(j))
                if plus is not None:
                    dve.wait_ge(*plus)
                c = j[-1]
                src = bank(j)[0:ROWS, 0:2 * D].rearrange("p (c d) -> p c d", d=D)
                v.tensor_tensor(dst[0:ROWS, 2 * c:2 * c + 2], src, other[0:ROWS, 2 * c:2 * c + 2], ALU.add).then_inc(*freed(j))

            def gating(n, j, rows, tiles):
                m, m2 = tiles * NE, tiles * NE * NE
                dve.wait_ge(*filled(j))
                lg = bank(j)[0:rows, 0:m].rearrange("p (c e) -> p c e", e=NE)
                top = mx[0:rows, 0, 0:tiles]
                link(v.tensor_reduce(top, lg, AX.X, ALU.max))
                sub = gsm[0:rows, 0, 0:m].rearrange("p (c e) -> p c e", e=NE)
                v.tensor_tensor(sub, lg, top.unsqueeze(2).broadcast_to([rows, tiles, NE]), ALU.subtract).then_inc(*freed(j))
                dve.wait_ge(*evacuated(j))
                dve.wait_ge(*gate_exp.at(n))
                e = gsm[0:rows, 1, 0:m].rearrange("p (c e) -> p c e", e=NE)
                tot = mx[0:rows, 1, 0:tiles]
                link(v.tensor_reduce(tot, e, AX.X, ALU.add))
                link(v.reciprocal(mx[0:rows, 2, 0:tiles], tot))
                gate = gsm[0:rows, 0, 0:m].rearrange("p (c e) -> p c e", e=NE)
                link(v.tensor_tensor(gate, e, mx[0:rows, 2, 0:tiles].unsqueeze(2).broadcast_to([rows, tiles, NE]), ALU.mult))
                gj = gate.unsqueeze(2).broadcast_to([rows, tiles, NE, NE])
                gi = gate.unsqueeze(3).broadcast_to([rows, tiles, NE, NE])
                above = gts[0:rows, 0, 0:m2].rearrange("p (c i j) -> p c i j", i=NE, j=NE)
                equal = gts[0:rows, 1, 0:m2].rearrange("p (c i j) -> p c i j", i=NE, j=NE)
                mark(v.tensor_tensor(above, gj, gi, ALU.is_gt))
                link(v.tensor_tensor(equal, gj, gi, ALU.is_equal))
                tri = con("tri", rows).rearrange("p (i j) -> p i j", j=NE).unsqueeze(1).broadcast_to([rows, tiles, NE, NE])
                link(v.tensor_tensor(equal, equal, tri, ALU.mult))
                link(v.tensor_tensor(above, above, equal, ALU.add))
                rank = gsm[0:rows, 2, 0:m]
                link(v.tensor_reduce(rank, above.rearrange("p c i j -> p (c i) j"), AX.X, ALU.add))
                keep = gsm[0:rows, 3, 0:m]
                link(v.tensor_scalar(keep, rank, TOPK - 0.5, None, ALU.is_lt))
                v.tensor_tensor(disp[0:rows, 0:tiles].rearrange("p c e -> p (c e)"), keep, gsm[0:rows, 0, 0:m], ALU.mult).then_inc(*disp_ready.inc(n))

            for s in range(2):
                for t in (nT[s], oT[s]):
                    v.memset(t[0:96], 0.0).then_inc(zeroed, 1)
                    v.memset(t[96:97], 1.0).then_inc(zeroed, 1)
            v.memset(nrep[1][96:97], 1.0).then_inc(zeroed, 1)
            dve.wait_ge(loaded["params"], 16)
            pos = prm("pos", ROWS)
            for i in range(2):
                mark(v.tensor_tensor(pos[GAP * i:GAP * i + 1], pos[GAP * i:GAP * i + 1],
                                     prm("cls")[GAP * i:GAP * i + 1], ALU.add))
            settle()
            for c in range(4):
                j = ("tok", c)
                dve.wait_ge(*filled(j))
                src = bank(j)[0:ROWS, 0:2 * D].rearrange("p (c d) -> p c d", d=D)
                v.tensor_tensor(h[0:ROWS, 2 * c:2 * c + 2], src, pos.unsqueeze(1).broadcast_to([ROWS, 2, D]), ALU.add).then_inc(*freed(j))
            dve.wait_ge(zeroed, 9)
            dve.wait_ge(loaded["consts"], 16)
            link(v.tensor_tensor(maskg[:], con("mask_k", 96).unsqueeze(1).broadcast_to([96, 2, HH]),
                                 prm("gk", 96).unsqueeze(2).broadcast_to([96, 2, HH]), ALU.mult))

            layernorm("A", h, xn, "tok")
            for q in range(2):
                nt_copy("A", q)
            for q in range(2):
                for s in range(2):
                    j = ("q", "A", q, s)
                    a = qT[s][:, QT * q:QT * q + QT]
                    dve.wait_ge(*elu_exp.at(("q", q, s)))
                    link(v.tensor_scalar(a, a, 1.0, None, ALU.min))
                    v.scalar_tensor_tensor(a, bank(j)[0:96, 0:QT], 0.0, a, ALU.max, ALU.add).then_inc(*freed(j))
            vtok = arf[0:ROWS, 0:PAIRS * H * (HD + 1)].rearrange("p (c h e) -> p c h e", h=H, e=HD + 1)
            ktok = x2
            link(v.memset(vtok[:, :, :, HD:HD + 1], 1.0))
            for p in range(PAIRS):
                j = ("kv", p)
                dve.wait_ge(*elu_exp.at(("k", p)))
                mark(v.tensor_copy(vtok[:, p, :, 0:HD], bank(j)[0:ROWS, D:2 * D].rearrange("p (h e) -> p h e", e=HD)))
                link(v.tensor_scalar(ktok[0:ROWS, p], ktok[0:ROWS, p], 1.0, None, ALU.min))
                v.scalar_tensor_tensor(ktok[0:ROWS, p], bank(j)[0:ROWS, 0:D], 0.0, ktok[0:ROWS, p], ALU.max, ALU.add).then_inc(*freed(j))
            kvs = big[0:96, 0:B * 2 * HH * (HD + 1)].rearrange("p (c a x) -> p c a x", a=2, x=2 * HH * (HD + 1))
            for c in range(4):
                for pr in range(2):
                    j = ("kvm", c, pr)
                    dve.wait_ge(*filled(j))
                    kw = HH * (HD + 1)
                    v.tensor_tensor(kvs[:, 2 * c:2 * c + 2, pr].rearrange("p c (s x) -> p c s x", x=kw),
                                    bank(j)[0:96, 0:4 * kw].rearrange("p (c s x) -> p c s x", s=2, x=kw),
                                    con("mask_kv", 96).unsqueeze(1).unsqueeze(1).broadcast_to([96, 2, 2, kw]), ALU.mult).then_inc(*freed(j))
            for c in range(4):
                j = ("lo", c)
                dve.wait_ge(*filled(j))
                src = bank(j)[0:ROWS, 0:2 * H * (HD + 1)].rearrange("p (c e) -> p c e", e=HD + 1)
                link(v.reciprocal(rs[0:ROWS, c], src[:, :, HD]))
                v.tensor_tensor(yt[0:ROWS, 2 * c:2 * c + 2].rearrange("p c (h e) -> p (c h) e", e=HD), src[:, :, 0:HD],
                                rs[0:ROWS, c].unsqueeze(2).broadcast_to([ROWS, 2 * H, HD]), ALU.mult).then_inc(*freed(j))
            for q in range(2):
                j = ("oT", "A", q, 1)
                dve.wait_ge(*filled(j))
                v.tensor_copy(oT[1][0:96, Q8 * q:Q8 * q + Q8, 0:TOK],
                              bank(j)[0:96, :].rearrange("p (i k) -> p i k", k=GAP)[:, :, 0:TOK]).then_inc(*freed(j))
            for c in range(4):
                add_bank(("p", "A", c), h, h, ("A", c))

            def softmax_attention(n):
                for q in range(2):
                    for s in range(2):
                        key_blocks(n, q, s)
                for p in range(4):
                    score_pair(n, p)
                for p in range(4):
                    value_blocks(n, p)
                for p in range(4, 8):
                    score_pair(n, p)
                for p in range(4, 8):
                    value_blocks(n, p)
                for q in range(2):
                    for s in range(2):
                        attend_out(n, q, s, True)

            layernorm("B", h, xn, "A")
            for q in range(2):
                nt_copy("B", q)
            gating("B", ("gate", "B"), ROWS, PAIRS)
            for q in range(2):
                j = ("dT", q)
                dve.wait_ge(*filled(j))
                v.tensor_copy(dispT[:, QT * q:QT * q + QT].rearrange("p (i k) -> p i k", k=TOK),
                              bank(j)[0:NE, :].rearrange("p (i k) -> p i k", k=GAP)[:, :, 0:TOK]).then_inc(*freed(j))
            for q in range(2):
                j = ("a", q)
                dve.wait_ge(*filled(j))
                dve.wait_ge(*evacuated(("dx", q)))
                v.tensor_tensor(ad[:, QT * q:QT * q + QT], bank(j)[:, 0:QT], dX[:, QT * q:QT * q + QT], ALU.mult).then_inc(*freed(j))
            softmax_attention("B")
            for c in range(4):
                add_bank(("p", "B", c), h, h, ("B", c))

            layernorm("C", h, xn, "B")
            for q in range(2):
                nt_copy("C", q)
            for p in range(PAIRS):
                j = ("qk", p)
                dve.wait_ge(*filled(j))
                for a in range(2):
                    mark(v.bn_stats(stats[0:ROWS, 2 * p + a], bank(j)[0:ROWS, D * a:D * a + D]))
                settle()
                mark(v.bn_aggr(mv[0:ROWS, 2 * p], stats[0:ROWS, 2 * p]))
                v.bn_aggr(mv[0:ROWS, 2 * p + 1], stats[0:ROWS, 2 * p + 1]).then_inc(*var_ready.inc(("Cqk", p)))
            qn = [x2, yt]
            for p in range(PAIRS):
                j = ("qk", p)
                dve.wait_ge(*rstd_ready.at(("Cqk", p)))
                for a in range(2):
                    ins = v.tensor_scalar(qn[a][0:ROWS, p], bank(j)[0:ROWS, D * a:D * a + D], mv[0:ROWS, 2 * p + a, 0:1],
                                          rstd[0:ROWS, 2 * p + a:2 * p + a + 1], ALU.subtract, ALU.mult)
                    if a == 0:
                        mark(ins)
                ins.then_inc(*freed(j))
            for q in range(2):
                for s in range(2):
                    j = ("q", "C", q, s)
                    dve.wait_ge(*filled(j))
                    v.tensor_scalar(qT[s][:, QT * q:QT * q + QT].rearrange("p (i k) -> p i k", k=TOK),
                                    bank(j)[0:96, :].rearrange("p (i k) -> p i k", k=GAP)[:, :, 0:TOK],
                                    prm("gq", 96)[:, s:s + 1], SCALE, ALU.mult, ALU.mult).then_inc(*freed(j))
                    key_blocks("C", q, s)

            def column_softmax(j):
                first, m = ET_JOBS[j]
                jb = ("e", "C", j)
                n = m * NG
                dve.wait_ge(*filled(jb))
                sc = bank(jb)[0:GR, 0:n * TOK].rearrange("p (a k) -> p a k", k=TOK)
                link(v.tensor_reduce(mx[0:GR, j, 0:n], sc, AX.X, ALU.max))
                v.tensor_tensor(ar[0:GR, j % 4][:, 0:n * TOK].rearrange("p (a k) -> p a k", k=TOK), sc,
                                mx[0:GR, j, 0:n].unsqueeze(2).broadcast_to([GR, n, TOK]), ALU.subtract).then_inc(*freed(jb))

            def column_norm(j):
                first, m = ET_JOBS[j]
                n = m * NG
                dve.wait_ge(*eexp.at(("C", j)))
                e = ar[0:GR, j % 4][:, 0:n * TOK].rearrange("p (a k) -> p a k", k=TOK)
                link(v.tensor_reduce(rs[0:GR, 0, 0:n], e, AX.X, ALU.add))
                link(v.reciprocal(rs[0:GR, 1, 0:n], rs[0:GR, 0, 0:n]))
                v.tensor_tensor(et[:, :, TOK * first:TOK * (first + m)].rearrange("p g (i k) -> p i g k", k=TOK),
                                e.rearrange("p (i g) k -> p i g k", g=NG),
                                rs[0:GR, 1, 0:n].rearrange("p (i g) -> p i g", g=NG).unsqueeze(3).broadcast_to([GR, m, NG, TOK]),
                                ALU.mult).then_inc(*et_ready.inc(("C", j)))

            for j in range(3):
                column_softmax(j)
            for p in range(4):
                value_blocks("C", p)
            for j in range(3):
                column_norm(j)
            for j in range(3, 6):
                column_softmax(j)
            for p in range(4, 8):
                value_blocks("C", p)
            for j in range(3, 6):
                column_norm(j)
            for q in range(2):
                for s in range(2):
                    attend_out("C", q, s, False)
            for c in range(4):
                add_bank(("p", "C", c), h, h, ("C", c), h_plus.at(("C", c // 2)))

            layernorm("D", h, xn, "C")
            for q in range(2):
                nt_copy("D", q)
            softmax_attention("D")
            for c in range(4):
                add_bank(("p", "D", c), yt, xn, ("Dy", c))
            layernorm("D2", yt, x2, "Dy")
            for q in range(2):
                nt_copy("D2", q)
            for q in range(2):
                for s in range(2):
                    j = ("f2", q, s)
                    dve.wait_ge(*filled(j))
                    if q == 1 and s == 0:
                        dve.wait_ge(mixed, 3)
                    bias = prm("b_fc2", 96)[:, s:s + 1] if q == 0 else b2s[:, s:s + 1]
                    v.tensor_scalar(oT[s][0:96, Q8 * q:Q8 * q + Q8, 0:TOK], bank(j)[0:96, 0:QT].rearrange("p (i k) -> p i k", k=TOK),
                                    bias, None, ALU.add).then_inc(*freed(j))
            for c in range(4):
                add_bank(("back", "M", c), h, h, ("D", c), h_plus.at(("D", c // 2)))

            layernorm("E", h, xn, "D")
            for q in range(2):
                nt_copy("E", q)
            for q in range(2):
                for s in range(2):
                    key_blocks("E", q, s)

            def poly(j):
                first, m = ET_JOBS[j]
                dve.wait_ge(*evacuated(("e", "E", j)))
                v.tensor_scalar(et[:, :, TOK * first:TOK * (first + m)].rearrange("p g (i k) -> p i g k", k=TOK),
                                ar[0:GR, j % 4][:, 0:m * NG * TOK].rearrange("p (i g k) -> p i g k", g=NG, k=TOK),
                                1.0, 0.0, ALU.add, ALU.max).then_inc(*et_ready.inc(("E", j)))
            for j in range(3):
                poly(j)
            for p in range(4):
                value_blocks("E", p)
            for j in range(3, 6):
                poly(j)
            for p in range(4, 8):
                value_blocks("E", p)
            for q in range(2):
                for s in range(2):
                    attend_out("E", q, s, True)
            for c in range(4):
                add_bank(("p", "E", c), h, h, ("E", c))

            layernorm("F", h, xn, "E")
            qf = [big[0:96, a * QT:(a + 1) * QT] for a in range(2)]
            for q in range(2):
                for s in range(2):
                    j = ("nT", "F", q, s)
                    dve.wait_ge(*filled(j))
                    src = bank(j)[0:96, :].rearrange("p (i k) -> p i k", k=GAP)[:, :, 0:TOK]
                    t3 = qf[0].rearrange("p (i k) -> p i k", k=TOK)
                    v.tensor_scalar(t3, src, 1.0 / ACT_SCALE, 127.0, ALU.mult, ALU.min).then_inc(*freed(j))
                    dve.wait_ge(*evacuated(j))
                    link(v.tensor_scalar(qf[1], qf[0], -128.0, ROUND, ALU.max, ALU.add))
                    v.tensor_scalar(nq[:, s, Q8 * q:Q8 * q + Q8, 0:TOK], qf[1].rearrange("p (i k) -> p i k", k=TOK),
                                    ROUND, None, ALU.subtract).then_inc(*nq_ready.inc((q, s)))
            for c in range(4):
                j = ("int", c)
                dve.wait_ge(*filled(j))
                dve.wait_ge(*h_plus.at(("F", c // 2)))
                src = bank(j)[0:ROWS, 0:2 * D].rearrange("p (c d) -> p c d", d=D)
                v.scalar_tensor_tensor(h[0:ROWS, 2 * c:2 * c + 2], src, EFF_SCALE, h[0:ROWS, 2 * c:2 * c + 2],
                                       ALU.mult, ALU.add).then_inc(*freed(j))

            layernorm("G", h, xn, "F")
            for q in range(2):
                nt_copy("G", q)
            softmax_attention("G")
            for c in range(4):
                add_bank(("back", "G", c), yt, xn, ("Gy", c))
            layernorm("G2", yt, x2, "Gy")
            for c in range(4):
                dve.wait_ge(*xn_ready.at(("G2", 1)))
                a = x2[0:ROWS, 2 * c:2 * c + 2]
                link(v.tensor_tensor(a, a, prm("gamma", ROWS).unsqueeze(1).broadcast_to([ROWS, 2, D]), ALU.mult))
                link(v.tensor_tensor(a, a, prm("beta", ROWS).unsqueeze(1).broadcast_to([ROWS, 2, D]), ALU.add))
                v.tensor_tensor(h[0:ROWS, 2 * c:2 * c + 2], h[0:ROWS, 2 * c:2 * c + 2], a, ALU.add).then_inc(*g_done.inc(c))

            layernorm("H", h, xn, "G")
            link(v.memset(xc[0:96, :, T:TPAD], 0.0))
            link(v.memset(xc[96:97], 1.0))
            for q in range(2):
                nt_copy("H", q)
            gating("H", ("gate", "H"), 128, CT)
            eT = dX[0:NE, 0:T]
            for a in range(2):
                j = ("eT", a)
                dve.wait_ge(*filled(j))
                n = 512 if a == 0 else T - 512
                v.tensor_copy(eT[:, 512 * a:512 * a + n], bank(j)[0:NE, 0:n]).then_inc(*freed(j))
            dve.wait_ge(h_back, 32)

            def tiles(c):
                return (128, slice(2 * c, 2 * c + 2)) if c < 2 else (crow[-1], slice(CT - 1, CT))
            for c in range(3):
                j = ("eb", c)
                r, sl = tiles(c)
                dve.wait_ge(*filled(j))
                n = sl.stop - sl.start
                v.tensor_tensor(acc[0:r, sl], bank(j)[0:r, 0:n * D].rearrange("p (c d) -> p c d", d=D), hc[0:r, sl], ALU.add).then_inc(*freed(j))
                dve.wait_ge(*evacuated(j))

            def add_expert(i, b):
                for c in range(3):
                    r, sl = tiles(c)
                    dve.wait_ge(fc2_done, i * 6 + (3 * b + c + 1))
                    for t in range(sl.start, sl.stop):
                        at = i * 2 + (b + t * NE)
                        gate = disp[:].rearrange("p c e -> p (c e)")[0:r, bass.ds(at, 1)]
                        ins = v.scalar_tensor_tensor(acc[0:r, t], PS[4 + c][0:r, (t - sl.start) * D:(t - sl.start + 1) * D],
                                                     gate, acc[0:r, t], ALU.mult, ALU.add)
                    ins.then_inc(acc_done, 1)
            with dve.Fori(0, NE // 2) as i:
                for b in range(2):
                    if b == 1:
                        dve.wait_ge(acc_done, i * 6 + 3)
                    add_expert(i, b)
                dve.wait_ge(acc_done, i * 6 + 6)

        @block.tensor
        def _(pe):
            mm = nc.tensor.matmul
            done = [0]

            def start_job(j):
                assert order[done[0]] == j, (order[done[0]], j)
                done[0] += 1
                b, k = where[j]
                if k:
                    pe.wait_ge(bank_read[b], k)
                return PS[b]

            def end_job(j, last):
                last.then_inc(bank_filled[where[j][0]], 1)

            def transposes(n, src, key, name="nT"):
                for q in range(2):
                    if key is not None:
                        pe.wait_ge(*xn_ready.at((key, q)))
                    for s in range(2):
                        j = (name, n, q, s)
                        ps = start_job(j)
                        for p in range(4):
                            last = nc.tensor.transpose(ps[0:96, 128 * p:128 * p + ROWS], src[0:ROWS, 4 * q + p, 96 * s:96 * s + 96], ident[0:ROWS, 0:ROWS])
                        end_job(j, last)

            def nt(k, q):
                return nT[k][0:96 + k, Q8 * q:Q8 * q + Q8, 0:TOK]

            def feature_job(j, seg, col, q, s, lora=False):
                ps = start_job(j)
                o = ps[0:96, 0:QT]
                for k in range(2):
                    last = mm(o, w(seg, k, col + 96 * s, 96), nt(k, q), start=(k == 0), stop=(k == 1 and not lora))
                if lora:
                    last = mm(o, bup[:, col + 96 * s:col + 96 * s + 96], ad[:, QT * q:QT * q + QT], start=False, stop=True)
                end_job(j, last)

            def value_job(n, p):
                j = ("v", n, p)
                pe.wait_ge(*rep_ready.at((n, p // 4)))
                if n == "B":
                    pe.wait_ge(adrep_ready, p // 4 + 1)
                ps = start_job(j)
                for i in range(2):
                    o = ps[0:GR, D * i:D * i + D]
                    for k in range(2):
                        last = mm(o, nrep[k][0:96 + k, 2 * p + i], w(n + "_qkv", k, 2 * D, D), start=(k == 0), stop=(k == 1 and n != "B"))
                    if n == "B":
                        last = mm(o, adrep[:, 2 * p + i], bup[:, 2 * D:3 * D], start=False, stop=True)
                end_job(j, last)

            def output_jobs(n, q, den):
                for s in range(2):
                    if den:
                        j = ("d", n, q, s)
                        ps = start_job(j)
                        for gg in range(2):
                            last = mm(ps[0:96, 0:QT], con("ones_g", GR)[:, HALF * gg:HALF * gg + HALF],
                                      et[:, 2 * s + gg, QT * q:QT * q + QT], start=(gg == 0), stop=(gg == 1))
                        end_job(j, last)
                    j = ("o", n, q, s)
                    ps = start_job(j)
                    for i in range(Q8):
                        for gg in range(2):
                            g, im = 2 * s + gg, Q8 * q + i
                            last = mm(ps[0:96, TOK * i:TOK * i + TOK], vblk[:, im, g], et[:, g, TOK * im:TOK * im + TOK],
                                      start=(gg == 0), stop=(gg == 1))
                    end_job(j, last)

            def proj_jobs(n):
                for c in range(4):
                    j = ("p", n, c)
                    ps = start_job(j)
                    for i in range(2):
                        p = 2 * c + i
                        for k in range(2):
                            wp = wps[0:96 + k, k] if n == "D" and c >= 2 else w(n + "_proj", k)
                            last = mm(ps[0:ROWS, D * i:D * i + D], oT[k][0:96 + k].rearrange("p i k -> p (i k)")[:, 128 * p:128 * p + ROWS],
                                      wp, start=(k == 0), stop=(k == 1))
                    end_job(j, last)

            def back_jobs(n):
                for c in range(4):
                    j = ("back", n, c)
                    ps = start_job(j)
                    for i in range(2):
                        for s in range(2):
                            last = nc.tensor.transpose(ps[0:ROWS, D * i + 96 * s:D * i + 96 * s + 96],
                                                       oT[s][0:96].rearrange("p i k -> p (i k)")[:, 128 * (2 * c + i):128 * (2 * c + i) + ROWS],
                                                       ident[0:96, 0:96])
                    end_job(j, last)

            def wait_evacuated(*jobs):
                for j in jobs:
                    pe.wait_ge(*evacuated(j))

            pe.wait_ge(loaded["tokw"], 16)
            for c in range(4):
                if c % 2 == 0:
                    pe.wait_ge(loaded[f"patch{c // 2}"], 16)
                ps = start_job(("tok", c))
                for i in range(2):
                    for k in range(PATCH_K):
                        last = mm(ps[0:ROWS, D * i:D * i + D], patch[:, 2 * c + i, k], tokw[:, k], start=(k == 0), stop=(k == PATCH_K - 1))
                end_job(("tok", c), last)
            pe.wait_ge(loaded["consts"], 16)

            for n, kind in ATT:
                transposes(n, x2 if n == "D" else xn, n)
                pe.wait_ge(loaded["E_qkv" if n == "G" else n + "_qkv"], 16)
                wait_evacuated(*nt_jobs(n))
                if n == "B":
                    ps = start_job(("gate", "B"))
                    for p in range(PAIRS):
                        for k in range(2):
                            last = mm(ps[0:ROWS, NE * p:NE * p + NE], nT[k][0:96 + k].rearrange("p i k -> p (i k)")[:, 128 * p:128 * p + ROWS],
                                      w("B_gate", k), start=(k == 0), stop=(k == 1))
                    end_job(("gate", "B"), last)
                    pe.wait_ge(*disp_ready.at("B"))
                    for q in range(2):
                        ps = start_job(("dT", q))
                        for p in range(4):
                            last = nc.tensor.transpose(ps[0:NE, 128 * p:128 * p + ROWS], disp[0:ROWS, 4 * q + p], ident[0:ROWS, 0:ROWS])
                        end_job(("dT", q), last)
                    pe.wait_ge(loaded["bup"], 16)
                    for q in range(2):
                        wait_evacuated(("dT", q))
                        ps = start_job(("dx", q))
                        end_job(("dx", q), mm(ps[:, 0:QT], con("expand", NE), dispT[:, QT * q:QT * q + QT], start=True, stop=True))
                        ps = start_job(("a", q))
                        for k in range(2):
                            last = mm(ps[:, 0:QT], w("B_down", k), nt(k, q), start=(k == 0), stop=(k == 1))
                        end_job(("a", q), last)
                    wait_evacuated(("a", 0), ("a", 1))
                if kind == COLUMN:
                    for p in range(PAIRS):
                        ps = start_job(("qk", p))
                        for k in range(2):
                            last = mm(ps[0:ROWS, 0:2 * D], nT[k][0:96 + k].rearrange("p i k -> p (i k)")[:, 128 * p:128 * p + ROWS],
                                      w("C_qkv", k, 0, 2 * D), start=(k == 0), stop=(k == 1))
                        end_job(("qk", p), last)
                    for q in range(2):
                        wait_evacuated(*[("qk", p) for p in range(4 * q, 4 * q + 4)])
                        for s in range(2):
                            for a, name in enumerate("qk"):
                                j = (name, "C", q, s)
                                ps = start_job(j)
                                for p in range(4):
                                    last = nc.tensor.transpose(ps[0:96, 128 * p:128 * p + ROWS], [x2, yt][a][0:ROWS, 4 * q + p, 96 * s:96 * s + 96], ident[0:ROWS, 0:ROWS])
                                end_job(j, last)
                elif kind == LINEAR:
                    for q in range(2):
                        for s in range(2):
                            feature_job(("q", n, q, s), "A_qkv", 0, q, s)
                    for p in range(PAIRS):
                        ps = start_job(("kv", p))
                        for k in range(2):
                            last = mm(ps[0:ROWS, 0:2 * D], nT[k][0:96 + k].rearrange("p i k -> p (i k)")[:, 128 * p:128 * p + ROWS],
                                      w("A_qkv", k, D, 2 * D), start=(k == 0), stop=(k == 1))
                        end_job(("kv", p), last)
                    vtok = arf[0:ROWS, 0:PAIRS * H * (HD + 1)].rearrange("p (c x) -> p c x", c=PAIRS)
                    kw = HH * (HD + 1)
                    for c in range(4):
                        wait_evacuated(("kv", 2 * c), ("kv", 2 * c + 1))
                        for pr in range(2):
                            j = ("kvm", c, pr)
                            ps = start_job(j)
                            r = slice(GAP * pr, GAP * pr + TOK)
                            for i in range(2):
                                for s in range(2):
                                    last = mm(ps[0:96, kw * (2 * i + s):kw * (2 * i + s) + kw], x2[r, 2 * c + i, 96 * s:96 * s + 96],
                                              vtok[r, 2 * c + i, kw * s:kw * s + kw], start=True, stop=True)
                            end_job(j, last)
                    wait_evacuated(*[("q", n, q, s) for q in range(2) for s in range(2)])
                    kvs = big[0:96, 0:B * 2 * kw].rearrange("p (c a x) -> p c a x", a=2, x=2 * kw)
                    for c in range(4):
                        wait_evacuated(("kvm", c, 0), ("kvm", c, 1))
                        j = ("lo", c)
                        ps = start_job(j)
                        for i in range(2):
                            for pr in range(2):
                                im = 2 * (2 * c + i) + pr
                                m = GAP if pr == 0 else TOK
                                for s in range(2):
                                    last = mm(ps[GAP * pr:GAP * pr + m, kw * (2 * i + s):kw * (2 * i + s) + kw],
                                              qT[s][:, TOK * im:TOK * im + m], kvs[:, 2 * c + i, pr, kw * s:kw * s + kw], start=True, stop=True)
                        end_job(j, last)
                    wait_evacuated(*[("lo", c) for c in range(4)])
                    transposes(n, yt, None, "oT")
                    wait_evacuated(*[("oT", n, q, s) for q in range(2) for s in range(2)])
                else:
                    for q in range(2):
                        for s in range(2):
                            for a, name in enumerate("qk"):
                                feature_job((name, n, q, s), n + "_qkv", D * a, q, s, lora=(n == "B"))
                if kind == SOFTMAX:
                    def score_job(p):
                        j = ("s", n, p)
                        wait_evacuated(*[(a, n, p // 4, s) for s in range(2) for a in "qk"])
                        ps = start_job(j)
                        for i in range(2):
                            im = 2 * p + i
                            m = GAP if i == 0 else TOK
                            for s in range(2):
                                last = mm(ps[GAP * i:GAP * i + m, HH * TOK * s:HH * TOK * s + HH * TOK], qT[s][:, TOK * im:TOK * im + m],
                                          kblk[s][:, im].rearrange("p h k -> p (h k)"), start=True, stop=True)
                        end_job(j, last)

                    def transpose_job(p):
                        j = ("t", n, p)
                        pe.wait_ge(*exp_ready.at((n, p)))
                        ps = start_job(j)
                        for g in range(NG):
                            last = nc.tensor.transpose(ps[0:GR, 128 * g:128 * g + ROWS], ar[0:ROWS, p % 4, GR * g:GR * g + GR], ident[0:ROWS, 0:ROWS])
                        end_job(j, last)
                    for p in range(4):
                        score_job(p)
                    for p in range(4):
                        value_job(n, p)
                    for q in range(2):
                        for p in range(4):
                            transpose_job(4 * q + p)
                        if q == 0:
                            for p in range(4, 8):
                                score_job(p)
                            for p in range(4, 8):
                                value_job(n, p)
                        wait_evacuated(*[("t", n, 4 * q + p) for p in range(4)], *[("v", n, 4 * q + p) for p in range(4)])
                        output_jobs(n, q, True)
                if kind in (COLUMN, POLY):
                    def direct_job(j):
                        first, m = ET_JOBS[j]
                        jb = ("e", n, j)
                        for q in sorted({im // Q8 for im in range(first, first + m)}):
                            wait_evacuated(*[(a, n, q, s) for s in range(2) for a in "qk"])
                        ps = start_job(jb)
                        for i in range(m):
                            im = first + i
                            for g in range(NG):
                                c = (NG * i + g) * TOK
                                s = g // 2
                                last = mm(ps[0:GR, c:c + TOK], kblk[s][:, im, HG * (g % 2):HG * (g % 2) + HG].rearrange("p h k -> p (h k)"), qT[s][:, TOK * im:TOK * im + TOK], start=True, stop=True)
                        end_job(jb, last)
                    for j in range(3):
                        direct_job(j)
                    for p in range(4):
                        value_job(n, p)
                    for j in range(3, 6):
                        direct_job(j)
                    for p in range(4, 8):
                        value_job(n, p)
                    for q in range(2):
                        wait_evacuated(*[("v", n, 4 * q + p) for p in range(4)])
                        pe.wait_ge(*et_ready.at((n, 2 if q == 0 else 5)))
                        output_jobs(n, q, kind == POLY)
                if kind != LINEAR:
                    wait_evacuated(*[("o", n, q, s) for q in range(2) for s in range(2)])
                if n == "D":
                    pe.wait_ge(mixed, 3)
                if n in HAS_PROJ:
                    proj_jobs(n)
                else:
                    back_jobs(n)
                if n == "D":
                    transposes("D2", x2, "D2")
                    wait_evacuated(*nt_jobs("D2"))

                    def fc1_jobs(q, br):
                        for m in range(MT):
                            j = ("f1", q, br, m)
                            ps = start_job(j)
                            for k in range(2 if br == 0 else 1):
                                r = min(96, KEEP[br])
                                at, width = SEG_AT["D_fc1"]
                                last = mm(ps[:, 0:QT], wt[0:r, at + k * width + 128 * m:at + k * width + 128 * m + 128],
                                          nT[k][0:r, Q8 * q:Q8 * q + Q8, 0:TOK], start=(k == 0), stop=(k == 1 or br > 0))
                            end_job(j, last)

                    def fc2_jobs(q):
                        for s in range(2):
                            j = ("f2", q, s)
                            ps = start_job(j)
                            steps = []
                            for br in range(3 if q else 1):
                                n_c = min(96, KEEP[br] - 96 * s)
                                if n_c > 0:
                                    wsrc = fc2s[br] if q else fc2w
                                    steps += [(ps[0:n_c, 0:QT], wsrc[:, m, 96 * s:96 * s + n_c], hid[:, q + br, m]) for m in range(MT)]
                            steps = steps[0:MT - 1] + steps[MT:] + steps[MT - 1:MT]
                            for x, (o, a, b) in enumerate(steps):
                                last = mm(o, a, b, start=(x == 0), stop=(x == len(steps) - 1))
                            end_job(j, last)
                    fc1_jobs(0, 0)
                    fc1_jobs(1, 0)
                    wait_evacuated(*[("f1", 0, 0, m) for m in range(MT)])
                    fc2_jobs(0)
                    fc1_jobs(1, 1)
                    fc1_jobs(1, 2)
                    wait_evacuated(*[("f1", 1, br, m) for br in range(3) for m in range(MT)])
                    fc2_jobs(1)
                    wait_evacuated(*[("f2", q, s) for q in range(2) for s in range(2)])
                    back_jobs("M")
                if n == "E":
                    transposes("F", xn, "F")
                    pe.wait_ge(wconv, 1)
                    for c in range(4):
                        j = ("int", c)
                        pe.wait_ge(*nq_ready.at((c // 2, 1)))
                        ps = start_job(j)
                        for i in range(2):
                            for k in range(2):
                                last = mm(ps[0:ROWS, D * i:D * i + D], nq[:, k].rearrange("p i k -> p (i k)")[:, 128 * (2 * c + i):128 * (2 * c + i) + ROWS],
                                          w8b[:, k], start=(k == 0), stop=(k == 1))
                        end_job(j, last)
            transposes("H", xn, "H")
            wait_evacuated(*nt_jobs("H"))
            ps = start_job(("gate", "H"))
            for c in range(CT):
                for k in range(2):
                    last = mm(ps[:, NE * c:NE * c + NE], xc[0:96 + k, k, 128 * c:128 * c + 128], w("H_gate", k), start=(k == 0), stop=(k == 1))
            end_job(("gate", "H"), last)
            pe.wait_ge(*disp_ready.at("H"))
            for a in range(2):
                ps = start_job(("eT", a))
                for c in range(4 * a, min(CT, 4 * a + 4)):
                    last = nc.tensor.transpose(ps[0:NE, 128 * (c - 4 * a):128 * (c - 4 * a) + 128], disp[:, c], ident[:, :])
                end_job(("eT", a), last)
            pe.wait_ge(loaded["b2e"], 16)
            wait_evacuated(("eT", 0), ("eT", 1))
            for c in range(3):
                ps = start_job(("eb", c))
                for i in range(2 if c < 2 else 1):
                    t = 2 * c + i
                    last = mm(ps[0:crow[t], D * i:D * i + D], dX[0:NE, 128 * t:128 * t + crow[t]], b2t[:], start=True, stop=True)
                end_job(("eb", c), last)
            wait_evacuated(("eb", 0), ("eb", 1), ("eb", 2))

            def fc1(i, b, first=False):
                pe.wait_ge(w1_loaded[b], i * 16 + 16)
                for m in range(MT):
                    for c in range(2):
                        x = 2 * m + c
                        if not (first and x < 4):
                            pe.wait_ge(gelu_done, i * 24 + (12 * b + x - 3))
                        ps = PS[x % 4]
                        for k in range(2):
                            last = mm(ps[:, 0:QT], w1b[:, b, k, 128 * m:128 * m + 128], xc[0:96, k, QT * c:QT * c + QT], start=(k == 0), stop=(k == 1))
                        last.then_inc(fc1_done, 1)

            def fc2(i, b, first=False):
                pe.wait_ge(w2_loaded[b], i * 16 + 16)
                pe.wait_ge(gelu_done, i * 24 + 12 * (b + 1))
                if not first:
                    pe.wait_ge(acc_done, i * 6 + 3 * b)
                for c in range(3):
                    for x in range(2 if c < 2 else 1):
                        t = 2 * c + x
                        for m in range(MT):
                            last = mm(PS[4 + c][0:crow[t], D * x:D * x + D], hbuf[b][:, m, 128 * t:128 * t + crow[t]], w2b[:, b, m],
                                      start=(m == 0), stop=(m == MT - 1))
                    last.then_inc(fc2_done, 1)

            fc1(0, 0, first=True)
            fc1(0, 1)
            fc2(0, 0, first=True)
            with pe.Fori(1, NE // 2) as i:
                fc1(i, 0)
                fc2(i - 1, 1)
                fc1(i, 1)
                fc2(i, 0)
            fc2(NE // 2 - 1, 1)


def kernel(**inputs):
    import numpy as np
    import concourse.bacc as _bacc
    from concourse import mybir as _mybir
    from concourse.bass_utils import run_bass_kernel_spmd as _run

    a = {k: np.asarray(v) for k, v in inputs.items()}
    f32 = np.float32

    def ktiles(wm, bias=None):
        n = wm.shape[1]
        o = np.zeros((97, 2, n), f32)
        o[0:96] = wm.reshape(2, 96, n).transpose(1, 0, 2)
        if bias is not None:
            o[96, 1] = bias
        return o.reshape(97, 2 * n)

    c_qkv = np.concatenate([a["L1_attn_Wq"].T, a["L1_attn_Wk"].T, a["L1_attn_Wv"].T], 1)
    c_bias = np.concatenate([np.zeros(D, f32), a["L1_attn_bk"], a["L1_attn_bv"]])
    seg = {
        "A_qkv": ktiles(a["L0_attn_w_qkv"].T), "A_proj": ktiles(a["L0_attn_w_proj"].T, a["L0_attn_b_proj"]),
        "B_qkv": ktiles(a["L0_ffn_W_qkv"].T, a["L0_ffn_b_qkv"]), "B_gate": ktiles(a["L0_ffn_W_gate"].T, a["L0_ffn_b_gate"]),
        "B_down": ktiles(a["L0_ffn_A"].reshape(NE * RANK, D).T), "B_proj": ktiles(a["L0_ffn_W_proj"].T, a["L0_ffn_b_proj"]),
        "C_qkv": ktiles(c_qkv, c_bias), "C_proj": ktiles(a["L1_attn_Wo"].T, a["L1_attn_bo"]),
        "D_qkv": ktiles(a["L1_ffn_w_qkv"]), "D_proj": ktiles(a["L1_ffn_w_proj"], a["L1_ffn_b_proj"]),
        "D_fc1": ktiles(a["L1_ffn_w_fc1"]),
        "E_qkv": ktiles(a["L2_attn_w_qkv"]), "E_proj": ktiles(a["L2_attn_w_proj"], a["L2_attn_b_proj"]),
        "G_qkv": ktiles(a["L3_attn_w_qkv"], a["L3_attn_b_qkv"]), "H_gate": ktiles(a["L3_ffn_Wr"], a["L3_ffn_br"]),
    }
    wpack = np.concatenate([seg[n] for n, _ in SEGS], 1)

    P = 16
    x = a["x"].reshape(B, 6, P, 6, P, 3).transpose(0, 1, 3, 2, 4, 5).reshape(B, 36, PATCH_K, 128)
    patches = np.zeros((128, PAIRS, PATCH_K, ROWS), f32)
    xt = x.transpose(3, 0, 2, 1).reshape(128, PAIRS, 2, PATCH_K, 36)
    for i in range(2):
        patches[:, :, :, GAP * i + 1:GAP * i + TOK] = xt[:, :, i]

    c128 = np.concatenate([
        a["L0_tok_W"].reshape(PATCH_K, 128, D).transpose(1, 0, 2).reshape(128, -1),
        a["L0_ffn_B_lora"].transpose(0, 2, 1).reshape(NE * RANK, 3 * D),
        a["L1_ffn_w_fc2"].reshape(MT, 128, D).transpose(1, 0, 2).reshape(128, -1)], 1)

    def cput(o, table, name, val):
        at, width = table[name]
        val = np.asarray(val, f32)
        o[0:val.shape[0], at:at + width] = val.reshape(val.shape[0], width)

    consts = np.zeros((128, CCOLS), f32)
    feat = np.arange(HALF)
    cput(consts, CONST_AT, "ident", np.eye(128))
    cput(consts, CONST_AT, "mask_k", feat[:, None] // HD == np.arange(HH)[None])
    row_head = np.arange(GR) // TOK
    col_head = feat // HD
    cput(consts, CONST_AT, "ones_g", np.stack([col_head[None] == HG * g + row_head[:, None] for g in range(2)], 1))
    cput(consts, CONST_AT, "mask_v", (np.arange(D)[None] // HD) % HG == row_head[:, None])
    cput(consts, CONST_AT, "mask_kv", feat[:, None] // HD == np.arange(HH * (HD + 1))[None] // (HD + 1))
    cput(consts, CONST_AT, "tri", np.broadcast_to(np.arange(NE)[None] < np.arange(NE)[:, None], (128, NE, NE)))
    cput(consts, CONST_AT, "expand", LORA_SCALE * (np.arange(NE)[:, None] == np.arange(128)[None] // RANK))
    for name, n in (("m96", D // 2), ("m64", D // 3)):
        m = np.zeros((97, 2, D), f32)
        r = np.arange(96)[:, None] + 96 * np.arange(2)[None]
        m[0:96] = (r < n)[:, :, None] & (np.arange(D) < n)
        m[96, 1] = np.arange(D) < n
        cput(consts, CONST_AT, name, m)
    for name, n in (("c96", D // 2), ("c64", D // 3)):
        cput(consts, CONST_AT, name, (np.arange(96)[:, None] + 96 * np.arange(2)[None]) < n)

    params = np.zeros((128, PCOLS), f32)
    for name, src in (("n1l_g", "L1_ffn_n1l_g"), ("n1l_b", "L1_ffn_n1l_b"), ("n1s_g", "L1_ffn_n1s_g"), ("n1s_b", "L1_ffn_n1s_b"),
                      ("n2l_g", "L1_ffn_n2l_g"), ("n2l_b", "L1_ffn_n2l_b"), ("n2s_g", "L1_ffn_n2s_g"), ("n2s_b", "L1_ffn_n2s_b"),
                      ("gq", "L1_attn_gq"), ("gk", "L1_attn_gk"), ("b_fc2", "L1_ffn_b_fc2")):
        cput(params, PARAM_AT, name, a[src].reshape(2, 96).T)
    cput(params, PARAM_AT, "b_fc1", a["L1_ffn_b_fc1"].reshape(MT, 128).T)
    cput(params, PARAM_AT, "b1", a["L3_ffn_b1"].reshape(NE, MT, 128).transpose(2, 0, 1))
    for name, src in (("gumbel", "L1_ffn_gumbel_weights"), ("bias_q", "L2_ffn_bias"), ("gamma", "L3_attn_ln_gamma"), ("beta", "L3_attn_ln_beta")):
        cput(params, PARAM_AT, name, np.broadcast_to(a[src], (128, a[src].size)))
    pos = np.zeros((128, D), f32)
    cls = np.zeros((128, D), f32)
    for i in range(2):
        pos[GAP * i:GAP * i + TOK] = a["L0_tok_pos_emb"][0]
        cls[GAP * i] = a["L0_tok_class_emb"][0, 0]
    cput(params, PARAM_AT, "pos", pos)
    cput(params, PARAM_AT, "cls", cls)

    arrays = {
        "patches": patches, "wpack": wpack, "c128": c128, "consts": consts, "params": params,
        "w8": np.ascontiguousarray(a["L2_ffn_weight_t"].reshape(2, 96, D).transpose(1, 0, 2)).reshape(96, 2 * D).view(np.int32), "b2e": a["L3_ffn_b2"],
        "w1": a["L3_ffn_W1"].reshape(NE, 2, 96, HID).transpose(0, 2, 1, 3),
        "w2": a["L3_ffn_W2"].reshape(NE, MT, 128, D).transpose(0, 2, 1, 3),
    }
    arrays = {f"in_{k}": np.ascontiguousarray(v) for k, v in arrays.items()}
    nc = _bacc.Bacc("TRN2", target_bir_lowering=False, num_devices=1)
    args = [nc.dram_tensor(k, v.shape, _mybir.dt.from_np(v.dtype), kind="ExternalInput").ap() for k, v in arrays.items()]
    args.append(nc.dram_tensor("out_0", (T, D), _mybir.dt.float32, kind="ExternalOutput").ap())
    build_tower(nc, *args)
    r = _run(nc, [arrays], core_ids=[0])
    return r.results[0]["out_0"].reshape(B, TOK, D)
```

```python
import concourse.bass as bass
from concourse import mybir
from contextlib import ExitStack

B, TOK, D, H = 16, 37, 192, 12
HD = D // H
PAIRS = B // 2
GAP = 64
ROWS = GAP + TOK
T = B * TOK
HALF = D // 2
HH = H // 2
NG, HG = 4, 3
GR = HG * TOK
Q8 = 8
QT = Q8 * TOK
PATCH_K = 6
HID, MT = 768, 6
NE, RANK, TOPK = 8, 16, 2
CT = 5
TPAD = CT * 128
EPS = 1e-5
LORA_SCALE = 2.0
ACT_SCALE, EFF_SCALE = 0.02, 0.02 * 0.01
ROUND = 1.5 * 2.0 ** 23
SCALE = HD ** -0.5

SEGS = [("A_qkv", 3 * D), ("A_proj", D), ("B_qkv", 3 * D), ("B_gate", NE), ("B_down", 128), ("B_proj", D),
        ("C_qkv", 3 * D), ("C_proj", D), ("D_qkv", 3 * D), ("D_proj", D), ("D_fc1", HID),
        ("E_qkv", 3 * D), ("E_proj", D), ("G_qkv", 3 * D), ("H_gate", NE)]
SEG_DRAM, WCOLS = {}, 0
for _n, _w in SEGS:
    SEG_DRAM[_n] = WCOLS
    WCOLS += 2 * _w
LATE = SEG_DRAM["E_qkv"]
SEG_AT = {_n: (SEG_DRAM[_n] % LATE, _w) for _n, _w in SEGS}
W1_AT = WCOLS - LATE
W2_AT = W1_AT + 2 * 2 * HID
WT_COLS = W2_AT + 2 * MT * D
LOADS = [("A_qkv", "A_proj"), ("B_qkv", "B_proj"), ("C_qkv", "C_proj"), ("D_qkv", "D_fc1"), ("E_qkv", "H_gate")]

CONSTS = [("ident", 128), ("mask_k", HH), ("mask_v", HG * HD), ("mask_kv", HH * (HD + 1)),
          ("tri", NE * NE), ("expand", 128), ("m96", 2 * D), ("m64", 2 * D), ("c96", 2), ("c64", 2)]
CONST_AT, CCOLS = {}, 0
for _n, _w in CONSTS:
    CONST_AT[_n] = (CCOLS, _w)
    CCOLS += _w

PARAMS = [("n1l_g", 2), ("n1l_b", 2), ("n1s_g", 2), ("n1s_b", 2), ("n2l_g", 2), ("n2l_b", 2), ("n2s_g", 2),
          ("n2s_b", 2), ("gq", 2), ("gk", 2), ("b_fc1", MT), ("b_fc2", 2), ("b1", NE * MT), ("gumbel", 3),
          ("bias_q", D), ("gamma", D), ("beta", D), ("pos", D), ("cls", D)]
PARAM_AT, PCOLS = {}, 0
for _n, _w in PARAMS:
    PARAM_AT[_n] = (PCOLS, _w)
    PCOLS += _w

LINEAR, SOFTMAX, COLUMN, POLY = "linear", "softmax", "column", "poly"
ATT = [("A", LINEAR), ("B", SOFTMAX), ("C", COLUMN), ("D", SOFTMAX), ("E", POLY), ("G", SOFTMAX)]
KIND = dict(ATT)
HAS_PROJ = "ABCDE"
DIRECT = [(0, 3), (3, 3), (6, 2)]
P8 = PAIRS // 2
VW = H * (HD + 1)
TAIL = 6
ZEROED = 8
LOADED_BY = {"A": "A_qkv", "B": "B_qkv", "C": "C_qkv", "D": "D_qkv", "E": "E_qkv"}
MLP_BR = [(0,), (0, 1, 2)]
KEEP = [D, D // 2, D // 3]

PHASES = ([("tok", "P")]
          + [("A", p) for p in ("T", "F", "M", "O", "Z", "P")]
          + [("B", p) for p in ("T", "G", "H", "F", "S", "W", "X", "O", "Z", "P")]
          + [("C", p) for p in ("T", "K", "R", "S", "W", "O", "Z", "P")]
          + [("D", p) for p in ("T", "F", "S", "W", "X", "O", "Z", "P")] + [("D2", p) for p in ("T", "U", "V", "P")]
          + [("E", p) for p in ("T", "F", "S", "W", "X", "O", "Z", "P")]
          + [("F", p) for p in ("T", "P")]
          + [("G", p) for p in ("T", "F", "S", "W", "X", "O")] + [("G2", "P")]
          + [("H", "T")])
ORDER = ("01001010110011010011010101001100110010101010100111001101010101001010010110101100010110011100110101010101010101")
SCHEDULE, _at = [], [0, 0]
for _q in map(int, ORDER):
    SCHEDULE.append(PHASES[_at[_q]] + (_q,))
    _at[_q] += 1
assert _at == [len(PHASES)] * 2
X_OCTS = [_q for _n, _p, _q in SCHEDULE if _n == "H"]
SECOND_G2 = max(i for i, _s in enumerate(SCHEDULE) if _s[0] == "G2")
NEXT_LN = {("tok", "P"): "A", ("A", "P"): "B", ("B", "P"): "C", ("C", "P"): "D", ("D", "P"): "D2", ("D2", "P"): "E",
           ("E", "P"): "F", ("F", "P"): "G", ("G", "O"): "G2", ("G2", "P"): "H"}


def phase_jobs(n, ph, q):
    cs, ps = range(2 * q, 2 * q + 2), range(P8 * q, P8 * q + P8)
    kind = KIND.get(n)
    if n == "tok":
        return [("tok", c) for c in cs]
    if ph == "T":
        return [("nT", n, q, s) for s in range(2)]
    if (n, ph) == ("A", "F"):
        return [("q", n, q, s) for s in range(2)] + [("kv", p) for p in ps]
    if (n, ph) == ("A", "M"):
        return [("kvm", c, par) for c in cs for par in range(2)]
    if ph == "Z":
        return [("oT", n, q, s) for s in range(2)]
    if ph == "G":
        return [("gate", q), ("a", q)]
    if ph == "H":
        return [("dT", q), ("dx", q)]
    if ph in ("F", "R"):
        return [(k, n, q, s) for s in range(2) for k in ("k", "q")]
    if ph == "K":
        return [("qk", p) for p in ps]
    if ph == "S":
        first = [("s", n, p) for p in ps] if kind != COLUMN else [("e", n, q, j) for j in range(3)]
        return first
    if ph == "W":
        return [("v", n, p) for p in ps]
    if ph == "X":
        return [("t", n, p) for p in ps]
    if ph == "O":
        return [("o", n, c) for c in cs]
    if ph == "U":
        return [("f1", q, 0, m) for m in range(MT)]
    if ph == "V":
        return [("f1", q, br, m) for br in MLP_BR[q][1:] for m in range(MT)] + [("f2", q, s) for s in range(2)]
    if (n, ph) == ("F", "P"):
        return [("int", c) for c in cs]
    if (n, ph) == ("G2", "P"):
        return []
    if (n, ph) == ("D2", "P"):
        return [("back", n, c) for c in cs]
    assert ph == "P", (n, ph)
    return [("p", n, c) for c in cs]


def job_order():
    jobs = [j for step in SCHEDULE for j in phase_jobs(*step)]
    tail = [("gate", "H"), ("eT", 0), ("eT", 1)] + [("eb", c) for c in range(3)]
    assert len(tail) == TAIL
    return jobs + tail


class Signal:

    def __init__(self, sem, events):
        self.sem, self.index, self.seen = sem, {e: i for i, e in enumerate(events)}, 0

    def inc(self, event):
        assert self.index[event] == self.seen, (event, self.seen)
        self.seen += 1
        return self.sem, 1

    def at(self, event):
        return self.sem, self.index[event] + 1


def build_tower(nc, patches, wpack, c128, consts, params, w8, b2e, w1, w2, out):
    F, FB = mybir.dt.float32, mybir.dt.bfloat16
    ALU, ACT, AX = mybir.AluOpType, mybir.ActivationFunctionType, mybir.AxisListType
    ctx = ExitStack()
    with ctx:
        def sb(name, shape, dt=F):
            return ctx.enter_context(nc.sbuf_tensor(name, shape, dt))

        def sem(name):
            return ctx.enter_context(nc.semaphore(name))

        wt = sb("weights", [128, WT_COLS])
        cst = sb("constants", [128, CCOLS])
        par = sb("parameters", [128, PCOLS])
        tokw = sb("tok_w", [128, PATCH_K, D])
        bup = sb("lora_up", [128, 3 * D])
        fc2w = sb("fc2_w", [128, MT, D])
        h = sb("h", [128, PAIRS, D])
        xn = sb("xn", [128, PAIRS, D])
        xy = sb("x2_y", [128, 2, 2, P8, D])
        x2 = [xy[:, q, 0] for q in range(2)]
        yt = [xy[:, q, 1] for q in range(2)]
        adrep = [xy[:, q].rearrange("p a c d -> p (a c d)")[:, 0:Q8 * GR].rearrange("p (i c) -> p i c", c=GR) for q in range(2)]
        nT = [sb(f"nT{s}", [97, B, GAP]) for s in range(2)]
        oT = [sb(f"oT{s}", [97, B, GAP]) for s in range(2)]
        qT = [sb(f"qT{s}", [96, T]) for s in range(2)]
        with ExitStack() as attention_only:
            rep_raw = attention_only.enter_context(nc.sbuf_tensor("rep", [128, 2, 2 * Q8 * GR], F))
            ar = attention_only.enter_context(nc.sbuf_tensor("arena_e", [128, PAIRS, H * TOK], F))
        w1h, w1l = (sb(n, [96, 2, 2, HID], mybir.dt.float32r) for n in ("w1_high", "w1_low"))
        xl = sb("x_low", [96, 2, T], mybir.dt.float32r)
        nrep = [[rep_raw[0:97, q, s * Q8 * GR:(s + 1) * Q8 * GR].rearrange("p (i c) -> p i c", c=GR) for s in range(2)] for q in range(2)]
        big = sb("arena_k", [128, 2, HH * T])
        bigf = big[:].rearrange("p q x -> p (q x)")
        kblk = [[big[0:96, q, s * HH * QT:(s + 1) * HH * QT].rearrange("p (i h k) -> p i h k", h=HH, k=TOK) for s in range(2)] for q in range(2)]
        patch = [big[:, q, 0:P8 * PATCH_K * ROWS].rearrange("p (c k t) -> p c k t", k=PATCH_K, t=ROWS) for q in range(2)]
        hid = [[big[:, q, b * MT * QT:(b + 1) * MT * QT].rearrange("p (m t) -> p m t", t=QT) for b in range(2)]
               + [rep_raw[:, q, :].rearrange("p (m t) -> p m t", t=QT)] for q in range(2)]
        hbuf = [bigf[:, b * MT * T:(b + 1) * MT * T].rearrange("p (m t) -> p m t", t=T) for b in range(2)]
        vblk_raw = sb("vblk", [128, B * VW])
        vblk = vblk_raw[0:GR].rearrange("p (i g r e) -> p i g r e", g=NG, r=HG, e=HD + 1)
        et_raw = sb("et", [128, 2, NG, QT])
        et = [et_raw[0:GR, q] for q in range(2)]
        ad, dX, dispT = ([et_raw[0:r, q, x] for q in range(2)] for r, x in ((128, 0), (128, 1), (NE, 2)))
        eT = et_raw[0:NE].rearrange("p q g t -> p (q g t)")
        disp = sb("disp", [128, PAIRS, NE])
        gsm = sb("gates", [128, 4, PAIRS * NE])
        stats = sb("stats", [128, PAIRS, 6])
        mv = sb("mean_var", [128, PAIRS, 2])
        rstd = sb("rstd", [128, PAIRS])
        nmr = sb("minus_mean_rstd", [128, PAIRS])
        rst2 = sb("rstd_second", [128, PAIRS])
        rtmp = sb("rstd_tmp", [128, 2 * PAIRS])
        stats_qk = sb("stats_qk", [128, 2 * PAIRS, 6])
        mv_qk = sb("mean_var_qk", [128, 2 * PAIRS, 2])
        rstd_qk = sb("rstd_qk", [128, 2 * PAIRS])
        mhalf = sb("minus_half", [128, 2 * PAIRS])
        mx = sb("score_max", [128, 8, H])
        rs = sb("row_recip", [128, 8, 2 * H])
        grow = sb("gate_rows", [128, 3, PAIRS])
        gqs = sb("gain_q_scaled", [96, 2])
        maskg = sb("mask_k_gain", [96, 2, HH])
        wps = sb("proj_small", [97, 2, D])
        b2s = sb("b_fc2_small", [96, 2])
        gcol = sb("gumbel_cols", [96, 2, 2])
        fc2s = [tokw[:]] + [sb(f"fc2_small{i}", [128, MT, KEEP[i]])[:] for i in (1, 2)]
        w8i = sb("w8_int", [96, 2 * D // 4], mybir.dt.int32)
        w8b = sb("w8_bf16", [96, 2, D], FB)
        nq = sb("n_quant", [96, 2, B, GAP], FB)
        b2t = sb("expert_b2", [NE, D])
        b1cur = sb("expert_b1", [128, 2, MT])
        xh = sb("x_high", [96, 2, T], mybir.dt.float32r)

        PS = [ctx.enter_context(nc.psum_tensor(f"bank{b}", [128, 512], F)) for b in range(8)]

        def w(name, k, a=0, n=None):
            at, width = SEG_AT[name]
            n = width if n is None else n
            return wt[0:96 + k, at + k * width + a:at + k * width + a + n]

        def con(name, rows=128):
            at, width = CONST_AT[name]
            return cst[0:rows, at:at + width]

        def prm(name, rows=128):
            at, width = PARAM_AT[name]
            return par[0:rows, at:at + width]

        ident = con("ident")

        order = job_order()
        where, _in_bank = {}, [0] * 8
        for i, j in enumerate(order):
            b = i % 8 if i < len(order) - TAIL else 4 + (i - len(order) + TAIL) % 4
            where[j] = (b, _in_bank[b])
            _in_bank[b] += 1
        bank_filled = [sem(f"bank{b}_filled") for b in range(8)]
        bank_read = [sem(f"bank{b}_read") for b in range(8)]

        def bank(j):
            return PS[where[j][0]]

        def filled(j):
            b, k = where[j]
            return bank_filled[b], k + 1

        def evacuated(j):
            b, k = where[j]
            return bank_read[b], k + 1

        def updated(name, c):
            job = {"tok": ("tok", c), "F": ("int", c), "D2": ("back", "D2", c), "G": ("back", "G", c)}.get(name, ("p", name, c))
            return g_done.at(c) if name == "G2" else evacuated(job)

        def freed(j):
            return bank_read[where[j][0]], 1

        loaded = {n: sem(f"loaded_{n}") for n in ["consts", "params", "tokw", "bup", "fc2w", "w8", "b2e"]
                  + [f"patch{c}" for c in range(PAIRS // 2)] + [a for a, _ in LOADS]}
        lns = [e for n, ph, q in SCHEDULE for e in ([(NEXT_LN[n, ph], q)] if (n, ph) in NEXT_LN
                                                      else [("Cqk", q)] if ph == "K" else [])]
        norms = [(n, q) for n, ph, q in SCHEDULE if ph == "T" or n == "G2"]

        def steps(*which):
            return [(n, q) for n, ph, q in SCHEDULE if (n, ph) in which]
        g_done = Signal(sem("g_done"), [c for _, q in steps(("G2", "P")) for c in (2 * q, 2 * q + 1)])
        var_ready = Signal(sem("var_ready"), lns)
        rstd_ready = Signal(sem("rstd_ready"), lns)
        xn_ready = Signal(sem("xn_ready"), norms)
        rep_ready = [Signal(sem(f"rep_ready{s}"), steps(*[(n, "T") for n in "BCDEG"])) for s in range(2)]
        adrep_ready = Signal(sem("adrep_ready"), steps(("B", "H")))
        h_plus = Signal(sem("h_plus"), steps(("C", "T"), ("D", "P"), ("F", "T")))
        smax = [(n, p) for n, q in steps(*[(n, "S") for n in "BDG"]) for p in range(P8 * q, P8 * q + P8)]
        exp_ready = Signal(sem("exp_ready"), smax)
        direct = [(n, q, j) for n, q in steps(("C", "S")) for j in range(3)]
        eexp = Signal(sem("eexp"), direct)
        et_ready = Signal(sem("et_ready"), direct)
        elu_exp = Signal(sem("elu_exp"), [e for _, q in steps(("A", "F")) for e in [("q", q, s) for s in range(2)]
                                          + [("k", p) for p in range(P8 * q, P8 * q + P8)]])
        zeroed = sem("zeroed")
        maskg_ready = sem("maskg_ready")
        mixed = sem("mixed")
        gates = [q for _, q in steps(("B", "G"))] + ["H"]
        gate_exp = Signal(sem("gate_exp"), gates)
        disp_ready = Signal(sem("disp_ready"), gates)
        wconv = sem("w8_converted")
        nq_ready = Signal(sem("nq_ready"), [(q, s) for _, q in steps(("F", "T")) for s in range(2)])
        dve_chain = sem("dve_chain")
        act_chain = sem("act_chain")
        pool_chain = sem("pool_chain")
        b1_ready = sem("b1_ready")
        fc1_done, gelu_done = sem("fc1_done"), sem("gelu_done")
        fc2_done, acc_done = sem("fc2_done"), sem("acc_done")
        w1_high, w1_low = sem("w1_high"), sem("w1_low")
        x_high, x_split = sem("x_high"), sem("x_split")
        w1_loaded = [sem(f"w1_loaded{b}") for b in range(2)]
        w2_loaded = [sem(f"w2_loaded{b}") for b in range(2)]
        h_stored, h_back, stored = sem("h_stored"), sem("h_back"), sem("stored")

        w1b = wt[0:96, W1_AT:W2_AT].rearrange("p (b k n) -> p b k n", b=2, k=2)
        w2b = wt[:, W2_AT:WT_COLS].rearrange("p (b m d) -> p b m d", b=2, m=MT)
        ec = vblk_raw[:, 0:2 * TPAD + 2 * CT * D]
        xc = ec[0:97, 0:2 * TPAD].rearrange("p (s t) -> p s t", s=2)
        hc = ec[:, 2 * TPAD:2 * TPAD + CT * D].rearrange("p (c d) -> p c d", d=D)
        acc = ec[:, 2 * TPAD + CT * D:2 * TPAD + 2 * CT * D].rearrange("p (c d) -> p c d", d=D)
        scratch = nc.dram_tensor("h_compact", (T, D), F).ap()
        crow = [min(128, T - 128 * c) for c in range(CT)]

        block = ctx.enter_context(nc.Block())

        def spaced(j):
            return bank(j)[0:96, :].rearrange("p (i k) -> p i k", k=GAP)[:, :, 0:TOK]

        @block.sync
        def _(sp):
            sp.dma_start(tokw[:], c128[:, 0:PATCH_K * D].rearrange("p (k d) -> p k d", d=D)).then_inc(loaded["tokw"], 16)
            for c in range(PAIRS // 2):
                a = 2 * c % P8
                sp.dma_start(patch[2 * c // P8][:, a:a + 2], patches[:, 2 * c:2 * c + 2]).then_inc(loaded[f"patch{c}"], 16)
            sp.dma_start(par[:], params).then_inc(loaded["params"], 16)
            sp.dma_start(w8i[:], w8).then_inc(loaded["w8"], 16)
            sp.dma_start(b2t[:], b2e).then_inc(loaded["b2e"], 16)
            for first, last in LOADS:
                a, z = SEG_AT[first][0], SEG_AT[last][0] + 2 * SEG_AT[last][1]
                late = first == "E_qkv"
                if late:
                    for c in (1, 3):
                        sp.wait_ge(*updated("B", c))
                d = SEG_DRAM[first]
                sp.dma_start(wt[0:97, a:z], wpack[:, d:d + z - a]).then_inc(loaded[first], 16)
                if first == "A_qkv":
                    sp.dma_start(bup[:], c128[:, PATCH_K * D:PATCH_K * D + 3 * D]).then_inc(loaded["bup"], 16)
                if first == "C_qkv":
                    sp.dma_start(fc2w[:], c128[:, PATCH_K * D + 3 * D:].rearrange("p (m d) -> p m d", d=D)).then_inc(loaded["fc2w"], 16)
            for c in (1, 3):
                sp.wait_ge(*updated("D2", c))
            for b in range(2):
                sp.dma_start(w1b[:, b], w1[b]).then_inc(w1_loaded[b], 16)
                sp.dma_start(w2b[:, b], w2[b]).then_inc(w2_loaded[b], 16)
            for c in (1, 3):
                sp.wait_ge(*updated("G2", c))
            hd = scratch.rearrange("(p i k) d -> i k p d", i=2, k=TOK)
            for i in range(2):
                sp.dma_start(hd[i], h[GAP * i:GAP * i + TOK]).then_inc(h_stored, 16)
            sp.wait_ge(h_stored, 32)
            sp.dma_start(hc[:, 0:CT - 1], scratch[0:128 * (CT - 1)].rearrange("(c p) d -> p c d", p=128)).then_inc(h_back, 16)
            sp.dma_start(hc[0:crow[-1], CT - 1], scratch[128 * (CT - 1):T]).then_inc(h_back, 16)
            with sp.Fori(0, NE // 2 - 1) as i:
                for b in range(2):
                    sp.wait_ge(w1_low, i * 2 + (b + 1))
                    sp.dma_start(w1b[:, b], w1[i * 2 + (2 + b)]).then_inc(w1_loaded[b], 16)
            sp.wait_ge(acc_done, 3 * NE)
            sp.dma_start(out[0:128 * (CT - 1)].rearrange("(c p) d -> p c d", p=128), acc[:, 0:CT - 1]).then_inc(stored, 16)
            sp.dma_start(out[128 * (CT - 1):T], acc[0:crow[-1], CT - 1]).then_inc(stored, 16)
            sp.wait_ge(stored, 32)

        @block.gpsimd
        def _(pool):
            g = nc.gpsimd
            links = [0]

            def link(ins):
                links[0] += 1
                ins.then_inc(pool_chain, 1)
                pool.wait_ge(pool_chain, links[0])

            link(g.memset(mhalf[:], -0.5))
            link(g.memset(nq[:], 0.0))

            def root(n, q):
                pool.wait_ge(*var_ready.at((n, q)))
                a = slice(P8 * q, P8 * q + P8)
                link(g.tensor_scalar(rtmp[0:ROWS, a], mv[0:ROWS, a, 1], EPS, None, ALU.add))
                link(g.tensor_scalar(nmr[0:ROWS, a], mv[0:ROWS, a, 0], -1.0, None, ALU.mult))
                link(g.tensor_tensor(rstd[0:ROWS, a], rtmp[0:ROWS, a], mhalf[0:ROWS, a], ALU.pow))
                if n == "D":
                    link(g.tensor_tensor(rtmp[0:ROWS, a], mv[0:ROWS, a, 1], rstd[0:ROWS, a], ALU.mult))
                    link(g.tensor_tensor(rtmp[0:ROWS, a], rtmp[0:ROWS, a], rstd[0:ROWS, a], ALU.mult))
                    link(g.tensor_scalar(rtmp[0:ROWS, a], rtmp[0:ROWS, a], EPS, None, ALU.add))
                    link(g.tensor_tensor(rst2[0:ROWS, a], rtmp[0:ROWS, a], mhalf[0:ROWS, a], ALU.pow))
                g.tensor_tensor(nmr[0:ROWS, a], nmr[0:ROWS, a], rstd[0:ROWS, a], ALU.mult).then_inc(*rstd_ready.inc((n, q)))
                pool.wait_ge(*rstd_ready.at((n, q)))

            def root_qk(q):
                pool.wait_ge(*var_ready.at(("Cqk", q)))
                a = slice(2 * P8 * q, 2 * P8 * q + 2 * P8)
                link(g.tensor_scalar(rtmp[0:ROWS, a], mv_qk[0:ROWS, a, 1], EPS, None, ALU.add))
                g.tensor_tensor(rstd_qk[0:ROWS, a], rtmp[0:ROWS, a], mhalf[0:ROWS, a], ALU.pow).then_inc(*rstd_ready.inc(("Cqk", q)))
                pool.wait_ge(*rstd_ready.at(("Cqk", q)))

            def add_to_h(n, q, src):
                a = slice(P8 * q, P8 * q + P8)
                g.tensor_tensor(h[0:ROWS, a], h[0:ROWS, a], src, ALU.add).then_inc(*h_plus.inc((n, q)))
                pool.wait_ge(*h_plus.at((n, q)))

            def mix_small():
                for name in ("params", "consts", "D_qkv", "fc2w"):
                    pool.wait_ge(loaded[name], 16)
                gw, m96, m64 = prm("gumbel"), con("m96", 97), con("m64", 97)
                gm = m96.rearrange("p (k d) -> p k d", k=2)
                link(g.tensor_scalar(m96, m96, gw[0:97, 1:2], gw[0:97, 0:1], ALU.mult, ALU.add))
                link(g.tensor_scalar(m64, m64, gw[0:97, 2:3], None, ALU.mult))
                link(g.tensor_tensor(m96, m96, m64, ALU.add))
                for k in range(2):
                    link(g.tensor_tensor(wps[0:96 + k, k], w("D_proj", k), gm[0:96 + k, k], ALU.mult))
                link(g.tensor_scalar(gcol[:, 0], con("c96", 96), gw[0:96, 1:2], gw[0:96, 0:1], ALU.mult, ALU.add))
                link(g.tensor_scalar(gcol[:, 1], con("c64", 96), gw[0:96, 2:3], None, ALU.mult))
                link(g.tensor_tensor(gcol[:, 0], gcol[:, 0], gcol[:, 1], ALU.add))
                link(g.tensor_tensor(b2s[:], prm("b_fc2", 96), gcol[:, 0], ALU.mult))

            def mix_fc2(i):
                for c in range(4):
                    pool.wait_ge(*filled(("tok", c)))
                g.tensor_scalar(fc2s[i], fc2w[:, :, 0:KEEP[i]], prm("gumbel")[:, i:i + 1], None, ALU.mult).then_inc(mixed, 1)
                pool.wait_ge(mixed, i + 1)

            def split_low(e, b):
                pool.wait_ge(w1_high, e + 1)
                g.tensor_tensor(w1l[:, b], w1b[:, b], w1h[:, b].bitcast(F), ALU.subtract).then_inc(w1_low, 1)
                pool.wait_ge(w1_low, e + 1)

            for step, (n, ph, q) in enumerate(SCHEDULE):
                if (n, ph, q) == ("A", "F", 0):
                    mix_small()
                if n == "B" and ph in "GHF" and q == 0:
                    mix_fc2("GHF".index(ph))
                if (n, ph, q) == ("B", "G", 1):
                    pool.wait_ge(loaded["w8"], 16)
                    g.tensor_copy(w8b[:].rearrange("p k d -> p (k d)"), w8i[:].bitcast(mybir.dt.int8)).then_inc(wconv, 1)
                    pool.wait_ge(wconv, 1)
                if step == SECOND_G2:
                    split_low(0, 0)
                if (n, ph) in NEXT_LN:
                    root(NEXT_LN[n, ph], q)
                if ph == "K":
                    root_qk(q)
                if (n, ph) == ("C", "T"):
                    pool.wait_ge(*xn_ready.at((n, q)))
                    add_to_h(n, q, xn[0:ROWS, P8 * q:P8 * q + P8])
                if (n, ph) == ("D", "P"):
                    for c in (2 * q, 2 * q + 1):
                        pool.wait_ge(*updated("D", c))
                    add_to_h(n, q, yt[q][0:ROWS])
                if (n, ph) == ("F", "T"):
                    pool.wait_ge(*xn_ready.at((n, q)))
                    add_to_h(n, q, prm("bias_q", ROWS).unsqueeze(1).broadcast_to([ROWS, P8, D]))
                if step == SECOND_G2:
                    split_low(1, 1)
            with pool.Fori(1, NE // 2) as i:
                for b in range(2):
                    split_low(i * 2 + b, b)

        @block.scalar
        def _(act):
            sc = nc.scalar
            links = [0]
            act.dma_start(cst[:], consts).then_inc(loaded["consts"], 16)

            def mark(ins):
                links[0] += 1
                ins.then_inc(act_chain, 1)

            def normalise(n, q):
                act.wait_ge(*rstd_ready.at((n, q)))
                for p in range(P8):
                    r = P8 * q + p
                    src, dst = (yt[q][0:ROWS, p], x2[q][0:ROWS, p]) if n in ("D2", "G2") else (h[0:ROWS, r], xn[0:ROWS, r])
                    ins = sc.activation(dst, src, ACT.Identity, scale=rstd[0:ROWS, r:r + 1], bias=nmr[0:ROWS, r:r + 1])
                    if n == "D" or p < P8 - 1:
                        mark(ins)
                if n == "D":
                    act.wait_ge(act_chain, links[0])
                    for p in range(P8):
                        ins = sc.activation(x2[q][0:ROWS, p], xn[0:ROWS, P8 * q + p], ACT.Identity,
                                            scale=rst2[0:ROWS, P8 * q + p:P8 * q + p + 1], bias=0.0)
                        if p < P8 - 1:
                            mark(ins)
                ins.then_inc(*xn_ready.inc((n, q)))

            def nt_copy(n, q):
                j = ("nT", n, q, 0)
                act.wait_ge(*filled(j))
                src = spaced(j)
                dst = nT[0][0:96, Q8 * q:Q8 * q + Q8, 0:TOK]
                if n in ("D", "D2"):
                    ln = ("n1" if n == "D" else "n2") + ("l" if q == 0 else "s")
                    sc.activation(dst, src, ACT.Identity, bias=prm(ln + "_b", 96)[:, 0:1], scale=prm(ln + "_g", 96)[:, 0:1]).then_inc(*freed(j))
                elif n == "H":
                    sc.activation(xc[0:96, 0, QT * q:QT * q + QT].rearrange("p (i k) -> p i k", k=TOK), src, ACT.Copy).then_inc(*freed(j))
                else:
                    sc.activation(dst, src, ACT.Copy).then_inc(*freed(j))
                if n == "H":
                    act.wait_ge(*evacuated(j))
                    sc.activation(xh[:, 0, QT * q:QT * q + QT], xc[0:96, 0, QT * q:QT * q + QT], ACT.Copy).then_inc(x_high, 1)
                if n in "BCDEG":
                    act.wait_ge(*evacuated(j))
                    sc.activation(nrep[q][0][0:96].rearrange("p i (r k) -> p i r k", k=TOK),
                                  dst.unsqueeze(2).broadcast_to([96, Q8, HG, TOK]), ACT.Copy).then_inc(*rep_ready[0].inc((n, q)))

            def key_blocks(n, q):
                j = ("k", n, q, 0)
                act.wait_ge(*filled(j))
                mask = maskg[:, 0] if n == "C" else con("mask_k", 96)
                src = spaced(j) if n == "C" else bank(j)[0:96, 0:QT].rearrange("p (i k) -> p i k", k=TOK)
                for x in range(HH):
                    ins = sc.activation(kblk[q][0][:, :, x], src, ACT.Copy, scale=mask[:, x:x + 1])
                    if x < HH - 1:
                        mark(ins)
                ins.then_inc(*freed(j))

            def split_high(e, b):
                act.wait_ge(w1_loaded[b], e // 2 * 16 + 16)
                sc.activation(w1h[:, b], w1b[:, b], ACT.Copy).then_inc(w1_high, 1)

            act.wait_ge(zeroed, ZEROED)
            act.wait_ge(loaded["params"], 16)
            act.wait_ge(loaded["consts"], 16)
            for step, (n, ph, q) in enumerate(SCHEDULE):
                ps = range(P8 * q, P8 * q + P8)
                kind = KIND.get(n)
                if ph == "T" or n == "G2":
                    normalise(n, q)
                if ph == "T" and n != "F":
                    nt_copy(n, q)
                if (n, ph) == ("A", "F"):
                    for s in range(2):
                        j = ("q", n, q, s)
                        act.wait_ge(*filled(j))
                        sc.activation(qT[s][:, QT * q:QT * q + QT], bank(j)[0:96, 0:QT], ACT.Exp).then_inc(*elu_exp.inc(("q", q, s)))
                    for p in ps:
                        act.wait_ge(*filled(("kv", p)))
                        sc.activation(x2[q][0:ROWS, p % P8], bank(("kv", p))[0:ROWS, 0:D], ACT.Exp).then_inc(*elu_exp.inc(("k", p)))
                if ph == "Z":
                    j = ("oT", n, q, 0)
                    act.wait_ge(*filled(j))
                    sc.activation(oT[0][0:96, Q8 * q:Q8 * q + Q8, 0:TOK], spaced(j), ACT.Copy).then_inc(*freed(j))
                if ph == "G":
                    act.wait_ge(*evacuated(("gate", q)))
                    a = slice(P8 * NE * q, P8 * NE * q + P8 * NE)
                    sc.activation(gsm[0:ROWS, 1, a], gsm[0:ROWS, 0, a], ACT.Exp).then_inc(*gate_exp.inc(q))
                if ph == "H":
                    j = ("dx", q)
                    act.wait_ge(*filled(j))
                    sc.activation(dX[q], bank(j)[:, 0:QT], ACT.Copy).then_inc(*freed(j))
                if ph == "F" and n != "A" or ph == "R":
                    if n == "C":
                        act.wait_ge(maskg_ready, 2)
                    key_blocks(n, q)
                    for s in range(2):
                        j = ("q", n, q, s)
                        act.wait_ge(*filled(j))
                        if n == "C":
                            sc.activation(qT[s][:, QT * q:QT * q + QT].rearrange("p (i k) -> p i k", k=TOK), spaced(j),
                                          ACT.Copy, scale=gqs[:, s:s + 1]).then_inc(*freed(j))
                        else:
                            sc.activation(qT[s][:, QT * q:QT * q + QT], bank(j)[0:96, 0:QT], ACT.Copy, scale=SCALE).then_inc(*freed(j))
                if ph == "S" and kind == SOFTMAX:
                    for p in ps:
                        act.wait_ge(*evacuated(("s", n, p)))
                        sc.activation(ar[0:ROWS, p], ar[0:ROWS, p], ACT.Exp).then_inc(*exp_ready.inc((n, p)))
                if ph == "S" and kind == POLY:
                    for p in ps:
                        j = ("s", n, p)
                        act.wait_ge(*filled(j))
                        sc.activation(ar[0:ROWS, p], bank(j)[0:ROWS, 0:H * TOK], ACT.Square, bias=1.0).then_inc(*freed(j))
                if ph == "S" and kind == COLUMN:
                    for x in range(3):
                        act.wait_ge(*evacuated(("e", n, q, x)))
                        a = ar[0:GR, P8 * q + x, 0:DIRECT[x][1] * NG * TOK]
                        sc.activation(a, a, ACT.Exp).then_inc(*eexp.inc((n, q, x)))
                if ph == "X" and kind == SOFTMAX:
                    if n == "B":
                        act.wait_ge(*adrep_ready.at(("B", q)))
                    for p in ps:
                        j = ("t", n, p)
                        act.wait_ge(*filled(j))
                        sc.activation(et[q][:, :, 2 * TOK * (p % P8):2 * TOK * (p % P8) + 2 * TOK].rearrange("p g (i k) -> p g i k", k=TOK),
                                      bank(j)[0:GR, :].rearrange("p (g i k) -> p g i k", g=NG, k=GAP)[:, :, :, 0:TOK],
                                      ACT.Copy).then_inc(*freed(j))
                if ph == "O" and n == "C":
                    for c in range(2 * q, 2 * q + 2):
                        j = ("o", n, c)
                        act.wait_ge(*filled(j))
                        a = 2 * c - P8 * q
                        sc.activation(x2[q][0:ROWS, a:a + 2].rearrange("p c (h e) -> p (c h) e", e=HD),
                                      bank(j)[0:ROWS, 0:2 * VW].rearrange("p (c e) -> p c e", e=HD + 1)[:, :, 0:HD], ACT.Copy).then_inc(*freed(j))
                if ph in "UV":
                    for br in MLP_BR[q][:1] if ph == "U" else MLP_BR[q][1:]:
                        for m in range(MT):
                            j = ("f1", q, br, m)
                            act.wait_ge(*filled(j))
                            sc.activation(hid[q][br][:, m], bank(j)[:, 0:QT], ACT.Gelu, bias=prm("b_fc1")[:, m:m + 1]).then_inc(*freed(j))
                if step == SECOND_G2:
                    for p in range(PAIRS):
                        act.wait_ge(*filled(("v", "G", p)))
                        act.wait_ge(*filled(("t", "G", p)))
                    for b in range(2):
                        split_high(b, b)
            act.wait_ge(*evacuated(("gate", "H")))
            sc.activation(gsm[:, 1, 0:CT * NE], gsm[:, 0, 0:CT * NE], ACT.Exp).then_inc(*gate_exp.inc("H"))

            def gelus(i, b, lag=0):
                at = PARAM_AT["b1"][0] + (b - 2 * lag) * MT
                src = par[:, at + i * 2 * MT:at + i * 2 * MT + MT] if isinstance(i, int) else par[:, bass.ds(i * (2 * MT) + at, MT)]
                sc.activation(b1cur[:, b], src, ACT.Copy).then_inc(b1_ready, 1)
                act.wait_ge(b1_ready, i * 2 + (b + 1 - 2 * lag))
                if lag or i:
                    act.wait_ge(fc2_done, i * 6 + (3 * (b + 1) - 6 - 6 * lag))
                    act.dma_start(w2b[:, b], w2[i * 2 + (b - 2 * lag)]).then_inc(w2_loaded[b], 16)
                for m in range(MT):
                    for c in range(2):
                        act.wait_ge(fc1_done, i * 24 + (12 * b + 2 * m + c + 1 - 24 * lag))
                        sc.activation(hbuf[b][:, m, QT * c:QT * c + QT], PS[(2 * m + c) % 4][:, 0:QT], ACT.Gelu,
                                      bias=b1cur[:, b, m:m + 1]).then_inc(gelu_done, 1)
            for b in range(2):
                gelus(0, b)
                split_high(2 + b, b)
            with act.Fori(2, NE // 2) as i:
                for b in range(2):
                    gelus(i, b, lag=1)
                    act.wait_ge(w1_loaded[b], i * 16 + 16)
                    sc.activation(w1h[:, b], w1b[:, b], ACT.Copy).then_inc(w1_high, 1)
            for b in range(2):
                gelus(NE // 2 - 1, b)

        @block.vector
        def _(dve):
            v = nc.vector
            links = [0]

            def mark(ins):
                links[0] += 1
                ins.then_inc(dve_chain, 1)

            def settle():
                dve.wait_ge(dve_chain, links[0])

            def link(ins):
                mark(ins)
                settle()

            def moments(n, q, upd):
                for p in range(P8 * q, P8 * q + P8):
                    if p % 2 == 0 and upd != "G":
                        dve.wait_ge(*updated(upd, p // 2))
                    mark(v.bn_stats(stats[0:ROWS, p], yt[q][0:ROWS, p % P8] if n in ("D2", "G2") else h[0:ROWS, p]))
                settle()
                for p in range(P8 * q, P8 * q + P8):
                    ins = v.bn_aggr(mv[0:ROWS, p], stats[0:ROWS, p])
                    if p < P8 * q + P8 - 1:
                        mark(ins)
                ins.then_inc(*var_ready.inc((n, q)))

            def nt_copy(n, q):
                j = ("nT", n, q, 1)
                dve.wait_ge(*filled(j))
                src = spaced(j)
                dst = nT[1][0:96, Q8 * q:Q8 * q + Q8, 0:TOK]
                if n in ("D", "D2"):
                    ln = ("n1" if n == "D" else "n2") + ("l" if q == 0 else "s")
                    v.tensor_scalar(dst, src, prm(ln + "_g", 96)[:, 1:2], prm(ln + "_b", 96)[:, 1:2],
                                    ALU.mult, ALU.add).then_inc(*freed(j))
                elif n == "H":
                    v.tensor_copy(xc[0:96, 1, QT * q:QT * q + QT].rearrange("p (i k) -> p i k", k=TOK), src).then_inc(*freed(j))
                else:
                    v.tensor_copy(dst, src).then_inc(*freed(j))
                if n == "H":
                    dve.wait_ge(*evacuated(j))
                    a = slice(QT * q, QT * q + QT)
                    link(v.tensor_copy(xh[:, 1, a], xc[0:96, 1, a]))
                    dve.wait_ge(*evacuated(("nT", n, q, 0)))
                    dve.wait_ge(x_high, X_OCTS.index(q) + 1)
                    for p in range(PAIRS):
                        dve.wait_ge(*filled(("t", "G", p)))
                    v.tensor_tensor(xl[:, :, a], xc[0:96, :, a], xh[:, :, a].bitcast(F), ALU.subtract).then_inc(x_split, 1)
                if n in "BCDEG":
                    dve.wait_ge(*evacuated(j))
                    v.tensor_copy(nrep[q][1].rearrange("p i (r k) -> p i r k", k=TOK),
                                  nT[1][0:97, Q8 * q:Q8 * q + Q8, 0:TOK].unsqueeze(2).broadcast_to([97, Q8, HG, TOK])).then_inc(*rep_ready[1].inc((n, q)))

            def key_blocks(n, q):
                j = ("k", n, q, 1)
                dve.wait_ge(*filled(j))
                mask = maskg[:, 1] if n == "C" else con("mask_k", 96)
                src = spaced(j) if n == "C" else bank(j)[0:96, 0:QT].rearrange("p (i k) -> p i k", k=TOK)
                v.tensor_tensor(kblk[q][1], src.unsqueeze(2).broadcast_to([96, Q8, HH, TOK]),
                                mask.unsqueeze(1).unsqueeze(3).broadcast_to([96, Q8, HH, TOK]), ALU.mult).then_inc(*freed(j))

            def value_blocks(n, p):
                j = ("v", n, p)
                dve.wait_ge(*filled(j))
                src = bank(j)[0:GR, 0:2 * D].rearrange("p (a r e) -> p a r e", r=HG, e=HD)
                m = con("mask_v", GR).rearrange("p (r e) -> p r e", e=HD).unsqueeze(1).broadcast_to([GR, 2 * NG, HG, HD])
                v.tensor_tensor(vblk[:, 2 * p:2 * p + 2].rearrange("p i g r e -> p (i g) r e")[:, :, :, 0:HD], src, m, ALU.mult).then_inc(*freed(j))

            def score_pair(n, p):
                j = ("s", n, p)
                dve.wait_ge(*filled(j))
                sc = bank(j)[0:ROWS, 0:H * TOK].rearrange("p (h k) -> p h k", k=TOK)
                link(v.tensor_reduce(mx[0:ROWS, p], sc, AX.X, ALU.max))
                v.tensor_tensor(ar[0:ROWS, p].rearrange("p (h k) -> p h k", k=TOK), sc,
                                mx[0:ROWS, p].unsqueeze(2).broadcast_to([ROWS, H, TOK]), ALU.subtract).then_inc(*freed(j))

            def column_softmax(q, x):
                first, m = DIRECT[x]
                j = ("e", "C", q, x)
                dve.wait_ge(*filled(j))
                sc = bank(j)[0:GR, 0:m * NG * TOK].rearrange("p (a k) -> p a k", k=TOK)
                top = mx[0:GR, P8 * q + x, 0:m * NG]
                link(v.tensor_reduce(top, sc, AX.X, ALU.max))
                v.tensor_tensor(ar[0:GR, P8 * q + x, 0:m * NG * TOK].rearrange("p (a k) -> p a k", k=TOK), sc,
                                top.unsqueeze(2).broadcast_to([GR, m * NG, TOK]), ALU.subtract).then_inc(*freed(j))

            def column_norm(q, x):
                first, m = DIRECT[x]
                dve.wait_ge(*eexp.at(("C", q, x)))
                e = ar[0:GR, P8 * q + x, 0:m * NG * TOK]
                tot, inv = rs[0:GR, P8 * q + x, 0:m * NG], rs[0:GR, P8 * q + x, H:H + m * NG]
                link(v.tensor_reduce(tot, e.rearrange("p (a k) -> p a k", k=TOK), AX.X, ALU.add))
                link(v.reciprocal(inv, tot))
                v.tensor_tensor(et[q][:, :, TOK * first:TOK * (first + m)].rearrange("p g (i k) -> p i g k", k=TOK),
                                e.rearrange("p (i g k) -> p i g k", g=NG, k=TOK),
                                inv.rearrange("p (i g) -> p i g", g=NG).unsqueeze(3).broadcast_to([GR, m, NG, TOK]),
                                ALU.mult).then_inc(*et_ready.inc(("C", q, x)))

            def poly(p):
                j, q = ("t", "E", p), p // P8
                dve.wait_ge(*filled(j))
                a = 2 * TOK * (p % P8)
                v.tensor_scalar(et[q][:, :, a:a + 2 * TOK].rearrange("p g (i k) -> p g i k", k=TOK),
                                bank(j)[0:GR, :].rearrange("p (g i k) -> p g i k", g=NG, k=GAP)[:, :, :, 0:TOK],
                                1.0, 0.0, ALU.add, ALU.max).then_inc(*freed(j))

            def add_bank(j, dst, other):
                dve.wait_ge(*filled(j))
                v.tensor_tensor(dst, bank(j)[0:ROWS, 0:2 * D].rearrange("p (c d) -> p c d", d=D), other, ALU.add).then_inc(*freed(j))

            def gating(n, j, rows, tiles, first, scratch):
                m, g0 = tiles * NE, first * NE
                dve.wait_ge(*filled(j))
                lg = bank(j)[0:rows, 0:m].rearrange("p (c e) -> p c e", e=NE)
                top, tot, inv = (grow[0:rows, x, first:first + tiles] for x in range(3))
                link(v.tensor_reduce(top, lg, AX.X, ALU.max))
                gate, e, rank, keep = (gsm[0:rows, x, g0:g0 + m] for x in range(4))
                gate3, e3 = (x.rearrange("p (c e) -> p c e", e=NE) for x in (gate, e))
                v.tensor_tensor(gate3, lg, top.unsqueeze(2).broadcast_to([rows, tiles, NE]), ALU.subtract).then_inc(*freed(j))
                dve.wait_ge(*evacuated(j))
                dve.wait_ge(*gate_exp.at(n))
                link(v.tensor_reduce(tot, e3, AX.X, ALU.add))
                link(v.reciprocal(inv, tot))
                link(v.tensor_tensor(gate3, e3, inv.unsqueeze(2).broadcast_to([rows, tiles, NE]), ALU.mult))
                gj = gate3.unsqueeze(2).broadcast_to([rows, tiles, NE, NE])
                gi = gate3.unsqueeze(3).broadcast_to([rows, tiles, NE, NE])
                above, equal = (scratch[0:rows, x * m * NE:(x + 1) * m * NE].rearrange("p (c i j) -> p c i j", i=NE, j=NE) for x in range(2))
                mark(v.tensor_tensor(above, gj, gi, ALU.is_gt))
                link(v.tensor_tensor(equal, gj, gi, ALU.is_equal))
                tri = con("tri", rows).rearrange("p (i j) -> p i j", j=NE).unsqueeze(1).broadcast_to([rows, tiles, NE, NE])
                link(v.tensor_tensor(equal, equal, tri, ALU.mult))
                link(v.tensor_tensor(above, above, equal, ALU.add))
                link(v.tensor_reduce(rank, above.rearrange("p c i j -> p (c i) j"), AX.X, ALU.add))
                link(v.tensor_scalar(keep, rank, TOPK - 0.5, None, ALU.is_lt))
                v.tensor_tensor(disp[0:rows, first:first + tiles].rearrange("p c e -> p (c e)"), keep, gate, ALU.mult).then_inc(*disp_ready.inc(n))

            for s in range(2):
                for t in (nT[s], oT[s]):
                    v.memset(t[0:96], 0.0).then_inc(zeroed, 1)
                    v.memset(t[96:97], 1.0).then_inc(zeroed, 1)
            dve.wait_ge(loaded["params"], 16)
            pos = prm("pos", ROWS)
            for i in range(2):
                mark(v.tensor_tensor(pos[GAP * i:GAP * i + 1], pos[GAP * i:GAP * i + 1], prm("cls")[GAP * i:GAP * i + 1], ALU.add))
            settle()
            dve.wait_ge(zeroed, ZEROED)

            for n, ph, q in SCHEDULE:
                kind = KIND.get(n)
                cs, ps = range(2 * q, 2 * q + 2), range(P8 * q, P8 * q + P8)
                if n == "tok":
                    for c in cs:
                        add_bank(("tok", c), h[0:ROWS, 2 * c:2 * c + 2], pos.unsqueeze(1).broadcast_to([ROWS, 2, D]))
                if ph == "T" and n != "F":
                    if (n, q) == ("H", 0):
                        link(v.memset(xc[0:96, :, T:TPAD], 0.0))
                        link(v.memset(xc[96:97], 1.0))
                    nt_copy(n, q)
                if (n, ph) == ("A", "F"):
                    if q == 0:
                        dve.wait_ge(loaded["consts"], 16)
                        link(v.tensor_copy(vblk[:, :, :, :, HD].rearrange("p i g r -> p (i g) r"),
                                           con("mask_v", GR).rearrange("p (r e) -> p r e", e=HD)[:, :, 0].unsqueeze(1).broadcast_to([GR, B * NG, HG])))
                        v.tensor_tensor(maskg[:], con("mask_k", 96).unsqueeze(1).broadcast_to([96, 2, HH]),
                                        prm("gk", 96).unsqueeze(2).broadcast_to([96, 2, HH]), ALU.mult).then_inc(maskg_ready, 1)
                        v.tensor_scalar(gqs[:], prm("gq", 96), SCALE, None, ALU.mult).then_inc(maskg_ready, 1)
                    for s in range(2):
                        j = ("q", n, q, s)
                        a = qT[s][:, QT * q:QT * q + QT]
                        dve.wait_ge(*elu_exp.at(("q", q, s)))
                        link(v.tensor_scalar(a, a, 1.0, None, ALU.min))
                        v.scalar_tensor_tensor(a, bank(j)[0:96, 0:QT], 0.0, a, ALU.max, ALU.add).then_inc(*freed(j))
                    vt = ar[0:ROWS, P8 * q:P8 * q + P8, 0:VW].rearrange("p c (h e) -> p c h e", e=HD + 1)
                    link(v.memset(vt[:, :, :, HD:HD + 1], 1.0))
                    for p in ps:
                        j = ("kv", p)
                        k = x2[q][0:ROWS, p % P8]
                        dve.wait_ge(*elu_exp.at(("k", p)))
                        mark(v.tensor_copy(vt[:, p % P8, :, 0:HD], bank(j)[0:ROWS, D:2 * D].rearrange("p (h e) -> p h e", e=HD)))
                        link(v.tensor_scalar(k, k, 1.0, None, ALU.min))
                        v.scalar_tensor_tensor(k, bank(j)[0:ROWS, 0:D], 0.0, k, ALU.max, ALU.add).then_inc(*freed(j))
                if ph == "M":
                    kvs = big[0:96, q, 0:P8 * 2 * VW].rearrange("p (c a x) -> p c a x", a=2, x=VW)
                    for c in cs:
                        for pr in range(2):
                            j = ("kvm", c, pr)
                            dve.wait_ge(*filled(j))
                            a = 2 * c - P8 * q
                            v.tensor_tensor(kvs[:, a:a + 2, pr].rearrange("p c (s x) -> p c s x", s=2),
                                            bank(j)[0:96, 0:2 * VW].rearrange("p (c s x) -> p c s x", c=2, s=2),
                                            con("mask_kv", 96).unsqueeze(1).unsqueeze(1).broadcast_to([96, 2, 2, VW // 2]), ALU.mult).then_inc(*freed(j))
                if ph == "O" and n != "C":
                    for c in cs:
                        j = ("o", n, c)
                        dve.wait_ge(*filled(j))
                        src = bank(j)[0:ROWS, 0:2 * VW].rearrange("p (c e) -> p c e", e=HD + 1)
                        inv = rs[0:ROWS, c]
                        link(v.reciprocal(inv, src[:, :, HD]))
                        a = 2 * c - P8 * q
                        o = x2[q][0:ROWS, a:a + 2]
                        v.tensor_tensor(o.rearrange("p c (h e) -> p (c h) e", e=HD), src[:, :, 0:HD],
                                        inv.unsqueeze(2).broadcast_to([ROWS, 2 * H, HD]), ALU.mult).then_inc(*freed(j))
                        if n == "G":
                            dve.wait_ge(*evacuated(j))
                            mark(v.tensor_tensor(yt[q][0:ROWS, a:a + 2], o, xn[0:ROWS, 2 * c:2 * c + 2], ALU.add))
                    if n == "G":
                        settle()
                if ph == "Z":
                    j = ("oT", n, q, 1)
                    dve.wait_ge(*filled(j))
                    v.tensor_copy(oT[1][0:96, Q8 * q:Q8 * q + Q8, 0:TOK], spaced(j)).then_inc(*freed(j))
                if ph == "G":
                    gating(q, ("gate", q), ROWS, P8, P8 * q, et_raw[:, q, 1:3].rearrange("p g t -> p (g t)"))
                if ph == "H":
                    j = ("dT", q)
                    dve.wait_ge(*filled(j))
                    v.tensor_copy(dispT[q].rearrange("p (i k) -> p i k", k=TOK),
                                  bank(j)[0:NE, :].rearrange("p (i k) -> p i k", k=GAP)[:, :, 0:TOK]).then_inc(*freed(j))
                    j = ("a", q)
                    dve.wait_ge(*filled(j))
                    dve.wait_ge(*evacuated(("dx", q)))
                    v.tensor_tensor(ad[q], bank(j)[:, 0:QT], dX[q], ALU.mult).then_inc(*freed(j))
                    dve.wait_ge(*evacuated(j))
                    v.tensor_copy(adrep[q].rearrange("p i (r k) -> p i r k", k=TOK),
                                  ad[q].rearrange("p (i k) -> p i k", k=TOK).unsqueeze(2).broadcast_to([128, Q8, HG, TOK])).then_inc(*adrep_ready.inc((n, q)))
                if ph == "K":
                    for p in ps:
                        dve.wait_ge(*filled(("qk", p)))
                        for a in range(2):
                            mark(v.bn_stats(stats_qk[0:ROWS, 2 * p + a], bank(("qk", p))[0:ROWS, D * a:D * a + D]))
                    settle()
                    for x in range(2 * P8 * q, 2 * P8 * q + 2 * P8):
                        ins = v.bn_aggr(mv_qk[0:ROWS, x], stats_qk[0:ROWS, x])
                        if x < 2 * P8 * (q + 1) - 1:
                            mark(ins)
                    ins.then_inc(*var_ready.inc(("Cqk", q)))
                if ph == "R":
                    dve.wait_ge(*rstd_ready.at(("Cqk", q)))
                    for p in ps:
                        j = ("qk", p)
                        for a, dst in enumerate((x2[q], yt[q])):
                            ins = v.tensor_scalar(dst[0:ROWS, p % P8], bank(j)[0:ROWS, D * a:D * a + D], mv_qk[0:ROWS, 2 * p + a, 0:1],
                                                  rstd_qk[0:ROWS, 2 * p + a:2 * p + a + 1], ALU.subtract, ALU.mult)
                            if a == 0:
                                mark(ins)
                        ins.then_inc(*freed(j))
                if ph == "F" and n != "A" or ph == "R":
                    key_blocks(n, q)
                if ph == "S":
                    if kind == SOFTMAX:
                        for p in ps:
                            score_pair(n, p)
                    elif kind == COLUMN:
                        for x in range(3):
                            column_softmax(q, x)
                        for x in range(3):
                            column_norm(q, x)
                if (n, ph) == ("E", "X"):
                    for p in ps:
                        poly(p)
                if ph == "W":
                    for p in ps:
                        value_blocks(n, p)
                if (n, ph) == ("F", "T"):
                    qf = [big[0:96, q, a * QT:(a + 1) * QT] for a in range(4)]
                    for s in range(2):
                        j = ("nT", "F", q, s)
                        dve.wait_ge(*filled(j))
                        v.tensor_scalar(qf[2 * s].rearrange("p (i k) -> p i k", k=TOK), spaced(j), 1.0 / ACT_SCALE, 127.0, ALU.mult, ALU.min).then_inc(*freed(j))
                    for s in range(2):
                        dve.wait_ge(*evacuated(("nT", "F", q, s)))
                        mark(v.tensor_scalar(qf[2 * s + 1], qf[2 * s], -128.0, ROUND, ALU.max, ALU.add))
                    settle()
                    for s in range(2):
                        v.tensor_scalar(nq[:, s, Q8 * q:Q8 * q + Q8, 0:TOK], qf[2 * s + 1].rearrange("p (i k) -> p i k", k=TOK),
                                        ROUND, None, ALU.subtract).then_inc(*nq_ready.inc((q, s)))
                if ph == "V":
                    if q == 1:
                        dve.wait_ge(mixed, 3)
                    for s in range(2):
                        j = ("f2", q, s)
                        dve.wait_ge(*filled(j))
                        bias = prm("b_fc2", 96)[:, s:s + 1] if q == 0 else b2s[:, s:s + 1]
                        v.tensor_scalar(oT[s][0:96, Q8 * q:Q8 * q + Q8, 0:TOK], bank(j)[0:96, 0:QT].rearrange("p (i k) -> p i k", k=TOK),
                                        bias, None, ALU.add).then_inc(*freed(j))
                if ph == "P" and n not in ("tok", "G2"):
                    if (n, ph) in (("C", "P"), ("D2", "P"), ("F", "P")):
                        dve.wait_ge(*h_plus.at(("D" if n == "D2" else n, q)))
                    for c in cs:
                        j = phase_jobs(n, ph, q)[c - 2 * q]
                        a = 2 * c - P8 * q
                        hc2, xn2, y2 = h[0:ROWS, 2 * c:2 * c + 2], xn[0:ROWS, 2 * c:2 * c + 2], yt[q][0:ROWS, a:a + 2]
                        if n == "F":
                            dve.wait_ge(*filled(j))
                            v.scalar_tensor_tensor(hc2, bank(j)[0:ROWS, 0:2 * D].rearrange("p (c d) -> p c d", d=D), EFF_SCALE, hc2,
                                                   ALU.mult, ALU.add).then_inc(*freed(j))
                        elif n == "D":
                            add_bank(j, y2, xn2)
                        else:
                            add_bank(j, hc2, hc2)
                if n == "G2":
                    dve.wait_ge(*xn_ready.at((n, q)))
                    for c in cs:
                        a = x2[q][0:ROWS, 2 * c - P8 * q:2 * c - P8 * q + 2]
                        link(v.tensor_tensor(a, a, prm("gamma", ROWS).unsqueeze(1).broadcast_to([ROWS, 2, D]), ALU.mult))
                        link(v.tensor_tensor(a, a, prm("beta", ROWS).unsqueeze(1).broadcast_to([ROWS, 2, D]), ALU.add))
                        v.tensor_tensor(h[0:ROWS, 2 * c:2 * c + 2], h[0:ROWS, 2 * c:2 * c + 2], a, ALU.add).then_inc(*g_done.inc(c))
                if (n, ph) in NEXT_LN:
                    moments(NEXT_LN[n, ph], q, n)

            gating("H", ("gate", "H"), 128, CT, 0, et_raw[:].rearrange("p q g t -> p (q g t)")[:, T:])
            for a in range(2):
                j = ("eT", a)
                dve.wait_ge(*filled(j))
                n = 512 if a == 0 else T - 512
                v.tensor_copy(eT[:, 512 * a:512 * a + n], bank(j)[0:NE, 0:n]).then_inc(*freed(j))
            dve.wait_ge(h_back, 32)

            def tiles(c):
                return (128, slice(2 * c, 2 * c + 2)) if c < 2 else (crow[-1], slice(CT - 1, CT))
            for c in range(3):
                j = ("eb", c)
                r, sl = tiles(c)
                dve.wait_ge(*filled(j))
                n = sl.stop - sl.start
                v.tensor_tensor(acc[0:r, sl], bank(j)[0:r, 0:n * D].rearrange("p (c d) -> p c d", d=D), hc[0:r, sl], ALU.add).then_inc(*freed(j))
                dve.wait_ge(*evacuated(j))

            def add_expert(i, b):
                for c in range(3):
                    r, sl = tiles(c)
                    dve.wait_ge(fc2_done, i * 6 + (3 * b + c + 1))
                    for t in range(sl.start, sl.stop):
                        at = i * 2 + (b + t * NE)
                        gate = disp[:].rearrange("p c e -> p (c e)")[0:r, bass.ds(at, 1)]
                        ins = v.scalar_tensor_tensor(acc[0:r, t], PS[4 + c][0:r, (t - sl.start) * D:(t - sl.start + 1) * D],
                                                     gate, acc[0:r, t], ALU.mult, ALU.add)
                    ins.then_inc(acc_done, 1)
            with dve.Fori(0, NE // 2) as i:
                for b in range(2):
                    if b == 1:
                        dve.wait_ge(acc_done, i * 6 + 3)
                    add_expert(i, b)
                dve.wait_ge(acc_done, i * 6 + 6)

        @block.tensor
        def _(pe):
            mm = nc.tensor.matmul
            done = [0]

            def start_job(j):
                assert order[done[0]] == j, (order[done[0]], j)
                done[0] += 1
                b, k = where[j]
                if k:
                    pe.wait_ge(bank_read[b], k)
                return PS[b]

            def end_job(j, last):
                last.then_inc(bank_filled[where[j][0]], 1)

            def wait_evacuated(*jobs):
                for j in jobs:
                    pe.wait_ge(*evacuated(j))

            def transposes(j, src, s):
                ps = start_job(j)
                for p in range(P8):
                    last = nc.tensor.transpose(ps[0:96, 128 * p:128 * p + ROWS], src[0:ROWS, p, 96 * s:96 * s + 96], ident[0:ROWS, 0:ROWS])
                end_job(j, last)

            def nt(k, q):
                return nT[k][0:96 + k, Q8 * q:Q8 * q + Q8, 0:TOK]

            def pair_cols(t, k, p):
                return t[k][0:96 + k].rearrange("p i k -> p (i k)")[:, 128 * p:128 * p + ROWS]

            def feature_job(j, seg, col, q, s, lora=False):
                ps = start_job(j)
                o = ps[0:96, 0:QT]
                for k in range(2):
                    last = mm(o, w(seg, k, col + 96 * s, 96), nt(k, q), start=(k == 0), stop=(k == 1 and not lora))
                if lora:
                    last = mm(o, bup[:, col + 96 * s:col + 96 * s + 96], ad[q], start=False, stop=True)
                end_job(j, last)

            def token_job(j, t, p, wk, n):
                ps = start_job(j)
                for k in range(2):
                    last = mm(ps[0:ROWS, 0:n], pair_cols(t, k, p), wk(k), start=(k == 0), stop=(k == 1))
                end_job(j, last)

            def value_job(n, p):
                j = ("v", n, p)
                q = p // P8
                ps = start_job(j)
                for i in range(2):
                    o = ps[0:GR, D * i:D * i + D]
                    im = 2 * (p % P8) + i
                    for k in range(2):
                        last = mm(o, nrep[q][k][0:96 + k, im], w(n + "_qkv", k, 2 * D, D), start=(k == 0), stop=(k == 1 and n != "B"))
                    if n == "B":
                        last = mm(o, adrep[q][:, im], bup[:, 2 * D:3 * D], start=False, stop=True)
                end_job(j, last)

            pe.wait_ge(loaded["tokw"], 16)
            for n, ph, q in SCHEDULE:
                kind = KIND.get(n)
                cs, ps8 = range(2 * q, 2 * q + 2), range(P8 * q, P8 * q + P8)
                if n == "tok":
                    for c in cs:
                        pe.wait_ge(loaded[f"patch{c}"], 16)
                        ps = start_job(("tok", c))
                        for i in range(2):
                            for k in range(PATCH_K):
                                last = mm(ps[0:ROWS, D * i:D * i + D], patch[q][:, 2 * c - P8 * q + i, k], tokw[:, k],
                                          start=(k == 0), stop=(k == PATCH_K - 1))
                        end_job(("tok", c), last)
                    if q == 0:
                        pe.wait_ge(loaded["consts"], 16)
                if ph == "T":
                    pe.wait_ge(*xn_ready.at((n, q)))
                    for s in range(2):
                        transposes(("nT", n, q, s), x2[q] if n in ("D", "D2") else xn[:, P8 * q:P8 * q + P8], s)
                    if n in LOADED_BY and q == 0:
                        pe.wait_ge(loaded[LOADED_BY[n]], 16)
                if (n, ph) == ("A", "F"):
                    wait_evacuated(("nT", n, q, 0), ("nT", n, q, 1))
                    for s in range(2):
                        feature_job(("q", n, q, s), "A_qkv", 0, q, s)
                    for p in ps8:
                        token_job(("kv", p), nT, p, lambda k: w("A_qkv", k, D, 2 * D), 2 * D)
                if ph == "M":
                    for c in cs:
                        wait_evacuated(("kv", 2 * c), ("kv", 2 * c + 1))
                        for pr in range(2):
                            ps = start_job(("kvm", c, pr))
                            r = slice(GAP * pr, GAP * pr + TOK)
                            for i in range(2):
                                for s in range(2):
                                    last = mm(ps[0:96, VW * i + VW // 2 * s:VW * i + VW // 2 * (s + 1)], x2[q][r, 2 * c - P8 * q + i, 96 * s:96 * s + 96],
                                              ar[r, 2 * c + i, VW // 2 * s:VW // 2 * (s + 1)], start=True, stop=True)
                            end_job(("kvm", c, pr), last)
                if (n, ph) == ("A", "O"):
                    wait_evacuated(("q", n, q, 0), ("q", n, q, 1))
                    kvs = big[0:96, q, 0:P8 * 2 * VW].rearrange("p (c a x) -> p c a x", a=2, x=VW)
                    for c in cs:
                        wait_evacuated(("kvm", c, 0), ("kvm", c, 1))
                        ps = start_job(("o", n, c))
                        for i in range(2):
                            for pr in range(2):
                                im = 2 * (2 * c + i) + pr
                                m = GAP if pr == 0 else TOK
                                for s in range(2):
                                    last = mm(ps[GAP * pr:GAP * pr + m, VW * i + VW // 2 * s:VW * i + VW // 2 * (s + 1)],
                                              qT[s][:, TOK * im:TOK * im + m], kvs[:, 2 * c - P8 * q + i, pr, VW // 2 * s:VW // 2 * (s + 1)],
                                              start=True, stop=True)
                        end_job(("o", n, c), last)
                if ph == "Z":
                    wait_evacuated(*[("o", n, c) for c in cs])
                    for s in range(2):
                        transposes(("oT", n, q, s), x2[q], s)
                if ph == "G":
                    wait_evacuated(("nT", n, q, 0), ("nT", n, q, 1))
                    ps = start_job(("gate", q))
                    for p in range(P8):
                        for k in range(2):
                            last = mm(ps[0:ROWS, NE * p:NE * p + NE], pair_cols(nT, k, P8 * q + p), w("B_gate", k), start=(k == 0), stop=(k == 1))
                    end_job(("gate", q), last)
                    ps = start_job(("a", q))
                    for k in range(2):
                        last = mm(ps[:, 0:QT], w("B_down", k), nt(k, q), start=(k == 0), stop=(k == 1))
                    end_job(("a", q), last)
                if ph == "H":
                    pe.wait_ge(*disp_ready.at(q))
                    ps = start_job(("dT", q))
                    for p in range(P8):
                        last = nc.tensor.transpose(ps[0:NE, 128 * p:128 * p + ROWS], disp[0:ROWS, P8 * q + p], ident[0:ROWS, 0:ROWS])
                    end_job(("dT", q), last)
                    if q == 0:
                        pe.wait_ge(loaded["bup"], 16)
                    wait_evacuated(("dT", q))
                    ps = start_job(("dx", q))
                    end_job(("dx", q), mm(ps[:, 0:QT], con("expand", NE), dispT[q], start=True, stop=True))
                if ph == "K":
                    wait_evacuated(("nT", n, q, 0), ("nT", n, q, 1))
                    for p in ps8:
                        token_job(("qk", p), nT, p, lambda k: w("C_qkv", k, 0, 2 * D), 2 * D)
                if ph == "R":
                    wait_evacuated(*[("qk", p) for p in ps8])
                    for s in range(2):
                        transposes(("k", n, q, s), yt[q], s)
                        transposes(("q", n, q, s), x2[q], s)
                if ph == "F" and n != "A":
                    wait_evacuated(("nT", n, q, 0), ("nT", n, q, 1))
                    if n == "B":
                        wait_evacuated(("a", q))
                    for s in range(2):
                        feature_job(("k", n, q, s), n + "_qkv", D, q, s, lora=(n == "B"))
                        feature_job(("q", n, q, s), n + "_qkv", 0, q, s, lora=(n == "B"))
                if ph == "S":
                    wait_evacuated(*[(a, n, q, s) for s in range(2) for a in "kq"])
                    if kind != COLUMN:
                        for p in ps8:
                            j = ("s", n, p)
                            ps = start_job(j)
                            for i in range(2):
                                im = 2 * p + i
                                m = GAP if i == 0 else TOK
                                for s in range(2):
                                    last = mm(ps[GAP * i:GAP * i + m, HH * TOK * s:HH * TOK * s + HH * TOK], qT[s][:, TOK * im:TOK * im + m],
                                              kblk[q][s][:, im % Q8].rearrange("p h k -> p (h k)"), start=True, stop=True)
                            end_job(j, last)
                    else:
                        for x, (first, m) in enumerate(DIRECT):
                            j = ("e", n, q, x)
                            ps = start_job(j)
                            for i in range(m):
                                im = first + i
                                for g in range(NG):
                                    c = (NG * i + g) * TOK
                                    last = mm(ps[0:GR, c:c + TOK], kblk[q][g // 2][:, im, HG * (g % 2):HG * (g % 2) + HG].rearrange("p h k -> p (h k)"),
                                              qT[g // 2][:, QT * q + TOK * im:QT * q + TOK * im + TOK], start=True, stop=True)
                            end_job(j, last)
                if ph == "W":
                    for s in range(2):
                        pe.wait_ge(*rep_ready[s].at((n, q)))
                    if n == "B":
                        pe.wait_ge(*adrep_ready.at((n, q)))
                    for p in ps8:
                        value_job(n, p)
                if ph == "X":
                    for p in ps8:
                        j = ("t", n, p)
                        pe.wait_ge(*(exp_ready.at((n, p)) if kind == SOFTMAX else evacuated(("s", n, p))))
                        ps = start_job(j)
                        for g in range(NG):
                            last = nc.tensor.transpose(ps[0:GR, 128 * g:128 * g + ROWS], ar[0:ROWS, p, GR * g:GR * g + GR], ident[0:ROWS, 0:ROWS])
                        end_job(j, last)
                if ph == "O" and n != "A":
                    wait_evacuated(*[("v", n, p) for p in ps8])
                    if kind != COLUMN:
                        wait_evacuated(*[("t", n, p) for p in ps8])
                    else:
                        pe.wait_ge(*et_ready.at((n, q, 2)))
                    gw = VW // NG
                    for c in cs:
                        ps = start_job(("o", n, c))
                        for i in range(2):
                            for g in range(NG):
                                for pr in range(2):
                                    im = 2 * (2 * c + i) + pr
                                    m = GAP if pr == 0 else TOK
                                    last = mm(ps[GAP * pr:GAP * pr + m, VW * i + gw * g:VW * i + gw * (g + 1)],
                                              et[q][:, g, TOK * (im - Q8 * q):TOK * (im - Q8 * q) + m],
                                              vblk[:, im, g].rearrange("p r e -> p (r e)"), start=True, stop=True)
                        end_job(("o", n, c), last)
                if ph in "UV":
                    if ph == "U":
                        wait_evacuated(("nT", n, q, 0), ("nT", n, q, 1))
                    for br in MLP_BR[q][:1] if ph == "U" else MLP_BR[q][1:]:
                        for m in range(MT):
                            j = ("f1", q, br, m)
                            ps = start_job(j)
                            r = min(96, KEEP[br])
                            for k in range(2 if br == 0 else 1):
                                last = mm(ps[:, 0:QT], w("D_fc1", k, 128 * m, 128)[0:r], nT[k][0:r, Q8 * q:Q8 * q + Q8, 0:TOK],
                                          start=(k == 0), stop=(k == 1 or br > 0))
                            end_job(j, last)
                if ph == "V":
                    wait_evacuated(*[("f1", q, br, m) for br in MLP_BR[q] for m in range(MT)])
                    pe.wait_ge(*((mixed, 3) if q else (loaded["fc2w"], 16)))
                    for s in range(2):
                        ps = start_job(("f2", q, s))
                        steps = []
                        for br in MLP_BR[q]:
                            n_c = min(96, KEEP[br] - 96 * s)
                            if n_c > 0:
                                wsrc = fc2s[br] if q else fc2w
                                steps += [(ps[0:n_c, 0:QT], wsrc[:, m, 96 * s:96 * s + n_c], hid[q][br][:, m]) for m in range(MT)]
                        steps = steps[0:MT - 1] + steps[MT:] + steps[MT - 1:MT]
                        for x, (o, a, b) in enumerate(steps):
                            last = mm(o, a, b, start=(x == 0), stop=(x == len(steps) - 1))
                        end_job(("f2", q, s), last)
                if (n, ph) == ("F", "P"):
                    if q == 0:
                        pe.wait_ge(wconv, 1)
                    pe.wait_ge(*nq_ready.at((q, 1)))
                    for c in cs:
                        ps = start_job(("int", c))
                        for i in range(2):
                            for k in range(2):
                                last = mm(ps[0:ROWS, D * i:D * i + D], nq[:, k].rearrange("p i k -> p (i k)")[:, 128 * (2 * c + i):128 * (2 * c + i) + ROWS],
                                          w8b[:, k], start=(k == 0), stop=(k == 1))
                        end_job(("int", c), last)
                elif (n, ph) == ("D2", "P"):
                    wait_evacuated(*[("f2", q, s) for s in range(2)])
                    for c in cs:
                        ps = start_job(("back", n, c))
                        for i in range(2):
                            for s in range(2):
                                last = nc.tensor.transpose(ps[0:ROWS, D * i + 96 * s:D * i + 96 * s + 96],
                                                           oT[s][0:96].rearrange("p i k -> p (i k)")[:, 128 * (2 * c + i):128 * (2 * c + i) + ROWS],
                                                           ident[0:96, 0:96])
                        end_job(("back", n, c), last)
                elif ph == "P" and n in KIND:
                    wait_evacuated(*[("oT", n, q, s) for s in range(2)])
                    if n == "D" and q == 1:
                        pe.wait_ge(mixed, 3)
                    for c in cs:
                        ps = start_job(("p", n, c))
                        for i in range(2):
                            for k in range(2):
                                wp = wps[0:96 + k, k] if n == "D" and q == 1 else w(n + "_proj", k)
                                last = mm(ps[0:ROWS, D * i:D * i + D], pair_cols(oT, k, 2 * c + i), wp, start=(k == 0), stop=(k == 1))
                        end_job(("p", n, c), last)
            wait_evacuated(*[("nT", "H", q, s) for q in range(2) for s in range(2)])
            ps = start_job(("gate", "H"))
            for c in range(CT):
                for k in range(2):
                    last = mm(ps[:, NE * c:NE * c + NE], xc[0:96 + k, k, 128 * c:128 * c + 128], w("H_gate", k), start=(k == 0), stop=(k == 1))
            end_job(("gate", "H"), last)
            def fc1(i, b, first=False):
                pe.wait_ge(w1_low, i * 2 + (b + 1))
                if first:
                    pe.wait_ge(x_split, 2)
                for m in range(MT):
                    for c in range(2):
                        x = 2 * m + c
                        if not (first and x < 4):
                            pe.wait_ge(gelu_done, i * 24 + (12 * b + x - 3))
                        ps = PS[x % 4]
                        parts = [(a[:, b, k, 128 * m:128 * m + 128], x[:, k, QT * c:QT * c + QT])
                                 for a, x in ((w1l, xh), (w1h, xl), (w1h, xh)) for k in range(2)]
                        for y, (a, x) in enumerate(parts):
                            last = mm(ps[:, 0:QT], a, x, start=(y == 0), stop=(y == len(parts) - 1))
                        last.then_inc(fc1_done, 1)

            wait_evacuated(*[max((j for j in order if where[j][0] == b), key=lambda j: where[j][1]) for b in range(4)])
            fc1(0, 0, first=True)
            pe.wait_ge(*disp_ready.at("H"))
            for a in range(2):
                ps = start_job(("eT", a))
                for c in range(4 * a, min(CT, 4 * a + 4)):
                    last = nc.tensor.transpose(ps[0:NE, 128 * (c - 4 * a):128 * (c - 4 * a) + 128], disp[:, c], ident[:, :])
                end_job(("eT", a), last)
            pe.wait_ge(loaded["b2e"], 16)
            wait_evacuated(("eT", 0), ("eT", 1))
            for c in range(3):
                ps = start_job(("eb", c))
                for i in range(2 if c < 2 else 1):
                    t = 2 * c + i
                    last = mm(ps[0:crow[t], D * i:D * i + D], eT[:, 128 * t:128 * t + crow[t]], b2t[:], start=True, stop=True)
                end_job(("eb", c), last)
            wait_evacuated(("eb", 0), ("eb", 1), ("eb", 2))

            def fc2(i, b, first=False):
                pe.wait_ge(w2_loaded[b], i * 16 + 16)
                pe.wait_ge(gelu_done, i * 24 + 12 * (b + 1))
                if not first:
                    pe.wait_ge(acc_done, i * 6 + 3 * b)
                for c in range(3):
                    for x in range(2 if c < 2 else 1):
                        t = 2 * c + x
                        for m in range(MT):
                            last = mm(PS[4 + c][0:crow[t], D * x:D * x + D], hbuf[b][:, m, 128 * t:128 * t + crow[t]], w2b[:, b, m],
                                      start=(m == 0), stop=(m == MT - 1))
                    last.then_inc(fc2_done, 1)

            fc1(0, 1)
            fc2(0, 0, first=True)
            with pe.Fori(1, NE // 2) as i:
                fc1(i, 0)
                fc2(i - 1, 1)
                fc1(i, 1)
                fc2(i, 0)
            fc2(NE // 2 - 1, 1)


def kernel(**inputs):
    import numpy as np
    import concourse.bacc as _bacc
    from concourse import mybir as _mybir
    from concourse.bass_utils import run_bass_kernel_spmd as _run

    a = {k: np.asarray(v) for k, v in inputs.items()}
    f32 = np.float32

    def ktiles(wm, bias=None):
        n = wm.shape[1]
        o = np.zeros((97, 2, n), f32)
        o[0:96] = wm.reshape(2, 96, n).transpose(1, 0, 2)
        if bias is not None:
            o[96, 1] = bias
        return o.reshape(97, 2 * n)

    c_qkv = np.concatenate([a["L1_attn_Wq"].T, a["L1_attn_Wk"].T, a["L1_attn_Wv"].T], 1)
    c_bias = np.concatenate([np.zeros(D, f32), a["L1_attn_bk"], a["L1_attn_bv"]])
    seg = {
        "A_qkv": ktiles(a["L0_attn_w_qkv"].T), "A_proj": ktiles(a["L0_attn_w_proj"].T, a["L0_attn_b_proj"]),
        "B_qkv": ktiles(a["L0_ffn_W_qkv"].T, a["L0_ffn_b_qkv"]), "B_gate": ktiles(a["L0_ffn_W_gate"].T, a["L0_ffn_b_gate"]),
        "B_down": ktiles(a["L0_ffn_A"].reshape(NE * RANK, D).T), "B_proj": ktiles(a["L0_ffn_W_proj"].T, a["L0_ffn_b_proj"]),
        "C_qkv": ktiles(c_qkv, c_bias), "C_proj": ktiles(a["L1_attn_Wo"].T, a["L1_attn_bo"]),
        "D_qkv": ktiles(a["L1_ffn_w_qkv"]), "D_proj": ktiles(a["L1_ffn_w_proj"], a["L1_ffn_b_proj"]),
        "D_fc1": ktiles(a["L1_ffn_w_fc1"]),
        "E_qkv": ktiles(a["L2_attn_w_qkv"]), "E_proj": ktiles(a["L2_attn_w_proj"], a["L2_attn_b_proj"]),
        "G_qkv": ktiles(a["L3_attn_w_qkv"], a["L3_attn_b_qkv"]), "H_gate": ktiles(a["L3_ffn_Wr"], a["L3_ffn_br"]),
    }
    wpack = np.concatenate([seg[n] for n, _ in SEGS], 1)

    P = 16
    x = a["x"].reshape(B, 6, P, 6, P, 3).transpose(0, 1, 3, 2, 4, 5).reshape(B, 36, PATCH_K, 128)
    patches = np.zeros((128, PAIRS, PATCH_K, ROWS), f32)
    xt = x.transpose(3, 0, 2, 1).reshape(128, PAIRS, 2, PATCH_K, 36)
    for i in range(2):
        patches[:, :, :, GAP * i + 1:GAP * i + TOK] = xt[:, :, i]

    c128 = np.concatenate([
        a["L0_tok_W"].reshape(PATCH_K, 128, D).transpose(1, 0, 2).reshape(128, -1),
        a["L0_ffn_B_lora"].transpose(0, 2, 1).reshape(NE * RANK, 3 * D),
        a["L1_ffn_w_fc2"].reshape(MT, 128, D).transpose(1, 0, 2).reshape(128, -1)], 1)

    def cput(o, table, name, val):
        at, width = table[name]
        val = np.asarray(val, f32)
        o[0:val.shape[0], at:at + width] = val.reshape(val.shape[0], width)

    consts = np.zeros((128, CCOLS), f32)
    feat = np.arange(HALF)
    cput(consts, CONST_AT, "ident", np.eye(128))
    cput(consts, CONST_AT, "mask_k", feat[:, None] // HD == np.arange(HH)[None])
    row_head = np.arange(GR) // TOK
    cput(consts, CONST_AT, "mask_v", np.arange(HG * HD)[None] // HD == row_head[:, None])
    cput(consts, CONST_AT, "mask_kv", feat[:, None] // HD == np.arange(HH * (HD + 1))[None] // (HD + 1))
    cput(consts, CONST_AT, "tri", np.broadcast_to(np.arange(NE)[None] < np.arange(NE)[:, None], (128, NE, NE)))
    cput(consts, CONST_AT, "expand", LORA_SCALE * (np.arange(NE)[:, None] == np.arange(128)[None] // RANK))
    for name, n in (("m96", D // 2), ("m64", D // 3)):
        m = np.zeros((97, 2, D), f32)
        r = np.arange(96)[:, None] + 96 * np.arange(2)[None]
        m[0:96] = (r < n)[:, :, None] & (np.arange(D) < n)
        m[96, 1] = np.arange(D) < n
        cput(consts, CONST_AT, name, m)
    for name, n in (("c96", D // 2), ("c64", D // 3)):
        cput(consts, CONST_AT, name, (np.arange(96)[:, None] + 96 * np.arange(2)[None]) < n)

    params = np.zeros((128, PCOLS), f32)
    for name, src in (("n1l_g", "L1_ffn_n1l_g"), ("n1l_b", "L1_ffn_n1l_b"), ("n1s_g", "L1_ffn_n1s_g"), ("n1s_b", "L1_ffn_n1s_b"),
                      ("n2l_g", "L1_ffn_n2l_g"), ("n2l_b", "L1_ffn_n2l_b"), ("n2s_g", "L1_ffn_n2s_g"), ("n2s_b", "L1_ffn_n2s_b"),
                      ("gq", "L1_attn_gq"), ("gk", "L1_attn_gk"), ("b_fc2", "L1_ffn_b_fc2")):
        cput(params, PARAM_AT, name, a[src].reshape(2, 96).T)
    cput(params, PARAM_AT, "b_fc1", a["L1_ffn_b_fc1"].reshape(MT, 128).T)
    cput(params, PARAM_AT, "b1", a["L3_ffn_b1"].reshape(NE, MT, 128).transpose(2, 0, 1))
    for name, src in (("gumbel", "L1_ffn_gumbel_weights"), ("bias_q", "L2_ffn_bias"), ("gamma", "L3_attn_ln_gamma"), ("beta", "L3_attn_ln_beta")):
        cput(params, PARAM_AT, name, np.broadcast_to(a[src], (128, a[src].size)))
    pos = np.zeros((128, D), f32)
    cls = np.zeros((128, D), f32)
    for i in range(2):
        pos[GAP * i:GAP * i + TOK] = a["L0_tok_pos_emb"][0]
        cls[GAP * i] = a["L0_tok_class_emb"][0, 0]
    cput(params, PARAM_AT, "pos", pos)
    cput(params, PARAM_AT, "cls", cls)

    arrays = {
        "patches": patches, "wpack": wpack, "c128": c128, "consts": consts, "params": params,
        "w8": np.ascontiguousarray(a["L2_ffn_weight_t"].reshape(2, 96, D).transpose(1, 0, 2)).reshape(96, 2 * D).view(np.int32), "b2e": a["L3_ffn_b2"],
        "w1": a["L3_ffn_W1"].reshape(NE, 2, 96, HID).transpose(0, 2, 1, 3),
        "w2": a["L3_ffn_W2"].reshape(NE, MT, 128, D).transpose(0, 2, 1, 3),
    }
    arrays = {f"in_{k}": np.ascontiguousarray(v) for k, v in arrays.items()}
    nc = _bacc.Bacc("TRN2", target_bir_lowering=False, num_devices=1)
    args = [nc.dram_tensor(k, v.shape, _mybir.dt.from_np(v.dtype), kind="ExternalInput").ap() for k, v in arrays.items()]
    args.append(nc.dram_tensor("out_0", (T, D), _mybir.dt.float32, kind="ExternalOutput").ap())
    build_tower(nc, *args)
    r = _run(nc, [arrays], core_ids=[0])
    return r.results[0]["out_0"].reshape(B, TOK, D)
```

```python
import concourse.bass as bass
from concourse import mybir
from contextlib import ExitStack

B, TOK, D, H = 16, 37, 192, 12
HD = D // H
PAIRS = B // 2
GAP = 64
ROWS = GAP + TOK
T = B * TOK
HALF = D // 2
HH = H // 2
NG, HG = 4, 3
GR = HG * TOK
Q8 = 8
QT = Q8 * TOK
PATCH_K = 6
HID, MT = 768, 6
NE, RANK, TOPK = 8, 16, 2
CT = 5
TPAD = CT * 128
EPS = 1e-5
LORA_SCALE = 2.0
ACT_SCALE, EFF_SCALE = 0.02, 0.02 * 0.01
ROUND = 1.5 * 2.0 ** 23
SCALE = HD ** -0.5

SEGS = [("A_qkv", 3 * D), ("A_proj", D), ("B_qkv", 3 * D), ("B_gate", NE), ("B_down", 128), ("B_proj", D),
        ("C_qkv", 3 * D), ("C_proj", D), ("D_qkv", 3 * D), ("D_proj", D), ("D_fc1", HID),
        ("E_qkv", 3 * D), ("E_proj", D), ("G_qkv", 3 * D)]
SEG_DRAM, WCOLS = {}, 0
for _n, _w in SEGS:
    SEG_DRAM[_n] = WCOLS
    WCOLS += 2 * _w
LATE = SEG_DRAM["E_qkv"]
SEG_AT = {_n: (SEG_DRAM[_n] % LATE, _w) for _n, _w in SEGS}
W1_AT = WCOLS - LATE
W2_AT = W1_AT + 2 * 2 * HID
WT_COLS = W2_AT + 2 * MT * D
LOADS = [("A_qkv", "A_proj"), ("B_qkv", "B_proj"), ("C_qkv", "C_proj"), ("D_qkv", "D_fc1"), ("E_qkv", "G_qkv")]

CONSTS = [("ident", 128), ("mask_k", HH), ("mask_v", HG * HD), ("mask_kv", HH * (HD + 1)),
          ("tri", NE * NE), ("expand", 128), ("m96", 2 * D), ("m64", 2 * D), ("c96", 2), ("c64", 2)]
CONST_AT, CCOLS = {}, 0
for _n, _w in CONSTS:
    CONST_AT[_n] = (CCOLS, _w)
    CCOLS += _w

PARAMS = [("n1l_g", 2), ("n1l_b", 2), ("n1s_g", 2), ("n1s_b", 2), ("n2l_g", 2), ("n2l_b", 2), ("n2s_g", 2),
          ("n2s_b", 2), ("gq", 2), ("gk", 2), ("b_fc1", MT), ("b_fc2", 2), ("b1", NE * MT), ("gumbel", 3), ("h_gate", 3 * NE),
          ("bias_q", D), ("gamma", D), ("beta", D), ("pos", D), ("cls", D)]
PARAM_AT, PCOLS = {}, 0
for _n, _w in PARAMS:
    PARAM_AT[_n] = (PCOLS, _w)
    PCOLS += _w

LINEAR, SOFTMAX, COLUMN, POLY = "linear", "softmax", "column", "poly"
ATT = [("A", LINEAR), ("B", SOFTMAX), ("C", COLUMN), ("D", SOFTMAX), ("E", POLY), ("G", SOFTMAX)]
KIND = dict(ATT)
P8 = PAIRS // 2
VW = H * (HD + 1)
TAIL = 8
ZEROED = 9
LOADED_BY = {"A": "A_qkv", "B": "B_qkv", "C": "C_qkv", "D": "D_qkv", "E": "E_qkv"}
MLP_BR = [(0,), (0, 1, 2)]
KEEP = [D, D // 2, D // 3]

PHASES = ([("tok", "P")]
          + [("A", p) for p in ("T", "F", "M", "O", "Z", "P")]
          + [("B", p) for p in ("T", "G", "H", "F", "S", "W", "X", "O", "Z", "P")]
          + [("C", p) for p in ("T", "K", "R", "S", "W", "X", "N", "O", "Z", "P")]
          + [("D", p) for p in ("T", "F", "S", "W", "X", "O", "Z", "P")] + [("D2", p) for p in ("T", "U", "V", "P")]
          + [("E", p) for p in ("T", "F", "S", "W", "X", "O", "Z", "P")]
          + [("F", p) for p in ("T", "P")]
          + [("G", p) for p in ("T", "F", "S", "W", "X", "O")] + [("G2", "P")]
          + [("H", "T")])
ORDER = ("010000101011011010101100100001010101010100101001101101110010100110110101010110010010101001101101101010010101011011")
SCHEDULE, _at = [], [0, 0]
for _q in map(int, ORDER):
    SCHEDULE.append(PHASES[_at[_q]] + (_q,))
    _at[_q] += 1
assert _at == [len(PHASES)] * 2
X_OCTS = [_q for _n, _p, _q in SCHEDULE if _n == "H"]
LAST_GX = max(i for i, _s in enumerate(SCHEDULE) if _s[:2] == ("G", "X"))
LAST_GO = max(i for i, _s in enumerate(SCHEDULE) if _s[:2] == ("G", "O"))
LAST_G2 = max(i for i, _s in enumerate(SCHEDULE) if _s[0] == "G2")
FIRST_H = min(i for i, _s in enumerate(SCHEDULE) if _s[0] == "H")
NEXT_LN = {("tok", "P"): "A", ("A", "P"): "B", ("B", "P"): "C", ("C", "P"): "D", ("D", "P"): "D2", ("D2", "P"): "E",
           ("E", "P"): "F", ("F", "P"): "G", ("G", "O"): "G2", ("G2", "P"): "H"}


def phase_jobs(n, ph, q):
    cs, ps = range(2 * q, 2 * q + 2), range(P8 * q, P8 * q + P8)
    kind = KIND.get(n)
    if n == "tok":
        return [("tok", c) for c in cs]
    if ph == "T":
        return [("nT", n, q, s) for s in range(2)]
    if (n, ph) == ("A", "F"):
        return [("q", n, q, s) for s in range(2)] + [("kv", p) for p in ps]
    if (n, ph) == ("A", "M"):
        return [("kvm", c, par) for c in cs for par in range(2)]
    if ph == "Z":
        return [("oT", n, q, s) for s in range(2)]
    if ph == "G":
        return [("gate", q), ("a", q)]
    if ph == "H":
        return [("dT", q), ("dx", q)]
    if ph in ("F", "R"):
        return [(k, n, q, s) for s in range(2) for k in ("k", "q")]
    if ph == "K":
        return [("qk", p) for p in ps]
    if ph == "S":
        return [("s", n, p) for p in ps]
    if ph == "W":
        return [("v", n, p) for p in ps]
    if ph == "X":
        return [("t", n, p) for p in ps]
    if ph == "O":
        return [("o", n, c) for c in cs]
    if ph == "U":
        return [("f1", q, br, m) for br in MLP_BR[q] for m in range(MT)]
    if ph == "V":
        return [("f2", q, s) for s in (1, 0)]
    if (n, ph) == ("F", "P"):
        return [("int", c) for c in cs]
    if ph == "N" or n == "G2":
        return []
    if (n, ph) == ("D2", "P"):
        return [("back", n, c) for c in cs]
    assert ph == "P", (n, ph)
    return [("p", n, c) for c in cs]


def job_order():
    jobs = [j for step in SCHEDULE for j in phase_jobs(*step)]
    return jobs + [("gate", "H"), ("eT", 0), ("eT", 1)] + [("eb", c) for c in range(3)]


class Signal:

    def __init__(self, sem, events):
        self.sem, self.index, self.seen = sem, {e: i for i, e in enumerate(events)}, 0

    def inc(self, event):
        assert self.index[event] == self.seen, (event, self.seen)
        self.seen += 1
        return self.sem, 1

    def at(self, event):
        return self.sem, self.index[event] + 1


def build_tower(nc, patches, wpack, c128, consts, params, w8, b2e, w1, w2, out):
    F, FB = mybir.dt.float32, mybir.dt.bfloat16
    ALU, ACT, AX = mybir.AluOpType, mybir.ActivationFunctionType, mybir.AxisListType
    ctx = ExitStack()
    with ctx:
        def sb(name, shape, dt=F):
            return ctx.enter_context(nc.sbuf_tensor(name, shape, dt))

        def sem(name):
            return ctx.enter_context(nc.semaphore(name))

        wt = sb("weights", [128, WT_COLS])
        cst = sb("constants", [128, CCOLS])
        par = sb("parameters", [128, PCOLS])
        tokw = sb("tok_w", [128, PATCH_K, D])
        bup = sb("lora_up", [128, 3 * D])
        fc2w = sb("fc2_w", [128, MT, D])
        h = sb("h", [128, PAIRS, D])
        xn = sb("xn", [128, PAIRS, D])
        xy = sb("x2_y", [128, 2, 2, P8, D])
        x2 = [xy[:, q, 0] for q in range(2)]
        yt = [xy[:, q, 1] for q in range(2)]
        adrep = [xy[:, q].rearrange("p a c d -> p (a c d)")[:, 0:Q8 * GR].rearrange("p (i c) -> p i c", c=GR) for q in range(2)]
        nT = [sb(f"nT{s}", [97, B, GAP]) for s in range(2)]
        oT = [sb(f"oT{s}", [97, B, GAP]) for s in range(2)]
        qT = [sb(f"qT{s}", [96, T]) for s in range(2)]
        with ExitStack() as attention_only:
            rep_raw = attention_only.enter_context(nc.sbuf_tensor("rep", [128, 2, 2 * Q8 * GR], F))
            ar = attention_only.enter_context(nc.sbuf_tensor("arena_e", [128, PAIRS, H * TOK], F))
        w1h, w1l = (sb(n, [128, 2, 2, HID], mybir.dt.float32r) for n in ("w1_high", "w1_low"))
        xl = sb("x_low", [128, 2, T], mybir.dt.float32r)
        nrep = [[rep_raw[0:97, q, s * Q8 * GR:(s + 1) * Q8 * GR].rearrange("p (i c) -> p i c", c=GR) for s in range(2)] for q in range(2)]
        big = sb("arena_k", [128, 2, HH * T])
        bigf = big[:].rearrange("p q x -> p (q x)")
        kblk = [[big[0:96, q, s * HH * QT:(s + 1) * HH * QT].rearrange("p (i h k) -> p i h k", h=HH, k=TOK) for s in range(2)] for q in range(2)]
        patch = [big[:, q, 0:P8 * PATCH_K * ROWS].rearrange("p (c k t) -> p c k t", k=PATCH_K, t=ROWS) for q in range(2)]
        hid = [[big[:, q, b * MT * QT:(b + 1) * MT * QT].rearrange("p (m t) -> p m t", t=QT) for b in range(2)]
               + [rep_raw[:, q, :].rearrange("p (m t) -> p m t", t=QT)] for q in range(2)]
        hbuf = [bigf[:, b * MT * T:(b + 1) * MT * T].rearrange("p (m t) -> p m t", t=T) for b in range(2)]
        vblk_raw = sb("vblk", [128, B * VW])
        vblk = vblk_raw[0:GR].rearrange("p (i g r e) -> p i g r e", g=NG, r=HG, e=HD + 1)
        et_raw = sb("et", [128, 2, NG, QT])
        et = [et_raw[0:GR, q] for q in range(2)]
        ad, dX, dispT = ([et_raw[0:r, q, x] for q in range(2)] for r, x in ((128, 0), (128, 1), (NE, 2)))
        eT = et_raw[0:NE].rearrange("p q g t -> p (q g t)")
        ones = sb("ones", [1, 128])
        disp = sb("disp", [128, PAIRS, NE])
        gsm = sb("gates", [128, 4, PAIRS * NE])
        stats = sb("stats", [128, PAIRS, 6])
        mv = sb("mean_var", [128, PAIRS, 2])
        rstd = sb("rstd", [128, PAIRS])
        nmr = sb("minus_mean_rstd", [128, PAIRS])
        rst2 = sb("rstd_second", [128, PAIRS])
        rtmp = sb("rstd_tmp", [128, 2 * PAIRS])
        stats_qk = sb("stats_qk", [128, 2 * PAIRS, 6])
        mv_qk = sb("mean_var_qk", [128, 2 * PAIRS, 2])
        rstd_qk = sb("rstd_qk", [128, 2 * PAIRS])
        mhalf = sb("minus_half", [128, 2 * PAIRS])
        mx = sb("score_max", [128, 8, H])
        rs = sb("row_recip", [128, 8, 2 * H])
        grow = sb("gate_rows", [128, 3, PAIRS])
        gqs = sb("gain_q_scaled", [96, 2])
        maskg = sb("mask_k_gain", [96, 2, HH])
        wps = sb("proj_small", [97, 2, D])
        b2s = sb("b_fc2_small", [96, 2])
        gcol = sb("gumbel_cols", [96, 2, 2])
        w8i = sb("w8_int", [96, 2 * D // 4], mybir.dt.int32)
        w8b = sb("w8_bf16", [96, 2, D], FB)
        nq = sb("n_quant", [96, 2, B, GAP], FB)
        b2t = sb("expert_b2", [NE, D])
        b1cur = sb("expert_b1", [128, 2, MT])
        xh = sb("x_high", [128, 2, T], mybir.dt.float32r)

        PS = [ctx.enter_context(nc.psum_tensor(f"bank{b}", [128, 512], F)) for b in range(8)]

        def w(name, k, a=0, n=None):
            at, width = SEG_AT[name]
            n = width if n is None else n
            return wt[0:96 + k, at + k * width + a:at + k * width + a + n]

        def con(name, rows=128):
            at, width = CONST_AT[name]
            return cst[0:rows, at:at + width]

        def prm(name, rows=128):
            at, width = PARAM_AT[name]
            return par[0:rows, at:at + width]

        ident = con("ident")

        order = job_order()
        where, _in_bank = {}, [0] * 8
        for i, j in enumerate(order):
            b = i % 8 if i < len(order) - TAIL else 4 + (i - len(order) + TAIL) % 4
            where[j] = (b, _in_bank[b])
            _in_bank[b] += 1
        bank_filled = [sem(f"bank{b}_filled") for b in range(8)]
        bank_read = [sem(f"bank{b}_read") for b in range(8)]

        def bank(j):
            return PS[where[j][0]]

        def filled(j):
            b, k = where[j]
            return bank_filled[b], k + 1

        def evacuated(j):
            b, k = where[j]
            return bank_read[b], k + 1

        def updated(name, c):
            job = {"tok": ("tok", c), "F": ("int", c), "D2": ("back", "D2", c), "G": ("back", "G", c)}.get(name, ("p", name, c))
            return g_done.at(c) if name == "G2" else evacuated(job)

        def freed(j):
            return bank_read[where[j][0]], 1

        loaded = {n: sem(f"loaded_{n}") for n in ["consts", "params", "tokw", "bup", "fc2w", "w8", "b2e"]
                  + [f"patch{c}" for c in range(PAIRS // 2)] + [a for a, _ in LOADS]}
        lns = [e for n, ph, q in SCHEDULE for e in ([(NEXT_LN[n, ph], q)] if (n, ph) in NEXT_LN
                                                      else [("Cqk", q)] if ph == "K" else [])]
        norms = [(n, q) for n, ph, q in SCHEDULE if ph == "T" or n == "G2"]

        def steps(*which):
            return [(n, q) for n, ph, q in SCHEDULE if (n, ph) in which]
        g_done = Signal(sem("g_done"), [c for _, q in steps(("G2", "P")) for c in (2 * q, 2 * q + 1)])
        var_ready = Signal(sem("var_ready"), lns)
        rstd_ready = Signal(sem("rstd_ready"), lns)
        xn_ready = Signal(sem("xn_ready"), norms)
        rep_ready = [Signal(sem(f"rep_ready{s}"), steps(*[(n, "T") for n in "BCDEG"])) for s in range(2)]
        adrep_ready = Signal(sem("adrep_ready"), steps(("B", "H")))
        h_plus = Signal(sem("h_plus"), steps(("C", "T"), ("D", "P"), ("F", "T"), ("G", "T")))
        smax = [(n, p) for n, q in steps(*[(n, "S") for n in "BDG"]) for p in range(P8 * q, P8 * q + P8)]
        exp_ready = Signal(sem("exp_ready"), smax)
        column = [p for _, q in steps(("C", "X")) for p in range(P8 * q, P8 * q + P8)]
        col_exp = Signal(sem("col_exp"), column)
        et_ready = Signal(sem("et_ready"), column)
        elu_exp = Signal(sem("elu_exp"), [e for _, q in steps(("A", "F")) for e in [("q", q, s) for s in range(2)]
                                          + [("k", p) for p in range(P8 * q, P8 * q + P8)]])
        zeroed = sem("zeroed")
        maskg_ready = sem("maskg_ready")
        mixed = sem("mixed")
        hid_mixed = sem("hid_mixed")
        gates = [q for _, q in steps(("B", "G"))] + ["H"]
        gate_exp = Signal(sem("gate_exp"), gates)
        disp_ready = Signal(sem("disp_ready"), gates)
        wconv = sem("w8_converted")
        nq_ready = Signal(sem("nq_ready"), [(q, s) for _, q in steps(("F", "T")) for s in range(2)])
        dve_chain = sem("dve_chain")
        act_chain = sem("act_chain")
        pool_chain = sem("pool_chain")
        b1_ready = sem("b1_ready")
        fc1_done, gelu_done = sem("fc1_done"), sem("gelu_done")
        fc2_done, acc_done = sem("fc2_done"), sem("acc_done")
        w1_high, w1_low = sem("w1_high"), sem("w1_low")
        xc_pads = sem("xc_pads")
        x_high, x_split = sem("x_high"), sem("x_split")
        w1_loaded = [sem(f"w1_loaded{b}") for b in range(2)]
        w2_loaded = [sem(f"w2_loaded{b}") for b in range(2)]
        h_stored, h_back, stored = sem("h_stored"), sem("h_back"), sem("stored")

        w1b = wt[:, W1_AT:W2_AT].rearrange("p (b k n) -> p b k n", b=2, k=2)
        w2b = wt[:, W2_AT:WT_COLS].rearrange("p (b m d) -> p b m d", b=2, m=MT)
        ec = vblk_raw[:, 0:2 * TPAD + 2 * CT * D]
        xc = ec[:, 0:2 * TPAD].rearrange("p (s t) -> p s t", s=2)
        hc = ec[:, 2 * TPAD:2 * TPAD + CT * D].rearrange("p (c d) -> p c d", d=D)
        acc = ec[:, 2 * TPAD + CT * D:2 * TPAD + 2 * CT * D].rearrange("p (c d) -> p c d", d=D)
        scratch = nc.dram_tensor("h_compact", (T, D), F).ap()
        crow = [min(128, T - 128 * c) for c in range(CT)]

        block = ctx.enter_context(nc.Block())

        def spaced(j, rows=96):
            return bank(j)[0:rows, :].rearrange("p (i k) -> p i k", k=GAP)[:, :, 0:TOK]

        @block.sync
        def _(sp):
            sp.dma_start(tokw[:], c128[:, 0:PATCH_K * D].rearrange("p (k d) -> p k d", d=D)).then_inc(loaded["tokw"], 16)
            for c in range(PAIRS // 2):
                a = 2 * c % P8
                sp.dma_start(patch[2 * c // P8][:, a:a + 2], patches[:, 2 * c:2 * c + 2]).then_inc(loaded[f"patch{c}"], 16)
            sp.dma_start(par[:], params).then_inc(loaded["params"], 16)
            sp.dma_start(w8i[:], w8).then_inc(loaded["w8"], 16)
            sp.dma_start(b2t[:], b2e).then_inc(loaded["b2e"], 16)
            for first, last in LOADS:
                a, z = SEG_AT[first][0], SEG_AT[last][0] + 2 * SEG_AT[last][1]
                late = first == "E_qkv"
                if late:
                    for c in (1, 3):
                        sp.wait_ge(*updated("B", c))
                d = SEG_DRAM[first]
                sp.dma_start(wt[0:97, a:z], wpack[:, d:d + z - a]).then_inc(loaded[first], 16)
                if first == "A_qkv":
                    sp.dma_start(bup[:], c128[:, PATCH_K * D:PATCH_K * D + 3 * D]).then_inc(loaded["bup"], 16)
                if first == "C_qkv":
                    sp.dma_start(fc2w[:], c128[:, PATCH_K * D + 3 * D:].rearrange("p (m d) -> p m d", d=D)).then_inc(loaded["fc2w"], 16)
            for c in (1, 3):
                sp.wait_ge(*updated("D2", c))
            for b in range(2):
                sp.dma_start(w1b[:, b], w1[b]).then_inc(w1_loaded[b], 16)
                sp.dma_start(w2b[:, b], w2[b]).then_inc(w2_loaded[b], 16)
            for c in (1, 3):
                sp.wait_ge(*updated("G2", c))
            hd = scratch.rearrange("(p i k) d -> i k p d", i=2, k=TOK)
            for i in range(2):
                sp.dma_start(hd[i], h[GAP * i:GAP * i + TOK]).then_inc(h_stored, 16)
            sp.wait_ge(h_stored, 32)
            sp.dma_start(hc[:, 0:CT - 1], scratch[0:128 * (CT - 1)].rearrange("(c p) d -> p c d", p=128)).then_inc(h_back, 16)
            sp.dma_start(hc[0:crow[-1], CT - 1], scratch[128 * (CT - 1):T]).then_inc(h_back, 16)
            with sp.Fori(0, NE // 2 - 1) as i:
                for b in range(2):
                    sp.wait_ge(w1_low, i * 2 + (b + 1))
                    sp.dma_start(w1b[:, b], w1[i * 2 + (2 + b)]).then_inc(w1_loaded[b], 16)
            sp.wait_ge(acc_done, 3 * NE)
            sp.dma_start(out[0:128 * (CT - 1)].rearrange("(c p) d -> p c d", p=128), acc[:, 0:CT - 1]).then_inc(stored, 16)
            sp.dma_start(out[128 * (CT - 1):T], acc[0:crow[-1], CT - 1]).then_inc(stored, 16)
            sp.wait_ge(stored, 32)

        @block.gpsimd
        def _(pool):
            g = nc.gpsimd
            links = [0]

            def link(ins):
                links[0] += 1
                ins.then_inc(pool_chain, 1)
                pool.wait_ge(pool_chain, links[0])

            link(g.memset(mhalf[:], -0.5))
            link(g.memset(nq[:], 0.0))

            def root(n, q):
                pool.wait_ge(*var_ready.at((n, q)))
                a = slice(P8 * q, P8 * q + P8)
                link(g.tensor_tensor(rstd[0:ROWS, a], rtmp[0:ROWS, a], mhalf[0:ROWS, a], ALU.pow))
                if n == "D":
                    link(g.tensor_tensor(rtmp[0:ROWS, a], mv[0:ROWS, a, 1], rstd[0:ROWS, a], ALU.mult))
                    link(g.tensor_tensor(rtmp[0:ROWS, a], rtmp[0:ROWS, a], rstd[0:ROWS, a], ALU.mult))
                    link(g.tensor_scalar(rtmp[0:ROWS, a], rtmp[0:ROWS, a], EPS, None, ALU.add))
                    link(g.tensor_tensor(rst2[0:ROWS, a], rtmp[0:ROWS, a], mhalf[0:ROWS, a], ALU.pow))
                g.tensor_tensor(nmr[0:ROWS, a], nmr[0:ROWS, a], rstd[0:ROWS, a], ALU.mult).then_inc(*rstd_ready.inc((n, q)))
                pool.wait_ge(*rstd_ready.at((n, q)))

            def root_qk(q):
                pool.wait_ge(*var_ready.at(("Cqk", q)))
                a = slice(2 * P8 * q, 2 * P8 * q + 2 * P8)
                link(g.tensor_scalar(rstd_qk[0:ROWS, a], mv_qk[0:ROWS, a, 1], EPS, None, ALU.add))
                g.tensor_tensor(rstd_qk[0:ROWS, a], rstd_qk[0:ROWS, a], mhalf[0:ROWS, a], ALU.pow).then_inc(*rstd_ready.inc(("Cqk", q)))
                pool.wait_ge(*rstd_ready.at(("Cqk", q)))

            def add_to_h(n, q, src):
                a = slice(P8 * q, P8 * q + P8)
                g.tensor_tensor(h[0:ROWS, a], h[0:ROWS, a], src, ALU.add).then_inc(*h_plus.inc((n, q)))
                pool.wait_ge(*h_plus.at((n, q)))

            def mix_small():
                for name in ("params", "consts", "D_qkv"):
                    pool.wait_ge(loaded[name], 16)
                gw, m96, m64 = prm("gumbel"), con("m96", 97), con("m64", 97)
                gm = m96.rearrange("p (k d) -> p k d", k=2)
                link(g.tensor_scalar(m96, m96, gw[0:97, 1:2], gw[0:97, 0:1], ALU.mult, ALU.add))
                link(g.tensor_scalar(m64, m64, gw[0:97, 2:3], None, ALU.mult))
                link(g.tensor_tensor(m96, m96, m64, ALU.add))
                for k in range(2):
                    link(g.tensor_tensor(wps[0:96 + k, k], w("D_proj", k), gm[0:96 + k, k], ALU.mult))
                link(g.tensor_scalar(gcol[:, 0], con("c96", 96), gw[0:96, 1:2], gw[0:96, 0:1], ALU.mult, ALU.add))
                link(g.tensor_scalar(gcol[:, 1], con("c64", 96), gw[0:96, 2:3], None, ALU.mult))
                link(g.tensor_tensor(gcol[:, 0], gcol[:, 0], gcol[:, 1], ALU.add))
                g.tensor_tensor(b2s[:], prm("b_fc2", 96), gcol[:, 0], ALU.mult).then_inc(mixed, 1)
                pool.wait_ge(mixed, 1)

            def split_low(e, b):
                pool.wait_ge(w1_high, e + 1)
                g.tensor_tensor(w1l[:, b], w1b[:, b], w1h[:, b].bitcast(F), ALU.subtract).then_inc(w1_low, 1)
                pool.wait_ge(w1_low, e + 1)

            for step, (n, ph, q) in enumerate(SCHEDULE):
                if (n, ph, q) == ("A", "F", 0):
                    mix_small()
                if (n, ph, q) == ("B", "G", 1):
                    pool.wait_ge(loaded["w8"], 16)
                    g.tensor_copy(w8b[:].rearrange("p k d -> p (k d)"), w8i[:].bitcast(mybir.dt.int8)).then_inc(wconv, 1)
                    pool.wait_ge(wconv, 1)
                if step == LAST_GO:
                    split_low(0, 0)
                if step == FIRST_H - 1:
                    for c in range(PAIRS // 2):
                        pool.wait_ge(*filled(("o", "G", c)))
                    g.memset(xc[:, :, T:TPAD], 0.0).then_inc(xc_pads, 1)
                    pool.wait_ge(xc_pads, 1)
                if step == LAST_G2:
                    split_low(1, 1)
                if (n, ph) in NEXT_LN:
                    root(NEXT_LN[n, ph], q)
                if ph == "K":
                    root_qk(q)
                if (n, ph) == ("C", "T"):
                    pool.wait_ge(*xn_ready.at((n, q)))
                    add_to_h(n, q, xn[0:ROWS, P8 * q:P8 * q + P8])
                if (n, ph) == ("D", "P"):
                    for c in (2 * q, 2 * q + 1):
                        pool.wait_ge(*updated("D", c))
                    add_to_h(n, q, yt[q][0:ROWS])
                if (n, ph) in (("F", "T"), ("G", "T")):
                    pool.wait_ge(*xn_ready.at((n, q)))
                    add_to_h(n, q, prm("bias_q" if n == "F" else "beta", ROWS).unsqueeze(1).broadcast_to([ROWS, P8, D]))
            with pool.Fori(1, NE // 2) as i:
                for b in range(2):
                    split_low(i * 2 + b, b)

        @block.scalar
        def _(act):
            sc = nc.scalar
            links = [0]
            act.dma_start(cst[:], consts).then_inc(loaded["consts"], 16)

            def mark(ins):
                links[0] += 1
                ins.then_inc(act_chain, 1)

            def normalise(n, q):
                act.wait_ge(*rstd_ready.at((n, q)))
                for p in range(P8):
                    r = P8 * q + p
                    src, dst = (yt[q][0:ROWS, p], x2[q][0:ROWS, p]) if n in ("D2", "G2") else (h[0:ROWS, r], xn[0:ROWS, r])
                    ins = sc.activation(dst, src, ACT.Identity, scale=rstd[0:ROWS, r:r + 1], bias=nmr[0:ROWS, r:r + 1])
                    if n == "D" or p < P8 - 1:
                        mark(ins)
                if n == "D":
                    act.wait_ge(act_chain, links[0])
                    for p in range(P8):
                        ins = sc.activation(x2[q][0:ROWS, p], xn[0:ROWS, P8 * q + p], ACT.Identity,
                                            scale=rst2[0:ROWS, P8 * q + p:P8 * q + p + 1], bias=0.0)
                        if p < P8 - 1:
                            mark(ins)
                ins.then_inc(*xn_ready.inc((n, q)))

            def nt_copy(n, q):
                j = ("nT", n, q, 0)
                act.wait_ge(*filled(j))
                src = spaced(j)
                dst = nT[0][0:96, Q8 * q:Q8 * q + Q8, 0:TOK]
                if n in ("D", "D2"):
                    ln = ("n1" if n == "D" else "n2") + ("l" if q == 0 else "s")
                    sc.activation(dst, src, ACT.Identity, bias=prm(ln + "_b", 96)[:, 0:1], scale=prm(ln + "_g", 96)[:, 0:1]).then_inc(*freed(j))
                elif n == "H":
                    sc.activation(xc[:, 0, QT * q:QT * q + QT].rearrange("p (i k) -> p i k", k=TOK), spaced(j, 128), ACT.Copy).then_inc(*freed(j))
                else:
                    sc.activation(dst, src, ACT.Copy).then_inc(*freed(j))
                if n == "H":
                    act.wait_ge(*evacuated(j))
                    sc.activation(xh[:, 0, QT * q:QT * q + QT], xc[:, 0, QT * q:QT * q + QT], ACT.Copy).then_inc(x_high, 1)
                if n in "BCDEG":
                    act.wait_ge(*evacuated(j))
                    sc.activation(nrep[q][0][0:96].rearrange("p i (r k) -> p i r k", k=TOK),
                                  dst.unsqueeze(2).broadcast_to([96, Q8, HG, TOK]), ACT.Copy).then_inc(*rep_ready[0].inc((n, q)))

            def key_blocks(n, q):
                j = ("k", n, q, 0)
                act.wait_ge(*filled(j))
                mask = maskg[:, 0] if n == "C" else con("mask_k", 96)
                src = spaced(j) if n == "C" else bank(j)[0:96, 0:QT].rearrange("p (i k) -> p i k", k=TOK)
                for x in range(HH):
                    ins = sc.activation(kblk[q][0][:, :, x], src, ACT.Copy, scale=mask[:, x:x + 1])
                    if x < HH - 1:
                        mark(ins)
                ins.then_inc(*freed(j))

            def split_high(e, b):
                act.wait_ge(w1_loaded[b], e // 2 * 16 + 16)
                sc.activation(w1h[:, b], w1b[:, b], ACT.Copy).then_inc(w1_high, 1)

            def first_gelus(b, c, base):
                for m in range(MT):
                    act.wait_ge(fc1_done, base + m + 1)
                    sc.activation(hbuf[b][:, m, QT * c:QT * c + QT], PS[(base + m) % 4][:, 0:QT], ACT.Gelu,
                                  bias=b1cur[:, b, m:m + 1]).then_inc(gelu_done, 1)

            act.wait_ge(zeroed, ZEROED)
            act.wait_ge(loaded["params"], 16)
            act.wait_ge(loaded["consts"], 16)
            for step, (n, ph, q) in enumerate(SCHEDULE):
                ps = range(P8 * q, P8 * q + P8)
                kind = KIND.get(n)
                if (n, q) == ("H", X_OCTS[1]):
                    for b in range(2):
                        sc.activation(b1cur[:, b], prm("b1")[:, MT * b:MT * b + MT], ACT.Copy).then_inc(b1_ready, 1)
                    act.wait_ge(b1_ready, 2)
                    first_gelus(0, X_OCTS[0], 0)
                if ph == "T" or n == "G2":
                    normalise(n, q)
                if (n, q) == ("H", X_OCTS[1]):
                    first_gelus(1, X_OCTS[0], MT)
                if ph == "T" and n != "F":
                    nt_copy(n, q)
                if (n, ph) == ("A", "F"):
                    for s in range(2):
                        j = ("q", n, q, s)
                        act.wait_ge(*filled(j))
                        sc.activation(qT[s][:, QT * q:QT * q + QT], bank(j)[0:96, 0:QT], ACT.Exp).then_inc(*elu_exp.inc(("q", q, s)))
                    for p in ps:
                        act.wait_ge(*filled(("kv", p)))
                        sc.activation(x2[q][0:ROWS, p % P8], bank(("kv", p))[0:ROWS, 0:D], ACT.Exp).then_inc(*elu_exp.inc(("k", p)))
                if ph == "Z":
                    j = ("oT", n, q, 0)
                    act.wait_ge(*filled(j))
                    sc.activation(oT[0][0:96, Q8 * q:Q8 * q + Q8, 0:TOK], spaced(j), ACT.Copy).then_inc(*freed(j))
                if ph == "G":
                    act.wait_ge(*evacuated(("gate", q)))
                    a = slice(P8 * NE * q, P8 * NE * q + P8 * NE)
                    sc.activation(gsm[0:ROWS, 1, a], gsm[0:ROWS, 0, a], ACT.Exp).then_inc(*gate_exp.inc(q))
                if ph == "H":
                    j = ("dx", q)
                    act.wait_ge(*filled(j))
                    sc.activation(dX[q], bank(j)[:, 0:QT], ACT.Copy).then_inc(*freed(j))
                if ph == "F" and n != "A" or ph == "R":
                    if n == "C":
                        act.wait_ge(maskg_ready, 2)
                    key_blocks(n, q)
                    for s in range(2):
                        j = ("q", n, q, s)
                        act.wait_ge(*filled(j))
                        if n == "C":
                            sc.activation(qT[s][:, QT * q:QT * q + QT].rearrange("p (i k) -> p i k", k=TOK), spaced(j),
                                          ACT.Copy, scale=gqs[:, s:s + 1]).then_inc(*freed(j))
                        else:
                            sc.activation(qT[s][:, QT * q:QT * q + QT], bank(j)[0:96, 0:QT], ACT.Copy, scale=SCALE).then_inc(*freed(j))
                if ph == "S" and kind == SOFTMAX:
                    for p in ps:
                        act.wait_ge(*evacuated(("s", n, p)))
                        sc.activation(ar[0:ROWS, p], ar[0:ROWS, p], ACT.Exp).then_inc(*exp_ready.inc((n, p)))
                if ph == "S" and kind == POLY:
                    for p in ps:
                        j = ("s", n, p)
                        act.wait_ge(*filled(j))
                        sc.activation(ar[0:ROWS, p], bank(j)[0:ROWS, 0:H * TOK], ACT.Square, bias=1.0).then_inc(*freed(j))
                if ph == "S" and kind == COLUMN:
                    for p in ps:
                        j = ("s", n, p)
                        act.wait_ge(*filled(j))
                        sc.activation(ar[0:ROWS, p], bank(j)[0:ROWS, 0:H * TOK], ACT.Copy).then_inc(*freed(j))
                if ph == "X" and kind == COLUMN:
                    for p in ps:
                        act.wait_ge(*evacuated(("t", n, p)))
                        a = ar[0:GR, p, 0:2 * NG * TOK]
                        sc.activation(a, a, ACT.Exp).then_inc(*col_exp.inc(p))
                if ph == "X" and kind == SOFTMAX:
                    if n == "B":
                        act.wait_ge(*adrep_ready.at(("B", q)))
                    for p in ps:
                        j = ("t", n, p)
                        act.wait_ge(*filled(j))
                        sc.activation(et[q][:, :, 2 * TOK * (p % P8):2 * TOK * (p % P8) + 2 * TOK].rearrange("p g (i k) -> p g i k", k=TOK),
                                      bank(j)[0:GR, :].rearrange("p (g i k) -> p g i k", g=NG, k=GAP)[:, :, :, 0:TOK],
                                      ACT.Copy).then_inc(*freed(j))
                if ph == "O" and n == "C":
                    for c in range(2 * q, 2 * q + 2):
                        j = ("o", n, c)
                        act.wait_ge(*filled(j))
                        a = 2 * c - P8 * q
                        sc.activation(x2[q][0:ROWS, a:a + 2].rearrange("p c (h e) -> p (c h) e", e=HD),
                                      bank(j)[0:ROWS, 0:2 * VW].rearrange("p (c e) -> p c e", e=HD + 1)[:, :, 0:HD], ACT.Copy).then_inc(*freed(j))
                if ph == "U":
                    for br in MLP_BR[q]:
                        for m in range(MT):
                            j = ("f1", q, br, m)
                            act.wait_ge(*filled(j))
                            sc.activation(hid[q][br][:, m], bank(j)[:, 0:QT], ACT.Gelu, bias=prm("b_fc1")[:, m:m + 1]).then_inc(*freed(j))
                if step == LAST_GX:
                    for p in range(PAIRS):
                        act.wait_ge(*filled(("v", "G", p)))
                        act.wait_ge(*filled(("t", "G", p)))
                    for b in range(2):
                        split_high(b, b)
            act.wait_ge(*evacuated(("gate", "H")))
            sc.activation(gsm[:, 1, 0:CT * NE], gsm[:, 0, 0:CT * NE], ACT.Exp).then_inc(*gate_exp.inc("H"))

            def gelus(i, b, lag=0):
                at = PARAM_AT["b1"][0] + (b - 2 * lag) * MT
                src = par[:, at + i * 2 * MT:at + i * 2 * MT + MT] if isinstance(i, int) else par[:, bass.ds(i * (2 * MT) + at, MT)]
                sc.activation(b1cur[:, b], src, ACT.Copy).then_inc(b1_ready, 1)
                act.wait_ge(b1_ready, i * 2 + (b + 1 - 2 * lag))
                if lag or i:
                    act.wait_ge(fc2_done, i * 6 + (3 * (b + 1) - 6 - 6 * lag))
                    act.dma_start(w2b[:, b], w2[i * 2 + (b - 2 * lag)]).then_inc(w2_loaded[b], 16)
                for m in range(MT):
                    for c in range(2):
                        act.wait_ge(fc1_done, i * 24 + (12 * b + 2 * m + c + 1 - 24 * lag))
                        sc.activation(hbuf[b][:, m, QT * c:QT * c + QT], PS[(2 * m + c) % 4][:, 0:QT], ACT.Gelu,
                                      bias=b1cur[:, b, m:m + 1]).then_inc(gelu_done, 1)
            for b in range(2):
                first_gelus(b, X_OCTS[1], (2 + b) * MT)
                split_high(2 + b, b)
            with act.Fori(2, NE // 2) as i:
                for b in range(2):
                    gelus(i, b, lag=1)
                    act.wait_ge(w1_loaded[b], i * 16 + 16)
                    sc.activation(w1h[:, b], w1b[:, b], ACT.Copy).then_inc(w1_high, 1)
            for b in range(2):
                gelus(NE // 2 - 1, b)

        @block.vector
        def _(dve):
            v = nc.vector
            links = [0]

            def mark(ins):
                links[0] += 1
                ins.then_inc(dve_chain, 1)

            def settle():
                dve.wait_ge(dve_chain, links[0])

            def link(ins):
                mark(ins)
                settle()

            def pair_stats(upd, c):
                n, q = NEXT_LN[upd, "O" if upd == "G" else "P"], 2 * c // P8
                if upd == "G":
                    settle()
                else:
                    dve.wait_ge(*updated(upd, c))
                for p in (2 * c, 2 * c + 1):
                    mark(v.bn_stats(stats[0:ROWS, p], yt[q][0:ROWS, p % P8] if n in ("D2", "G2") else h[0:ROWS, p]))

            def moments(n, q):
                settle()
                for p in range(P8 * q, P8 * q + P8):
                    mark(v.bn_aggr(mv[0:ROWS, p], stats[0:ROWS, p]))
                settle()
                a = slice(P8 * q, P8 * q + P8)
                mark(v.tensor_scalar(nmr[0:ROWS, a], mv[0:ROWS, a, 0], -1.0, None, ALU.mult))
                v.tensor_scalar(rtmp[0:ROWS, a], mv[0:ROWS, a, 1], EPS, None, ALU.add).then_inc(*var_ready.inc((n, q)))

            def nt_copy(n, q):
                j = ("nT", n, q, 1)
                dve.wait_ge(*filled(j))
                src = spaced(j)
                dst = nT[1][0:96, Q8 * q:Q8 * q + Q8, 0:TOK]
                if n in ("D", "D2"):
                    ln = ("n1" if n == "D" else "n2") + ("l" if q == 0 else "s")
                    v.tensor_scalar(dst, src, prm(ln + "_g", 96)[:, 1:2], prm(ln + "_b", 96)[:, 1:2],
                                    ALU.mult, ALU.add).then_inc(*freed(j))
                elif n == "H":
                    v.tensor_copy(xc[0:64, 1, QT * q:QT * q + QT].rearrange("p (i k) -> p i k", k=TOK), spaced(j, 64)).then_inc(*freed(j))
                else:
                    v.tensor_copy(dst, src).then_inc(*freed(j))
                if n == "H":
                    dve.wait_ge(*evacuated(j))
                    a = slice(QT * q, QT * q + QT)
                    link(v.tensor_copy(xh[0:64, 1, a], xc[0:64, 1, a]))
                    dve.wait_ge(*evacuated(("nT", n, q, 0)))
                    dve.wait_ge(x_high, X_OCTS.index(q) + 1)
                    for p in range(PAIRS):
                        dve.wait_ge(*filled(("t", "G", p)))
                    mark(v.tensor_copy(xl[0:64, 1, a], xh[0:64, 1, a].bitcast(F)))
                    mark(v.tensor_tensor(xl[64:128, 1, a], xc[0:64, 1, a], xh[0:64, 1, a].bitcast(F), ALU.subtract))
                    v.tensor_tensor(xl[:, 0, a], xc[:, 0, a], xh[:, 0, a].bitcast(F), ALU.subtract).then_inc(x_split, 1)
                if n in "BCDEG":
                    dve.wait_ge(*evacuated(j))
                    v.tensor_copy(nrep[q][1].rearrange("p i (r k) -> p i r k", k=TOK),
                                  nT[1][0:97, Q8 * q:Q8 * q + Q8, 0:TOK].unsqueeze(2).broadcast_to([97, Q8, HG, TOK])).then_inc(*rep_ready[1].inc((n, q)))

            def key_blocks(n, q):
                j = ("k", n, q, 1)
                dve.wait_ge(*filled(j))
                mask = maskg[:, 1] if n == "C" else con("mask_k", 96)
                src = spaced(j) if n == "C" else bank(j)[0:96, 0:QT].rearrange("p (i k) -> p i k", k=TOK)
                v.tensor_tensor(kblk[q][1], src.unsqueeze(2).broadcast_to([96, Q8, HH, TOK]),
                                mask.unsqueeze(1).unsqueeze(3).broadcast_to([96, Q8, HH, TOK]), ALU.mult).then_inc(*freed(j))

            def value_blocks(n, p):
                j = ("v", n, p)
                dve.wait_ge(*filled(j))
                src = bank(j)[0:GR, 0:2 * D].rearrange("p (a r e) -> p a r e", r=HG, e=HD)
                m = con("mask_v", GR).rearrange("p (r e) -> p r e", e=HD).unsqueeze(1).broadcast_to([GR, 2 * NG, HG, HD])
                v.tensor_tensor(vblk[:, 2 * p:2 * p + 2].rearrange("p i g r e -> p (i g) r e")[:, :, :, 0:HD], src, m, ALU.mult).then_inc(*freed(j))

            def score_pair(n, p):
                j = ("s", n, p)
                dve.wait_ge(*filled(j))
                sc = bank(j)[0:ROWS, 0:H * TOK].rearrange("p (h k) -> p h k", k=TOK)
                link(v.tensor_reduce(mx[0:ROWS, p], sc, AX.X, ALU.max))
                v.tensor_tensor(ar[0:ROWS, p].rearrange("p (h k) -> p h k", k=TOK), sc,
                                mx[0:ROWS, p].unsqueeze(2).broadcast_to([ROWS, H, TOK]), ALU.subtract).then_inc(*freed(j))

            def column_softmax(p):
                j = ("t", "C", p)
                dve.wait_ge(*filled(j))
                sc = bank(j)[0:GR, :].rearrange("p (a k) -> p a k", k=GAP)[:, :, 0:TOK]
                link(v.tensor_reduce(mx[0:GR, p, 0:2 * NG], sc, AX.X, ALU.max))
                v.tensor_tensor(ar[0:GR, p, 0:2 * NG * TOK].rearrange("p (a k) -> p a k", k=TOK), sc,
                                mx[0:GR, p, 0:2 * NG].unsqueeze(2).broadcast_to([GR, 2 * NG, TOK]), ALU.subtract).then_inc(*freed(j))

            def column_norm(p):
                dve.wait_ge(*col_exp.at(p))
                e = ar[0:GR, p, 0:2 * NG * TOK]
                tot, inv = rs[0:GR, p, 0:2 * NG], rs[0:GR, p, H:H + 2 * NG]
                link(v.tensor_reduce(tot, e.rearrange("p (a k) -> p a k", k=TOK), AX.X, ALU.add))
                link(v.reciprocal(inv, tot))
                a = 2 * TOK * (p % P8)
                v.tensor_tensor(et[p // P8][:, :, a:a + 2 * TOK].rearrange("p g (i k) -> p g i k", k=TOK),
                                e.rearrange("p (g i k) -> p g i k", g=NG, k=TOK),
                                inv.rearrange("p (g i) -> p g i", g=NG).unsqueeze(3).broadcast_to([GR, NG, 2, TOK]),
                                ALU.mult).then_inc(*et_ready.inc(p))

            def poly(p):
                j, q = ("t", "E", p), p // P8
                dve.wait_ge(*filled(j))
                a = 2 * TOK * (p % P8)
                v.tensor_scalar(et[q][:, :, a:a + 2 * TOK].rearrange("p g (i k) -> p g i k", k=TOK),
                                bank(j)[0:GR, :].rearrange("p (g i k) -> p g i k", g=NG, k=GAP)[:, :, :, 0:TOK],
                                1.0, 0.0, ALU.add, ALU.max).then_inc(*freed(j))

            def add_bank(j, dst, other):
                dve.wait_ge(*filled(j))
                v.tensor_tensor(dst, bank(j)[0:ROWS, 0:2 * D].rearrange("p (c d) -> p c d", d=D), other, ALU.add).then_inc(*freed(j))

            def gating(n, j, rows, tiles, first, scratch):
                m, g0 = tiles * NE, first * NE
                dve.wait_ge(*filled(j))
                lg = bank(j)[0:rows, 0:m].rearrange("p (c e) -> p c e", e=NE)
                top, tot, inv = (grow[0:rows, x, first:first + tiles] for x in range(3))
                link(v.tensor_reduce(top, lg, AX.X, ALU.max))
                gate, e, rank, keep = (gsm[0:rows, x, g0:g0 + m] for x in range(4))
                gate3, e3 = (x.rearrange("p (c e) -> p c e", e=NE) for x in (gate, e))
                v.tensor_tensor(gate3, lg, top.unsqueeze(2).broadcast_to([rows, tiles, NE]), ALU.subtract).then_inc(*freed(j))
                dve.wait_ge(*evacuated(j))
                dve.wait_ge(*gate_exp.at(n))
                mark(v.tensor_reduce(tot, e3, AX.X, ALU.add))
                diff, equal = (scratch[0:rows, x * m * NE:(x + 1) * m * NE].rearrange("p (c i j) -> p c i j", i=NE, j=NE) for x in range(2))
                link(v.tensor_tensor(diff, e3.unsqueeze(2).broadcast_to([rows, tiles, NE, NE]),
                                     e3.unsqueeze(3).broadcast_to([rows, tiles, NE, NE]), ALU.subtract))
                mark(v.reciprocal(inv, tot))
                tri = con("tri", rows).rearrange("p (i j) -> p i j", j=NE).unsqueeze(1).broadcast_to([rows, tiles, NE, NE])
                link(v.scalar_tensor_tensor(equal, diff, 0.0, tri, ALU.is_equal, ALU.mult))
                link(v.scalar_tensor_tensor(equal, diff, 0.0, equal, ALU.is_gt, ALU.add))
                link(v.tensor_reduce(rank, equal.rearrange("p c i j -> p (c i) j"), AX.X, ALU.add))
                link(v.scalar_tensor_tensor(keep, rank, TOPK - 0.5, e, ALU.is_lt, ALU.mult))
                v.tensor_tensor(disp[0:rows, first:first + tiles], keep.rearrange("p (c e) -> p c e", e=NE),
                                inv.unsqueeze(2).broadcast_to([rows, tiles, NE]), ALU.mult).then_inc(*disp_ready.inc(n))

            for s in range(2):
                for t in (nT[s], oT[s]):
                    v.memset(t[0:96], 0.0).then_inc(zeroed, 1)
                    v.memset(t[96:97], 1.0).then_inc(zeroed, 1)
            v.memset(ones[:], 1.0).then_inc(zeroed, 1)
            dve.wait_ge(loaded["params"], 16)
            pos = prm("pos", ROWS)
            for i in range(2):
                mark(v.tensor_tensor(pos[GAP * i:GAP * i + 1], pos[GAP * i:GAP * i + 1], prm("cls")[GAP * i:GAP * i + 1], ALU.add))
            settle()
            dve.wait_ge(zeroed, ZEROED)

            for n, ph, q in SCHEDULE:
                kind = KIND.get(n)
                cs, ps = range(2 * q, 2 * q + 2), range(P8 * q, P8 * q + P8)
                if n == "tok":
                    for c in cs:
                        add_bank(("tok", c), h[0:ROWS, 2 * c:2 * c + 2], pos.unsqueeze(1).broadcast_to([ROWS, 2, D]))
                        pair_stats(n, c)
                if ph == "T" and n != "F":
                    if n == "H":
                        dve.wait_ge(xc_pads, 1)
                    nt_copy(n, q)
                if (n, ph) == ("A", "F"):
                    if q == 0:
                        dve.wait_ge(loaded["consts"], 16)
                        link(v.tensor_copy(vblk[:, :, :, :, HD].rearrange("p i g r -> p (i g) r"),
                                           con("mask_v", GR).rearrange("p (r e) -> p r e", e=HD)[:, :, 0].unsqueeze(1).broadcast_to([GR, B * NG, HG])))
                        v.tensor_tensor(maskg[:], con("mask_k", 96).unsqueeze(1).broadcast_to([96, 2, HH]),
                                        prm("gk", 96).unsqueeze(2).broadcast_to([96, 2, HH]), ALU.mult).then_inc(maskg_ready, 1)
                        v.tensor_scalar(gqs[:], prm("gq", 96), SCALE, None, ALU.mult).then_inc(maskg_ready, 1)
                    for s in range(2):
                        j = ("q", n, q, s)
                        a = qT[s][:, QT * q:QT * q + QT]
                        dve.wait_ge(*elu_exp.at(("q", q, s)))
                        link(v.tensor_scalar(a, a, 1.0, None, ALU.min))
                        v.scalar_tensor_tensor(a, bank(j)[0:96, 0:QT], 0.0, a, ALU.max, ALU.add).then_inc(*freed(j))
                    vt = ar[0:ROWS, P8 * q:P8 * q + P8, 0:VW].rearrange("p c (h e) -> p c h e", e=HD + 1)
                    link(v.memset(vt[:, :, :, HD:HD + 1], 1.0))
                    for p in ps:
                        j = ("kv", p)
                        k = x2[q][0:ROWS, p % P8]
                        dve.wait_ge(*elu_exp.at(("k", p)))
                        mark(v.tensor_copy(vt[:, p % P8, :, 0:HD], bank(j)[0:ROWS, D:2 * D].rearrange("p (h e) -> p h e", e=HD)))
                        link(v.tensor_scalar(k, k, 1.0, None, ALU.min))
                        v.scalar_tensor_tensor(k, bank(j)[0:ROWS, 0:D], 0.0, k, ALU.max, ALU.add).then_inc(*freed(j))
                if ph == "M":
                    kvs = big[0:96, q, 0:P8 * 2 * VW].rearrange("p (c a x) -> p c a x", a=2, x=VW)
                    for c in cs:
                        for pr in range(2):
                            j = ("kvm", c, pr)
                            dve.wait_ge(*filled(j))
                            a = 2 * c - P8 * q
                            v.tensor_tensor(kvs[:, a:a + 2, pr].rearrange("p c (s x) -> p c s x", s=2),
                                            bank(j)[0:96, 0:2 * VW].rearrange("p (c s x) -> p c s x", c=2, s=2),
                                            con("mask_kv", 96).unsqueeze(1).unsqueeze(1).broadcast_to([96, 2, 2, VW // 2]), ALU.mult).then_inc(*freed(j))
                if ph == "O" and n != "C":
                    for c in cs:
                        j = ("o", n, c)
                        dve.wait_ge(*filled(j))
                        src = bank(j)[0:ROWS, 0:2 * VW].rearrange("p (c e) -> p c e", e=HD + 1)
                        inv = rs[0:ROWS, c]
                        link(v.reciprocal(inv, src[:, :, HD]))
                        a = 2 * c - P8 * q
                        o = x2[q][0:ROWS, a:a + 2]
                        v.tensor_tensor(o.rearrange("p c (h e) -> p (c h) e", e=HD), src[:, :, 0:HD],
                                        inv.unsqueeze(2).broadcast_to([ROWS, 2 * H, HD]), ALU.mult).then_inc(*freed(j))
                        if n == "G":
                            dve.wait_ge(*evacuated(j))
                            mark(v.tensor_tensor(yt[q][0:ROWS, a:a + 2], o, xn[0:ROWS, 2 * c:2 * c + 2], ALU.add))
                            pair_stats(n, c)
                if ph == "Z":
                    j = ("oT", n, q, 1)
                    dve.wait_ge(*filled(j))
                    v.tensor_copy(oT[1][0:96, Q8 * q:Q8 * q + Q8, 0:TOK], spaced(j)).then_inc(*freed(j))
                if ph == "G":
                    gating(q, ("gate", q), ROWS, P8, P8 * q, et_raw[:, q, 1:3].rearrange("p g t -> p (g t)"))
                if ph == "H":
                    j = ("dT", q)
                    dve.wait_ge(*filled(j))
                    v.tensor_copy(dispT[q].rearrange("p (i k) -> p i k", k=TOK),
                                  bank(j)[0:NE, :].rearrange("p (i k) -> p i k", k=GAP)[:, :, 0:TOK]).then_inc(*freed(j))
                    j = ("a", q)
                    dve.wait_ge(*filled(j))
                    dve.wait_ge(*evacuated(("dx", q)))
                    v.tensor_tensor(ad[q], bank(j)[:, 0:QT], dX[q], ALU.mult).then_inc(*freed(j))
                    dve.wait_ge(*evacuated(j))
                    v.tensor_copy(adrep[q].rearrange("p i (r k) -> p i r k", k=TOK),
                                  ad[q].rearrange("p (i k) -> p i k", k=TOK).unsqueeze(2).broadcast_to([128, Q8, HG, TOK])).then_inc(*adrep_ready.inc((n, q)))
                if ph == "K":
                    for p in ps:
                        dve.wait_ge(*filled(("qk", p)))
                        for a in range(2):
                            mark(v.bn_stats(stats_qk[0:ROWS, 2 * p + a], bank(("qk", p))[0:ROWS, D * a:D * a + D]))
                    settle()
                    for x in range(2 * P8 * q, 2 * P8 * q + 2 * P8):
                        ins = v.bn_aggr(mv_qk[0:ROWS, x], stats_qk[0:ROWS, x])
                        if x < 2 * P8 * (q + 1) - 1:
                            mark(ins)
                    ins.then_inc(*var_ready.inc(("Cqk", q)))
                if ph == "R":
                    dve.wait_ge(*rstd_ready.at(("Cqk", q)))
                    for p in ps:
                        j = ("qk", p)
                        for a, dst in enumerate((x2[q], yt[q])):
                            ins = v.tensor_scalar(dst[0:ROWS, p % P8], bank(j)[0:ROWS, D * a:D * a + D], mv_qk[0:ROWS, 2 * p + a, 0:1],
                                                  rstd_qk[0:ROWS, 2 * p + a:2 * p + a + 1], ALU.subtract, ALU.mult)
                            if a == 0:
                                mark(ins)
                        ins.then_inc(*freed(j))
                if ph == "F" and n != "A" or ph == "R":
                    key_blocks(n, q)
                if ph == "S":
                    if kind == SOFTMAX:
                        for p in ps:
                            score_pair(n, p)
                if (n, ph) == ("C", "X"):
                    for p in ps:
                        column_softmax(p)
                if ph == "N":
                    for p in ps:
                        column_norm(p)
                if (n, ph) == ("E", "X"):
                    for p in ps:
                        poly(p)
                if ph == "W":
                    for p in ps:
                        value_blocks(n, p)
                if (n, ph) == ("F", "T"):
                    qf = [big[0:96, q, a * QT:(a + 1) * QT] for a in range(4)]
                    for s in range(2):
                        j = ("nT", "F", q, s)
                        dve.wait_ge(*filled(j))
                        v.tensor_scalar(qf[2 * s].rearrange("p (i k) -> p i k", k=TOK), spaced(j), 1.0 / ACT_SCALE, 127.0, ALU.mult, ALU.min).then_inc(*freed(j))
                    for s in range(2):
                        dve.wait_ge(*evacuated(("nT", "F", q, s)))
                        mark(v.tensor_scalar(qf[2 * s + 1], qf[2 * s], -128.0, ROUND, ALU.max, ALU.add))
                    settle()
                    for s in range(2):
                        v.tensor_scalar(nq[:, s, Q8 * q:Q8 * q + Q8, 0:TOK], qf[2 * s + 1].rearrange("p (i k) -> p i k", k=TOK),
                                        ROUND, None, ALU.subtract).then_inc(*nq_ready.inc((q, s)))
                if ph == "U" and q == 1:
                    for br in MLP_BR[q]:
                        g, now, sofar = prm("gumbel")[:, br:br + 1], hid[q][br], hid[q][br - 1]
                        for m in range(0, MT, 2):
                            t = slice(m, m + 2)
                            for x in range(2):
                                dve.wait_ge(*evacuated(("f1", q, br, m + x)))
                            if br:
                                dve.wait_ge(hid_mixed, (br - 1) * MT // 2 + m // 2 + 1)
                                v.scalar_tensor_tensor(now[:, t], now[:, t], g, sofar[:, t], ALU.mult, ALU.add).then_inc(hid_mixed, 1)
                            else:
                                v.tensor_scalar(now[:, t], now[:, t], g, None, ALU.mult).then_inc(hid_mixed, 1)
                if ph == "V":
                    if q == 1:
                        dve.wait_ge(mixed, 1)
                    for s in (1, 0):
                        j = ("f2", q, s)
                        dve.wait_ge(*filled(j))
                        bias = prm("b_fc2", 96)[:, s:s + 1] if q == 0 else b2s[:, s:s + 1]
                        v.tensor_scalar(oT[s][0:96, Q8 * q:Q8 * q + Q8, 0:TOK], bank(j)[0:96, 0:QT].rearrange("p (i k) -> p i k", k=TOK),
                                        bias, None, ALU.add).then_inc(*freed(j))
                if ph == "P" and n not in ("tok", "G2"):
                    if (n, ph) in (("C", "P"), ("D2", "P"), ("F", "P")):
                        dve.wait_ge(*h_plus.at(("D" if n == "D2" else n, q)))
                    for c in cs:
                        j = phase_jobs(n, ph, q)[c - 2 * q]
                        a = 2 * c - P8 * q
                        hc2, xn2, y2 = h[0:ROWS, 2 * c:2 * c + 2], xn[0:ROWS, 2 * c:2 * c + 2], yt[q][0:ROWS, a:a + 2]
                        if n == "F":
                            dve.wait_ge(*filled(j))
                            v.scalar_tensor_tensor(hc2, bank(j)[0:ROWS, 0:2 * D].rearrange("p (c d) -> p c d", d=D), EFF_SCALE, hc2,
                                                   ALU.mult, ALU.add).then_inc(*freed(j))
                        elif n == "D":
                            add_bank(j, y2, xn2)
                        else:
                            add_bank(j, hc2, hc2)
                        pair_stats(n, c)
                if n == "G2":
                    dve.wait_ge(*xn_ready.at((n, q)))
                    dve.wait_ge(*h_plus.at(("G", q)))
                    for c in cs:
                        a = x2[q][0:ROWS, 2 * c - P8 * q:2 * c - P8 * q + 2]
                        link(v.tensor_tensor(a, a, prm("gamma", ROWS).unsqueeze(1).broadcast_to([ROWS, 2, D]), ALU.mult))
                        v.tensor_tensor(h[0:ROWS, 2 * c:2 * c + 2], h[0:ROWS, 2 * c:2 * c + 2], a, ALU.add).then_inc(*g_done.inc(c))
                        pair_stats(n, c)
                if (n, ph) in NEXT_LN:
                    moments(NEXT_LN[n, ph], q)

            gating("H", ("gate", "H"), 128, CT, 0, et_raw[:].rearrange("p q g t -> p (q g t)")[:, T:])
            for a in range(2):
                j = ("eT", a)
                dve.wait_ge(*filled(j))
                n = 512 if a == 0 else T - 512
                v.tensor_copy(eT[:, 512 * a:512 * a + n], bank(j)[0:NE, 0:n]).then_inc(*freed(j))
            dve.wait_ge(h_back, 32)

            def tiles(c):
                return (128, slice(2 * c, 2 * c + 2)) if c < 2 else (crow[-1], slice(CT - 1, CT))
            for c in range(3):
                j = ("eb", c)
                r, sl = tiles(c)
                dve.wait_ge(*filled(j))
                n = sl.stop - sl.start
                v.tensor_tensor(acc[0:r, sl], bank(j)[0:r, 0:n * D].rearrange("p (c d) -> p c d", d=D), hc[0:r, sl], ALU.add).then_inc(*freed(j))
                dve.wait_ge(*evacuated(j))

            def add_expert(i, b):
                for c in range(3):
                    r, sl = tiles(c)
                    dve.wait_ge(fc2_done, i * 6 + (3 * b + c + 1))
                    for t in range(sl.start, sl.stop):
                        at = i * 2 + (b + t * NE)
                        gate = disp[:].rearrange("p c e -> p (c e)")[0:r, bass.ds(at, 1)]
                        ins = v.scalar_tensor_tensor(acc[0:r, t], PS[4 + c][0:r, (t - sl.start) * D:(t - sl.start + 1) * D],
                                                     gate, acc[0:r, t], ALU.mult, ALU.add)
                    ins.then_inc(acc_done, 1)
            with dve.Fori(0, NE // 2) as i:
                for b in range(2):
                    if b == 1:
                        dve.wait_ge(acc_done, i * 6 + 3)
                    add_expert(i, b)
                dve.wait_ge(acc_done, i * 6 + 6)

        @block.tensor
        def _(pe):
            mm = nc.tensor.matmul
            done = [0]

            def start_job(j):
                assert order[done[0]] == j, (order[done[0]], j)
                done[0] += 1
                b, k = where[j]
                if k:
                    pe.wait_ge(bank_read[b], k)
                return PS[b]

            def end_job(j, last):
                last.then_inc(bank_filled[where[j][0]], 1)

            def wait_evacuated(*jobs):
                for j in jobs:
                    pe.wait_ge(*evacuated(j))

            def transposes(j, src, s):
                ps = start_job(j)
                for p in range(P8):
                    last = nc.tensor.transpose(ps[0:96, 128 * p:128 * p + ROWS], src[0:ROWS, p, 96 * s:96 * s + 96], ident[0:ROWS, 0:ROWS])
                end_job(j, last)

            def expert_transposes(j, src, s):
                ps = start_job(j)
                for p in range(P8):
                    rows = 128 if s == 0 else D - 128
                    last = nc.tensor.transpose(ps[0:rows, 128 * p:128 * p + ROWS], src[0:ROWS, p, 128 * s:128 * s + rows], ident[0:ROWS, 0:ROWS])
                end_job(j, last)

            def nt(k, q):
                return nT[k][0:96 + k, Q8 * q:Q8 * q + Q8, 0:TOK]

            def pair_cols(t, k, p):
                return t[k][0:96 + k].rearrange("p i k -> p (i k)")[:, 128 * p:128 * p + ROWS]

            def feature_job(j, seg, col, q, s, lora=False):
                ps = start_job(j)
                o = ps[0:96, 0:QT]
                for k in range(2):
                    last = mm(o, w(seg, k, col + 96 * s, 96), nt(k, q), start=(k == 0), stop=(k == 1 and not lora))
                if lora:
                    last = mm(o, bup[:, col + 96 * s:col + 96 * s + 96], ad[q], start=False, stop=True)
                end_job(j, last)

            def token_job(j, t, p, wk, n):
                ps = start_job(j)
                for k in range(2):
                    last = mm(ps[0:ROWS, 0:n], pair_cols(t, k, p), wk(k), start=(k == 0), stop=(k == 1))
                end_job(j, last)

            def value_job(n, p):
                j = ("v", n, p)
                q = p // P8
                ps = start_job(j)
                for i in range(2):
                    o = ps[0:GR, D * i:D * i + D]
                    im = 2 * (p % P8) + i
                    for k in range(2):
                        last = mm(o, nrep[q][k][0:96 + k, im], w(n + "_qkv", k, 2 * D, D), start=(k == 0), stop=(k == 1 and n != "B"))
                    if n == "B":
                        last = mm(o, adrep[q][:, im], bup[:, 2 * D:3 * D], start=False, stop=True)
                end_job(j, last)

            def hidden(x, b, m, c):
                ps = PS[x % 4]
                parts = [(a[0:rows, b, k, 128 * m:128 * m + 128], t[0:rows, k, QT * c:QT * c + QT])
                         for a, t, k, rows in ((w1l, xh, 0, 128), (w1l, xh, 1, D - 128), (w1h, xl, 0, 128), (w1h, xl, 1, 128), (w1h, xh, 0, 128))]
                for y, (a, t) in enumerate(parts):
                    last = mm(ps[:, 0:QT], a, t, start=(y == 0), stop=(y == len(parts) - 1))
                last.then_inc(fc1_done, 1)

            def first_hidden(b, c, base):
                pe.wait_ge(w1_low, b + 1)
                pe.wait_ge(x_split, X_OCTS.index(c) + 1)
                for m in range(MT):
                    if base + m >= 4:
                        pe.wait_ge(gelu_done, base + m - 3)
                    hidden(base + m, b, m, c)

            pe.wait_ge(loaded["tokw"], 16)
            for n, ph, q in SCHEDULE:
                kind = KIND.get(n)
                if (n, q) == ("H", X_OCTS[1]):
                    wait_evacuated(*[max((j for j in order if where[j][0] == b), key=lambda j: where[j][1]) for b in range(4)])
                    for b in range(2):
                        first_hidden(b, X_OCTS[0], b * MT)
                cs, ps8 = range(2 * q, 2 * q + 2), range(P8 * q, P8 * q + P8)
                if n == "tok":
                    for c in cs:
                        pe.wait_ge(loaded[f"patch{c}"], 16)
                        ps = start_job(("tok", c))
                        for i in range(2):
                            for k in range(PATCH_K):
                                last = mm(ps[0:ROWS, D * i:D * i + D], patch[q][:, 2 * c - P8 * q + i, k], tokw[:, k],
                                          start=(k == 0), stop=(k == PATCH_K - 1))
                        end_job(("tok", c), last)
                    if q == 0:
                        pe.wait_ge(loaded["consts"], 16)
                if ph == "T":
                    pe.wait_ge(*xn_ready.at((n, q)))
                    for s in range(2):
                        (expert_transposes if n == "H" else transposes)(("nT", n, q, s), x2[q] if n in ("D", "D2") else xn[:, P8 * q:P8 * q + P8], s)
                    if n in LOADED_BY and q == 0:
                        pe.wait_ge(loaded[LOADED_BY[n]], 16)
                if (n, ph) == ("A", "F"):
                    wait_evacuated(("nT", n, q, 0), ("nT", n, q, 1))
                    for s in range(2):
                        feature_job(("q", n, q, s), "A_qkv", 0, q, s)
                    for p in ps8:
                        token_job(("kv", p), nT, p, lambda k: w("A_qkv", k, D, 2 * D), 2 * D)
                if ph == "M":
                    for c in cs:
                        wait_evacuated(("kv", 2 * c), ("kv", 2 * c + 1))
                        for pr in range(2):
                            ps = start_job(("kvm", c, pr))
                            r = slice(GAP * pr, GAP * pr + TOK)
                            for i in range(2):
                                for s in range(2):
                                    last = mm(ps[0:96, VW * i + VW // 2 * s:VW * i + VW // 2 * (s + 1)], x2[q][r, 2 * c - P8 * q + i, 96 * s:96 * s + 96],
                                              ar[r, 2 * c + i, VW // 2 * s:VW // 2 * (s + 1)], start=True, stop=True)
                            end_job(("kvm", c, pr), last)
                if (n, ph) == ("A", "O"):
                    wait_evacuated(("q", n, q, 0), ("q", n, q, 1))
                    kvs = big[0:96, q, 0:P8 * 2 * VW].rearrange("p (c a x) -> p c a x", a=2, x=VW)
                    for c in cs:
                        wait_evacuated(("kvm", c, 0), ("kvm", c, 1))
                        ps = start_job(("o", n, c))
                        for i in range(2):
                            for pr in range(2):
                                im = 2 * (2 * c + i) + pr
                                m = GAP if pr == 0 else TOK
                                for s in range(2):
                                    last = mm(ps[GAP * pr:GAP * pr + m, VW * i + VW // 2 * s:VW * i + VW // 2 * (s + 1)],
                                              qT[s][:, TOK * im:TOK * im + m], kvs[:, 2 * c - P8 * q + i, pr, VW // 2 * s:VW // 2 * (s + 1)],
                                              start=True, stop=True)
                        end_job(("o", n, c), last)
                if ph == "Z":
                    wait_evacuated(*[("o", n, c) for c in cs])
                    for s in range(2):
                        transposes(("oT", n, q, s), x2[q], s)
                if ph == "G":
                    wait_evacuated(("nT", n, q, 0), ("nT", n, q, 1))
                    ps = start_job(("gate", q))
                    for p in range(P8):
                        for k in range(2):
                            last = mm(ps[0:ROWS, NE * p:NE * p + NE], pair_cols(nT, k, P8 * q + p), w("B_gate", k), start=(k == 0), stop=(k == 1))
                    end_job(("gate", q), last)
                    ps = start_job(("a", q))
                    for k in range(2):
                        last = mm(ps[:, 0:QT], w("B_down", k), nt(k, q), start=(k == 0), stop=(k == 1))
                    end_job(("a", q), last)
                if ph == "H":
                    pe.wait_ge(*disp_ready.at(q))
                    ps = start_job(("dT", q))
                    for p in range(P8):
                        last = nc.tensor.transpose(ps[0:NE, 128 * p:128 * p + ROWS], disp[0:ROWS, P8 * q + p], ident[0:ROWS, 0:ROWS])
                    end_job(("dT", q), last)
                    if q == 0:
                        pe.wait_ge(loaded["bup"], 16)
                    wait_evacuated(("dT", q))
                    ps = start_job(("dx", q))
                    end_job(("dx", q), mm(ps[:, 0:QT], con("expand", NE), dispT[q], start=True, stop=True))
                if ph == "K":
                    wait_evacuated(("nT", n, q, 0), ("nT", n, q, 1))
                    for p in ps8:
                        token_job(("qk", p), nT, p, lambda k: w("C_qkv", k, 0, 2 * D), 2 * D)
                if ph == "R":
                    wait_evacuated(*[("qk", p) for p in ps8])
                    for s in range(2):
                        transposes(("k", n, q, s), yt[q], s)
                        transposes(("q", n, q, s), x2[q], s)
                if ph == "F" and n != "A":
                    wait_evacuated(("nT", n, q, 0), ("nT", n, q, 1))
                    if n == "B":
                        wait_evacuated(("a", q))
                    for s in range(2):
                        feature_job(("k", n, q, s), n + "_qkv", D, q, s, lora=(n == "B"))
                        feature_job(("q", n, q, s), n + "_qkv", 0, q, s, lora=(n == "B"))
                if ph == "S":
                    wait_evacuated(*[(a, n, q, s) for s in range(2) for a in "kq"])
                    for p in ps8:
                        j = ("s", n, p)
                        ps = start_job(j)
                        for i in range(2):
                            im = 2 * p + i
                            m = GAP if i == 0 else TOK
                            for s in range(2):
                                last = mm(ps[GAP * i:GAP * i + m, HH * TOK * s:HH * TOK * s + HH * TOK], qT[s][:, TOK * im:TOK * im + m],
                                          kblk[q][s][:, im % Q8].rearrange("p h k -> p (h k)"), start=True, stop=True)
                        end_job(j, last)
                if ph == "W":
                    for s in range(2):
                        pe.wait_ge(*rep_ready[s].at((n, q)))
                    if n == "B":
                        pe.wait_ge(*adrep_ready.at((n, q)))
                    for p in ps8:
                        value_job(n, p)
                if ph == "X":
                    for p in ps8:
                        j = ("t", n, p)
                        pe.wait_ge(*(exp_ready.at((n, p)) if kind == SOFTMAX else evacuated(("s", n, p))))
                        ps = start_job(j)
                        for g in range(NG):
                            last = nc.tensor.transpose(ps[0:GR, 128 * g:128 * g + ROWS], ar[0:ROWS, p, GR * g:GR * g + GR], ident[0:ROWS, 0:ROWS])
                        end_job(j, last)
                if ph == "O" and n != "A":
                    wait_evacuated(*[("v", n, p) for p in ps8])
                    wait_evacuated(*[("t", n, p) for p in ps8])
                    if kind == COLUMN:
                        pe.wait_ge(*et_ready.at(ps8[-1]))
                    gw = VW // NG
                    for c in cs:
                        ps = start_job(("o", n, c))
                        for i in range(2):
                            for g in range(NG):
                                for pr in range(2):
                                    im = 2 * (2 * c + i) + pr
                                    m = GAP if pr == 0 else TOK
                                    last = mm(ps[GAP * pr:GAP * pr + m, VW * i + gw * g:VW * i + gw * (g + 1)],
                                              et[q][:, g, TOK * (im - Q8 * q):TOK * (im - Q8 * q) + m],
                                              vblk[:, im, g].rearrange("p r e -> p (r e)"), start=True, stop=True)
                        end_job(("o", n, c), last)
                if ph == "U":
                    wait_evacuated(("nT", n, q, 0), ("nT", n, q, 1))
                    for br in MLP_BR[q]:
                        parts = [(k, min(96, KEEP[br] - 96 * k)) for k in range(2) if KEEP[br] > 96 * k]
                        for m in range(MT):
                            j = ("f1", q, br, m)
                            ps = start_job(j)
                            for x, (k, r) in enumerate(parts):
                                last = mm(ps[:, 0:QT], w("D_fc1", k, 128 * m, 128)[0:r], nT[k][0:r, Q8 * q:Q8 * q + Q8, 0:TOK],
                                          start=(x == 0), stop=(x == len(parts) - 1))
                            end_job(j, last)
                if ph == "V":
                    pe.wait_ge(loaded["fc2w"], 16)
                    for s in (1, 0):
                        ps = start_job(("f2", q, s))
                        groups = [(64, 96, 1), (0, 64, 2)] if (q, s) == (1, 0) else [(96 * s, 96 * s + 96, 0)]
                        for a, z, br in groups:
                            for m in range(MT):
                                if q == 0:
                                    wait_evacuated(("f1", q, br, m))
                                elif m % 2 == 0:
                                    pe.wait_ge(hid_mixed, (br * MT + m) // 2 + 1)
                                last = mm(ps[a - 96 * s:z - 96 * s, 0:QT], fc2w[:, m, a:z], hid[q][br][:, m], start=(m == 0), stop=(m == MT - 1))
                        end_job(("f2", q, s), last)
                if (n, ph) == ("F", "P"):
                    if q == 0:
                        pe.wait_ge(wconv, 1)
                    pe.wait_ge(*nq_ready.at((q, 1)))
                    for c in cs:
                        ps = start_job(("int", c))
                        for i in range(2):
                            for k in range(2):
                                last = mm(ps[0:ROWS, D * i:D * i + D], nq[:, k].rearrange("p i k -> p (i k)")[:, 128 * (2 * c + i):128 * (2 * c + i) + ROWS],
                                          w8b[:, k], start=(k == 0), stop=(k == 1))
                        end_job(("int", c), last)
                elif (n, ph) == ("D2", "P"):
                    wait_evacuated(*[("f2", q, s) for s in range(2)])
                    for c in cs:
                        ps = start_job(("back", n, c))
                        for i in range(2):
                            for s in range(2):
                                last = nc.tensor.transpose(ps[0:ROWS, D * i + 96 * s:D * i + 96 * s + 96],
                                                           oT[s][0:96].rearrange("p i k -> p (i k)")[:, 128 * (2 * c + i):128 * (2 * c + i) + ROWS],
                                                           ident[0:96, 0:96])
                        end_job(("back", n, c), last)
                elif ph == "P" and n in KIND:
                    wait_evacuated(*[("oT", n, q, s) for s in range(2)])
                    if n == "D" and q == 1:
                        pe.wait_ge(mixed, 1)
                    for c in cs:
                        ps = start_job(("p", n, c))
                        for i in range(2):
                            for k in range(2):
                                wp = wps[0:96 + k, k] if n == "D" and q == 1 else w(n + "_proj", k)
                                last = mm(ps[0:ROWS, D * i:D * i + D], pair_cols(oT, k, 2 * c + i), wp, start=(k == 0), stop=(k == 1))
                        end_job(("p", n, c), last)
            wait_evacuated(*[("nT", "H", q, s) for q in range(2) for s in range(2)])
            pe.wait_ge(zeroed, ZEROED)
            ps = start_job(("gate", "H"))
            pe.wait_ge(loaded["params"], 16)
            hg = prm("h_gate").rearrange("p (k e) -> p k e", k=3)
            for c in range(CT):
                for x, (a, wg) in enumerate(((xc[:, 0, 128 * c:128 * c + 128], hg[:, 0]), (xc[0:64, 1, 128 * c:128 * c + 128], hg[0:64, 1]),
                                             (ones[:], hg[0:1, 2]))):
                    last = mm(ps[:, NE * c:NE * c + NE], a, wg, start=(x == 0), stop=(x == 2))
            end_job(("gate", "H"), last)
            first_hidden(0, X_OCTS[1], 2 * MT)
            pe.wait_ge(*disp_ready.at("H"))
            for a in range(2):
                ps = start_job(("eT", a))
                for c in range(4 * a, min(CT, 4 * a + 4)):
                    last = nc.tensor.transpose(ps[0:NE, 128 * (c - 4 * a):128 * (c - 4 * a) + 128], disp[:, c], ident[:, :])
                end_job(("eT", a), last)
            pe.wait_ge(loaded["b2e"], 16)
            wait_evacuated(("eT", 0), ("eT", 1))
            for c in range(3):
                ps = start_job(("eb", c))
                for i in range(2 if c < 2 else 1):
                    t = 2 * c + i
                    last = mm(ps[0:crow[t], D * i:D * i + D], eT[:, 128 * t:128 * t + crow[t]], b2t[:], start=True, stop=True)
                end_job(("eb", c), last)
            wait_evacuated(("eb", 0), ("eb", 1), ("eb", 2))

            def fc1(i, b):
                pe.wait_ge(w1_low, i * 2 + (b + 1))
                for m in range(MT):
                    for c in range(2):
                        x = 2 * m + c
                        pe.wait_ge(gelu_done, i * 24 + (12 * b + x - 3))
                        hidden(x, b, m, c)

            def fc2(i, b, first=False):
                pe.wait_ge(w2_loaded[b], i * 16 + 16)
                pe.wait_ge(gelu_done, 3 * MT if first else i * 24 + 12 * (b + 1))
                if not first:
                    pe.wait_ge(acc_done, i * 6 + 3 * b)
                for c in range(3):
                    for x in range(2 if c < 2 else 1):
                        t = 2 * c + x
                        for m in range(MT):
                            last = mm(PS[4 + c][0:crow[t], D * x:D * x + D], hbuf[b][:, m, 128 * t:128 * t + crow[t]], w2b[:, b, m],
                                      start=(m == 0), stop=(m == MT - 1))
                    last.then_inc(fc2_done, 1)

            first_hidden(1, X_OCTS[1], 3 * MT)
            fc2(0, 0, first=True)
            with pe.Fori(1, NE // 2) as i:
                fc1(i, 0)
                fc2(i - 1, 1)
                fc1(i, 1)
                fc2(i, 0)
            fc2(NE // 2 - 1, 1)


def kernel(**inputs):
    import numpy as np
    import concourse.bacc as _bacc
    from concourse import mybir as _mybir
    from concourse.bass_utils import run_bass_kernel_spmd as _run

    a = {k: np.asarray(v) for k, v in inputs.items()}
    f32 = np.float32

    def ktiles(wm, bias=None):
        n = wm.shape[1]
        o = np.zeros((97, 2, n), f32)
        o[0:96] = wm.reshape(2, 96, n).transpose(1, 0, 2)
        if bias is not None:
            o[96, 1] = bias
        return o.reshape(97, 2 * n)

    c_qkv = np.concatenate([a["L1_attn_Wq"].T, a["L1_attn_Wk"].T, a["L1_attn_Wv"].T], 1)
    c_bias = np.concatenate([np.zeros(D, f32), a["L1_attn_bk"], a["L1_attn_bv"]])
    seg = {
        "A_qkv": ktiles(a["L0_attn_w_qkv"].T), "A_proj": ktiles(a["L0_attn_w_proj"].T, a["L0_attn_b_proj"]),
        "B_qkv": ktiles(a["L0_ffn_W_qkv"].T, a["L0_ffn_b_qkv"]), "B_gate": ktiles(a["L0_ffn_W_gate"].T, a["L0_ffn_b_gate"]),
        "B_down": ktiles(a["L0_ffn_A"].reshape(NE * RANK, D).T), "B_proj": ktiles(a["L0_ffn_W_proj"].T, a["L0_ffn_b_proj"]),
        "C_qkv": ktiles(c_qkv, c_bias), "C_proj": ktiles(a["L1_attn_Wo"].T, a["L1_attn_bo"]),
        "D_qkv": ktiles(a["L1_ffn_w_qkv"]), "D_proj": ktiles(a["L1_ffn_w_proj"], a["L1_ffn_b_proj"]),
        "D_fc1": ktiles(a["L1_ffn_w_fc1"]),
        "E_qkv": ktiles(a["L2_attn_w_qkv"]), "E_proj": ktiles(a["L2_attn_w_proj"], a["L2_attn_b_proj"]),
        "G_qkv": ktiles(a["L3_attn_w_qkv"], a["L3_attn_b_qkv"]),
    }
    wpack = np.concatenate([seg[n] for n, _ in SEGS], 1)

    P = 16
    x = a["x"].reshape(B, 6, P, 6, P, 3).transpose(0, 1, 3, 2, 4, 5).reshape(B, 36, PATCH_K, 128)
    patches = np.zeros((128, PAIRS, PATCH_K, ROWS), f32)
    xt = x.transpose(3, 0, 2, 1).reshape(128, PAIRS, 2, PATCH_K, 36)
    for i in range(2):
        patches[:, :, :, GAP * i + 1:GAP * i + TOK] = xt[:, :, i]

    c128 = np.concatenate([
        a["L0_tok_W"].reshape(PATCH_K, 128, D).transpose(1, 0, 2).reshape(128, -1),
        a["L0_ffn_B_lora"].transpose(0, 2, 1).reshape(NE * RANK, 3 * D),
        a["L1_ffn_w_fc2"].reshape(MT, 128, D).transpose(1, 0, 2).reshape(128, -1)], 1)

    def cput(o, table, name, val):
        at, width = table[name]
        val = np.asarray(val, f32)
        o[0:val.shape[0], at:at + width] = val.reshape(val.shape[0], width)

    consts = np.zeros((128, CCOLS), f32)
    feat = np.arange(HALF)
    cput(consts, CONST_AT, "ident", np.eye(128))
    cput(consts, CONST_AT, "mask_k", feat[:, None] // HD == np.arange(HH)[None])
    row_head = np.arange(GR) // TOK
    cput(consts, CONST_AT, "mask_v", np.arange(HG * HD)[None] // HD == row_head[:, None])
    cput(consts, CONST_AT, "mask_kv", feat[:, None] // HD == np.arange(HH * (HD + 1))[None] // (HD + 1))
    cput(consts, CONST_AT, "tri", np.broadcast_to(np.arange(NE)[None] < np.arange(NE)[:, None], (128, NE, NE)))
    cput(consts, CONST_AT, "expand", LORA_SCALE * (np.arange(NE)[:, None] == np.arange(128)[None] // RANK))
    for name, n in (("m96", D // 2), ("m64", D // 3)):
        m = np.zeros((97, 2, D), f32)
        r = np.arange(96)[:, None] + 96 * np.arange(2)[None]
        m[0:96] = (r < n)[:, :, None] & (np.arange(D) < n)
        m[96, 1] = np.arange(D) < n
        cput(consts, CONST_AT, name, m)
    for name, n in (("c96", D // 2), ("c64", D // 3)):
        cput(consts, CONST_AT, name, (np.arange(96)[:, None] + 96 * np.arange(2)[None]) < n)

    params = np.zeros((128, PCOLS), f32)
    for name, src in (("n1l_g", "L1_ffn_n1l_g"), ("n1l_b", "L1_ffn_n1l_b"), ("n1s_g", "L1_ffn_n1s_g"), ("n1s_b", "L1_ffn_n1s_b"),
                      ("n2l_g", "L1_ffn_n2l_g"), ("n2l_b", "L1_ffn_n2l_b"), ("n2s_g", "L1_ffn_n2s_g"), ("n2s_b", "L1_ffn_n2s_b"),
                      ("gq", "L1_attn_gq"), ("gk", "L1_attn_gk"), ("b_fc2", "L1_ffn_b_fc2")):
        cput(params, PARAM_AT, name, a[src].reshape(2, 96).T)
    hg = np.zeros((128, 3, NE), f32)
    hg[:, 0], hg[0:64, 1], hg[0, 2] = a["L3_ffn_Wr"][0:128], a["L3_ffn_Wr"][128:], a["L3_ffn_br"]
    cput(params, PARAM_AT, "h_gate", hg)
    cput(params, PARAM_AT, "b_fc1", a["L1_ffn_b_fc1"].reshape(MT, 128).T)
    cput(params, PARAM_AT, "b1", a["L3_ffn_b1"].reshape(NE, MT, 128).transpose(2, 0, 1))
    for name, src in (("gumbel", "L1_ffn_gumbel_weights"), ("bias_q", "L2_ffn_bias"), ("gamma", "L3_attn_ln_gamma"), ("beta", "L3_attn_ln_beta")):
        cput(params, PARAM_AT, name, np.broadcast_to(a[src], (128, a[src].size)))
    pos = np.zeros((128, D), f32)
    cls = np.zeros((128, D), f32)
    for i in range(2):
        pos[GAP * i:GAP * i + TOK] = a["L0_tok_pos_emb"][0]
        cls[GAP * i] = a["L0_tok_class_emb"][0, 0]
    cput(params, PARAM_AT, "pos", pos)
    cput(params, PARAM_AT, "cls", cls)

    arrays = {
        "patches": patches, "wpack": wpack, "c128": c128, "consts": consts, "params": params,
        "w8": np.ascontiguousarray(a["L2_ffn_weight_t"].reshape(2, 96, D).transpose(1, 0, 2)).reshape(96, 2 * D).view(np.int32), "b2e": a["L3_ffn_b2"],
        "w1": np.stack([a["L3_ffn_W1"][:, 0:128], np.concatenate([a["L3_ffn_W1"][:, 128:]] * 2, 1)], 2),
        "w2": a["L3_ffn_W2"].reshape(NE, MT, 128, D).transpose(0, 2, 1, 3),
    }
    arrays = {f"in_{k}": np.ascontiguousarray(v) for k, v in arrays.items()}
    nc = _bacc.Bacc("TRN2", target_bir_lowering=False, num_devices=1)
    args = [nc.dram_tensor(k, v.shape, _mybir.dt.from_np(v.dtype), kind="ExternalInput").ap() for k, v in arrays.items()]
    args.append(nc.dram_tensor("out_0", (T, D), _mybir.dt.float32, kind="ExternalOutput").ap())
    build_tower(nc, *args)
    r = _run(nc, [arrays], core_ids=[0])
    return r.results[0]["out_0"].reshape(B, TOK, D)
```
